# Optimizing a Trainium2 kernel written in Bass

```python
import numpy as np
import jax
import jax.numpy as jnp

def _softmax(x, axis=-1):
    return jax.nn.softmax(x, axis=axis)

def _gelu(x):
    return jax.nn.gelu(x, approximate=True)

def _silu(x):
    return jax.nn.silu(x)

def _sigmoid(x):
    return jax.nn.sigmoid(x)

def _layernorm(x, axis=-1, eps=1e-05):
    m = jnp.mean(x, axis=axis, keepdims=True)
    v = jnp.var(x, axis=axis, keepdims=True)
    return (x - m) / jnp.sqrt(v + eps)

def _scatter_add(tgt, idx, src, axis=0):
    return tgt.at[idx].add(src)

def _segment_sum(src, seg, n):
    return jax.ops.segment_sum(src, seg, n)
kernel_name = 'mk_lm_tower_d1_tok_ids768_r4_048b5e'

def setup_inputs(seed: int=0):
    np.random.seed(seed)
    _w = jnp.asarray

    def _rec_inputs():
        import jax
        import jax.numpy as jnp
        _rk = jax.random.key(seed)
        x = jax.random.randint(jax.random.fold_in(_rk, 1), (32, 256), 0, 250, jnp.int32)
        return x
    x = _rec_inputs()

    def _L0_tok_setup():
        import jax, jax.numpy as jnp
        import numpy as np
        import math
        NUM_POS_FEATS = 96
        TEMPERATURE = 10000.0
        SPECIAL_TOKENS = (0, 1, 2)
        EPS = 1e-06
        key = jax.random.key(seed)
        B, S = (32, 1024)
        x = jax.random.randint(key, (B, S), 0, 250, dtype=jnp.int64)
        scale = jnp.full((1,), 2.0 * math.pi, dtype=jnp.float32)
        return {'x': x, 'scale': scale}
    _L0_tok_all = _L0_tok_setup()
    _L0_tok_in = {k: v for k, v in _L0_tok_all.items() if k in ('scale',)}
    del _L0_tok_all

    def _L0_attn_setup():
        import jax, jax.numpy as jnp
        import numpy as np
        import math
        B, N, C = (8, 1024, 192)
        H = 12
        DH = C // H
        M = 64
        LN_EPS = 1e-05

        def _phi(t, random_features):
            norm_sq = 0.5 * jnp.sum(t * t, axis=-1, keepdims=True)
            proj = jnp.einsum('bhnd,md->bhnm', t, random_features)
            return jnp.exp(proj - norm_sq) * (1.0 / math.sqrt(M))
        key = jax.random.key(seed)
        ks = jax.random.split(key, 7)
        x = jax.random.normal(ks[0], (B, N, C), dtype=jnp.float32)
        W_qkv = jax.random.normal(ks[1], (C, 3 * C), dtype=jnp.float32) * (1.0 / math.sqrt(C))
        W_proj = jax.random.normal(ks[2], (C, C), dtype=jnp.float32) * (1.0 / math.sqrt(C))
        b_proj = jnp.zeros((C,), dtype=jnp.float32)
        gamma = jnp.ones((C,), dtype=jnp.float32)
        beta = jnp.zeros((C,), dtype=jnp.float32)
        random_features = jax.random.normal(ks[3], (M, DH), dtype=jnp.float32) / math.sqrt(DH)
        return {'x': x, 'W_qkv': W_qkv, 'W_proj': W_proj, 'b_proj': b_proj, 'gamma': gamma, 'beta': beta, 'random_features': random_features}
    _L0_attn_all = _L0_attn_setup()
    _L0_attn_in = {k: v for k, v in _L0_attn_all.items() if k in ('W_qkv', 'W_proj', 'b_proj', 'gamma', 'beta', 'random_features')}
    del _L0_attn_all

    def _L0_ffn_setup():
        import jax, jax.numpy as jnp
        import numpy as np
        DIM = 192
        GROUP = 64
        E1, S1, E2 = (8, 16, 4)
        MULT = 4
        HID = int(DIM * MULT * 2 / 3)
        B, N = (4, 1024)

        def _l2norm(t, eps=1e-06):
            return t * jax.lax.rsqrt(jnp.sum(t * t, axis=-1, keepdims=True) + eps)

        def _forward(x, gamma_in, slots1, gamma2, w_slot2, w1, b1, w2, b2):
            b, n, d = x.shape
            G, g = (n // GROUP, GROUP)
            scale = d ** 0.5
            xn = _l2norm(x) * scale * gamma_in
            xg = xn.reshape(b, G, g, d)
            phi = _l2norm(slots1) * scale
            logits1 = jnp.einsum('bGgd,esd->bGges', xg, phi)
            disp1 = jax.nn.softmax(logits1, axis=2)
            comb1 = jax.nn.softmax(logits1.reshape(b, G, g, E1 * S1), -1)
            slots = jnp.einsum('bGgd,bGges->bGesd', xg, disp1)
            yn = _l2norm(slots) * scale * gamma2[None, None, :, None, :]
            ns = S1 // E2
            m = S1 // ns
            means = yn.reshape(b, G, E1, m, ns, d).mean(axis=4)
            se2 = jnp.einsum('bGkmd,kdf->bGkmf', means, w_slot2)
            se2 = se2.reshape(b, G, E1, m, E2, d).transpose(0, 1, 2, 4, 3, 5)
            se2 = _l2norm(se2) * scale
            logits2 = jnp.einsum('bGksd,bGkemd->bGksem', yn, se2)
            disp2 = jax.nn.softmax(logits2, axis=3)
            comb2 = jax.nn.softmax(logits2.reshape(b, G, E1, S1, E2 * m), -1)
            slots2 = jnp.einsum('bGksd,bGksem->bGkemd', yn, disp2)
            u = jnp.einsum('bGkemd,kedh->bGkemh', slots2, w1) + b1[None, None, :, :, None, :]
            v, gate = jnp.split(u, 2, axis=-1)
            act = v * jax.nn.gelu(gate)
            o = jnp.einsum('bGkemh,kehd->bGkemd', act, w2) + b2[None, None, :, :, None, :]
            out2 = jnp.einsum('bGkpd,bGksp->bGksd', o.reshape(b, G, E1, E2 * m, d), comb2)
            out = jnp.einsum('bGPd,bGgP->bGgd', out2.reshape(b, G, E1 * S1, d), comb1)
            return out.reshape(b, n, d)
        key = jax.random.key(seed)
        ks = jax.random.split(key, 8)
        p = lambda k, shape, s=0.02: jax.random.normal(k, shape, dtype=jnp.float32) * s
        return {'x': jax.random.normal(ks[0], (B, N, DIM), dtype=jnp.float32), 'gamma_in': jnp.ones((DIM,), jnp.float32), 'slots1': p(ks[1], (E1, S1, DIM), 1.0 / DIM ** 0.5), 'gamma2': jnp.ones((E1, DIM), jnp.float32), 'w_slot2': p(ks[2], (E1, DIM, E2 * DIM)), 'w1': p(ks[3], (E1, E2, DIM, 2 * HID)), 'b1': jnp.zeros((E1, E2, 2 * HID), jnp.float32), 'w2': p(ks[4], (E1, E2, HID, DIM)), 'b2': jnp.zeros((E1, E2, DIM), jnp.float32)}
    _L0_ffn_all = _L0_ffn_setup()
    _L0_ffn_in = {k: v for k, v in _L0_ffn_all.items() if k in ('gamma_in', 'slots1', 'gamma2', 'w_slot2', 'w1', 'b1', 'w2', 'b2')}
    del _L0_ffn_all
    return {'x': x, 'L0_tok_scale': _L0_tok_in['scale'], 'L0_attn_W_qkv': _L0_attn_in['W_qkv'], 'L0_attn_W_proj': _L0_attn_in['W_proj'], 'L0_attn_b_proj': _L0_attn_in['b_proj'], 'L0_attn_gamma': _L0_attn_in['gamma'], 'L0_attn_beta': _L0_attn_in['beta'], 'L0_attn_random_features': _L0_attn_in['random_features'], 'L0_ffn_gamma_in': _L0_ffn_in['gamma_in'], 'L0_ffn_slots1': _L0_ffn_in['slots1'], 'L0_ffn_gamma2': _L0_ffn_in['gamma2'], 'L0_ffn_w_slot2': _L0_ffn_in['w_slot2'], 'L0_ffn_w1': _L0_ffn_in['w1'], 'L0_ffn_b1': _L0_ffn_in['b1'], 'L0_ffn_w2': _L0_ffn_in['w2'], 'L0_ffn_b2': _L0_ffn_in['b2']}

def reference(x, L0_tok_scale, L0_attn_W_qkv, L0_attn_W_proj, L0_attn_b_proj, L0_attn_gamma, L0_attn_beta, L0_attn_random_features, L0_ffn_gamma_in, L0_ffn_slots1, L0_ffn_gamma2, L0_ffn_w_slot2, L0_ffn_w1, L0_ffn_b1, L0_ffn_w2, L0_ffn_b2):
    import jax
    import jax.numpy as jnp

    def _L0_tok_ref(x, scale):
        import jax, jax.numpy as jnp
        import numpy as np
        import math
        NUM_POS_FEATS = 96
        TEMPERATURE = 10000.0
        SPECIAL_TOKENS = (0, 1, 2)
        EPS = 1e-06
        B, S = x.shape
        F = NUM_POS_FEATS
        special = jnp.asarray(SPECIAL_TOKENS, dtype=x.dtype)
        ns = ~jnp.isin(x, special)
        posf = jnp.arange(S, dtype=jnp.float32)
        sort_key = jnp.where(ns, posf, jnp.float32(S))
        p_sorted = jnp.sort(sort_key, axis=1)
        last = jnp.max(jnp.where(ns, posf, -1.0), axis=1, keepdims=True)
        p_sorted = p_sorted / (last + EPS) * scale[0]
        dim_t = jnp.arange(F, dtype=jnp.float32)
        dim_t = TEMPERATURE ** (2.0 * jnp.floor(dim_t / 2.0) / F)
        idx = jnp.arange(S)
        even = idx % 2 == 0
        ev = ns & even
        od = ns & ~even
        k_e = jnp.cumsum(ev.astype(jnp.int32), axis=1) - 1
        k_o = jnp.cumsum(od.astype(jnp.int32), axis=1) - 1
        p_e = jnp.take_along_axis(p_sorted, jnp.clip(k_e, 0, S - 1), axis=1)
        p_o = jnp.take_along_axis(p_sorted, jnp.clip(k_o, 0, S - 1), axis=1)
        sin_part = jnp.where(ev[..., None], jnp.sin(p_e[..., None] / dim_t), 0.0)
        cos_part = jnp.where(od[..., None], jnp.cos(p_o[..., None] / dim_t), 0.0)
        return jnp.concatenate([sin_part, cos_part], axis=-1)

    def _L0_attn_ref(x, W_qkv, W_proj, b_proj, gamma, beta, random_features):
        import jax, jax.numpy as jnp
        import numpy as np
        import math
        B, N, C = (8, 1024, 192)
        H = 12
        DH = C // H
        M = 64
        LN_EPS = 1e-05

        def _phi(t, random_features):
            norm_sq = 0.5 * jnp.sum(t * t, axis=-1, keepdims=True)
            proj = jnp.einsum('bhnd,md->bhnm', t, random_features)
            return jnp.exp(proj - norm_sq) * (1.0 / math.sqrt(M))
        b, n, c = x.shape
        qkv = (x @ W_qkv).reshape(b, n, 3, H, DH)
        qkv = jnp.transpose(qkv, (2, 0, 3, 1, 4))
        q, k, v = (qkv[0], qkv[1], qkv[2])
        q_p = _phi(q, random_features)
        k_p = _phi(k, random_features)
        kv = jnp.einsum('bhnm,bhnd->bhmd', k_p, v)
        out = jnp.einsum('bhnm,bhmd->bhnd', q_p, kv)
        k_sum = jnp.sum(k_p, axis=2)
        normalizer = jnp.einsum('bhnm,bhm->bhn', q_p, k_sum)[..., None]
        out = out / (normalizer + 1e-06)
        x_attn = jnp.transpose(out, (0, 2, 1, 3)).reshape(b, n, c)
        x_attn = x_attn @ W_proj + b_proj
        y = x + x_attn
        mu = jnp.mean(y, axis=-1, keepdims=True)
        var = jnp.mean(jnp.square(y - mu), axis=-1, keepdims=True)
        return (y - mu) * jax.lax.rsqrt(var + LN_EPS) * gamma + beta

    def _L0_ffn_ref(x, gamma_in, slots1, gamma2, w_slot2, w1, b1, w2, b2):
        import jax, jax.numpy as jnp
        import numpy as np
        DIM = 192
        GROUP = 64
        E1, S1, E2 = (8, 16, 4)
        MULT = 4
        HID = int(DIM * MULT * 2 / 3)
        B, N = (4, 1024)

        def _l2norm(t, eps=1e-06):
            return t * jax.lax.rsqrt(jnp.sum(t * t, axis=-1, keepdims=True) + eps)

        def _forward(x, gamma_in, slots1, gamma2, w_slot2, w1, b1, w2, b2):
            b, n, d = x.shape
            G, g = (n // GROUP, GROUP)
            scale = d ** 0.5
            xn = _l2norm(x) * scale * gamma_in
            xg = xn.reshape(b, G, g, d)
            phi = _l2norm(slots1) * scale
            logits1 = jnp.einsum('bGgd,esd->bGges', xg, phi)
            disp1 = jax.nn.softmax(logits1, axis=2)
            comb1 = jax.nn.softmax(logits1.reshape(b, G, g, E1 * S1), -1)
            slots = jnp.einsum('bGgd,bGges->bGesd', xg, disp1)
            yn = _l2norm(slots) * scale * gamma2[None, None, :, None, :]
            ns = S1 // E2
            m = S1 // ns
            means = yn.reshape(b, G, E1, m, ns, d).mean(axis=4)
            se2 = jnp.einsum('bGkmd,kdf->bGkmf', means, w_slot2)
            se2 = se2.reshape(b, G, E1, m, E2, d).transpose(0, 1, 2, 4, 3, 5)
            se2 = _l2norm(se2) * scale
            logits2 = jnp.einsum('bGksd,bGkemd->bGksem', yn, se2)
            disp2 = jax.nn.softmax(logits2, axis=3)
            comb2 = jax.nn.softmax(logits2.reshape(b, G, E1, S1, E2 * m), -1)
            slots2 = jnp.einsum('bGksd,bGksem->bGkemd', yn, disp2)
            u = jnp.einsum('bGkemd,kedh->bGkemh', slots2, w1) + b1[None, None, :, :, None, :]
            v, gate = jnp.split(u, 2, axis=-1)
            act = v * jax.nn.gelu(gate)
            o = jnp.einsum('bGkemh,kehd->bGkemd', act, w2) + b2[None, None, :, :, None, :]
            out2 = jnp.einsum('bGkpd,bGksp->bGksd', o.reshape(b, G, E1, E2 * m, d), comb2)
            out = jnp.einsum('bGPd,bGgP->bGgd', out2.reshape(b, G, E1 * S1, d), comb1)
            return out.reshape(b, n, d)
        return _forward(x, gamma_in, slots1, gamma2, w_slot2, w1, b1, w2, b2)
    h = _L0_tok_ref(x, L0_tok_scale)
    h = h + _L0_attn_ref(_layernorm(h, axis=-1), L0_attn_W_qkv, L0_attn_W_proj, L0_attn_b_proj, L0_attn_gamma, L0_attn_beta, L0_attn_random_features)
    h = h + _L0_ffn_ref(_layernorm(h, axis=-1), L0_ffn_gamma_in, L0_ffn_slots1, L0_ffn_gamma2, L0_ffn_w_slot2, L0_ffn_w1, L0_ffn_b1, L0_ffn_w2, L0_ffn_b2)
    return h

_drawn_inputs = setup_inputs


def setup_inputs(seed=0):
    import zlib

    import numpy as np

    out = dict(_drawn_inputs(seed))
    spreads = {'L0_attn_b_proj': (0.0, 0.1),
     'L0_attn_gamma': (1.0, 0.2),
     'L0_attn_beta': (0.0, 0.1),
     'L0_ffn_gamma_in': (1.0, 0.2),
     'L0_ffn_gamma2': (1.0, 0.585),
     'L0_ffn_b1': (0.0, 0.8),
     'L0_ffn_b2': (0.0, 0.393)}
    factors = {'L0_attn_random_features': 3.227, 'L0_ffn_w1': 4.232, 'L0_ffn_w2': 4.033}
    for name, (base, spread) in spreads.items():
        noise = np.random.default_rng([zlib.crc32(name.encode()), seed]).standard_normal(out[name].shape)
        drawn = base * np.exp(spread * noise) if base else spread * noise
        out[name] = jnp.asarray(drawn.astype(out[name].dtype))
    for name, factor in factors.items():
        out[name] = (out[name] * factor).astype(out[name].dtype)
    return out
```

```python
import concourse.bass as bass
from concourse import mybir
from contextlib import ExitStack
import numpy as np

F32 = mybir.dt.float32
I32 = mybir.dt.int32
ALU = mybir.AluOpType
ACT = mybir.ActivationFunctionType
AX = mybir.AxisListType

NB, S, D = 32, 256, 192
F = D // 2
P = 128
GQ = S // 64
NT = S // P
H, DH, M = 12, 16, 64
HC = 4
NC_ = H // HC
NG = NB * GQ
NE, NS, E2 = 8, 16, 4
M2 = NS // E2
HID = 512
NHC = HID // P
ROWS = NG * M2
TE = NG * NS // P
GT = P // NS
CB = 4
CT = CB * NT
HX = F + 2

TWO_PI = 2.0 * np.pi
ROUND = float(1.5 * 2.0**23)
PI_HI = 6.28125
PI_LO = float(np.float32(TWO_PI - PI_HI))
PI_MAX = 3.1415925

C_ID, C_MRF, C_INV, C_M1, C_M2, C_EVEN, C_ODD, C_QUART, C_END = np.cumsum([0, P, HC * M, F, P, P, 1, 1, 1]).tolist()


def shape_constants():
    c = np.zeros((P, C_END), np.float32)
    c[:, C_ID:C_ID + P] = np.eye(P)
    for p in range(P):
        h = (p % 64) // DH
        c[p, C_MRF + h * M:C_MRF + (h + 1) * M] = 1.0 if p < 64 else -0.5
    c[:, C_INV:C_INV + F] = (1.0 / 10000.0 ** (2.0 * np.floor(np.arange(F) / 2.0) / F)).astype(np.float32)
    slot_group = np.arange(P) // NS
    inner_group = (np.arange(P) // M2) % GT
    other = np.where(slot_group[:, None] == inner_group[None, :], 0.0, -1e30)
    c[:, C_M1:C_M1 + P] = other
    c[:, C_M2:C_M2 + P] = other.T
    odd = (np.arange(P) // 32) % 2
    c[:, C_EVEN] = 1 - odd
    c[:, C_ODD] = odd
    c[:, C_QUART] = odd * (np.pi / 2)
    rows = np.zeros((NB, 2, S), np.float32)
    rows[:, 0] = np.arange(S) + 1
    rows[:, 1] = np.arange(S) % 2 == 0
    return c, rows


def exists(index):
    return not isinstance(index, int) or index >= 0


def build(nc, x, consts, rows, tok_scale, W_qkv, W_proj, b_proj, gamma, beta, rf, gamma_in, slots1,
          gamma2, w_slot2, w1, b1, w2, b2, out):
    rank_d = nc.dram_tensor("rank_d", (NB, S), F32).ap()
    enc_d = nc.dram_tensor("enc_d", (NB, P, NT, HX), F32).ap()
    encT_d = nc.dram_tensor("encT_d", (NB, F + 1, S), F32).ap()
    h2_d = nc.dram_tensor("h2_d", (NB, P, NT, D + 1), F32).ap()
    combT_d = nc.dram_tensor("combT_d", (NB, P, S), F32).ap()
    yn_d = nc.dram_tensor("yn_d", (NE, NG, NS, D), F32).ap()
    o2_d = nc.dram_tensor("o2_d", (NE, NG, NS, D), F32).ap()

    ctx = ExitStack()
    with ctx:
        def sem(name):
            return ctx.enter_context(nc.semaphore(name))

        def sb(name, shape, dt=F32, c=ctx):
            return c.enter_context(nc.sbuf_tensor(name, shape, dt))

        cst = sb("cst", [P, C_END])
        half = sb("half", [P, 8])
        ident = cst[:, C_ID:C_ID + P]
        bank = [ctx.enter_context(nc.psum_tensor(f"bank{i}", [P, 512], F32)) for i in range(8)]
        with ExitStack() as cw:
            wv = [sb(f"wv{i}", [F + 1, D], c=cw) for i in range(2)]
            wqk = [sb(f"wqk{i}", [F + 1, 2 * NC_, 2, HC * DH], c=cw) for i in range(2)]
            rfa = sb("rfa", [P, HC, M], c=cw)
            wp = [sb("wp0", [F, D], c=cw), sb("wp1", [F + 1, D], c=cw)]
            phiT = sb("phiT", [F, 2, P], c=cw)
            gam = sb("gam", [P, D], c=cw)
            bet = sb("bet", [P, D], c=cw)
            gin = sb("gin", [P, D], c=cw)
            g2r = sb("g2r", [P, D], c=cw)
            with ExitStack() as c0:
                encode(nc, c0, sem, lambda n, s, dt=F32: sb(n, s, dt, c0), bank, locals())
            with ExitStack() as c1:
                attend(nc, c1, sem, lambda n, s, dt=F32: sb(n, s, dt, c1), bank, locals())
        with ExitStack() as c2:
            experts(nc, c2, sem, lambda n, s, dt=F32: sb(n, s, dt, c2), bank, locals())
        with ExitStack() as c3:
            combine(nc, c3, sem, lambda n, s, dt=F32: sb(n, s, dt, c3), bank, locals())


def encode(nc, ctx, sem, sb, bank, g):
    cst, ident, half = g["cst"], g["ident"], g["half"]
    wv, wqk, rfa, wp, phiT = g["wv"], g["wqk"], g["rfa"], g["wp"], g["phiT"]
    xi = sb("xi", [NB, S], I32)
    row = sb("row", [NB, 2, S])
    xf = sb("xf", [NB, S])
    keep = sb("keep", [NB, S])
    tmp = sb("tmp", [NB, S])
    one = sb("one", [NB, S])
    cum = sb("cum", [NB, 3, S])
    perm = sb("perm", [NB, 3, S])
    small = sb("small", [NB, 4])
    tabs = sb("tabs", [P, 3, NB * NT])
    wraw = [sb(f"wraw{i}", [F, 3 * D]) for i in range(2)]
    ones = sb("ones", [F, F + 1])
    rfn = sb("rfn", [M, DH])
    rfr = sb("rfr", [M, HC, DH])
    sl = sb("sl", [P, D])
    sq1 = sb("sq1", [P, D])
    phn = sb("phn", [P, D])
    r1 = sb("r1", [P, 4])
    cb = sb("cb", [P, CB, S])
    kk = sb("kk", [P, 3, CT])
    junk = sb("junk", [P, CT, S])
    cnt = sb("cnt", [P, CT])
    psc = sb("psc", [P, CT])
    ang = sb("ang", [P, CT, F])
    nr = sb("nr", [P, CT, F])
    nr2 = sb("nr2", [P, CT, F])
    rd = sb("rd", [P, CT, F])
    rd2 = sb("rd2", [P, CT, F])
    rd3 = sb("rd3", [P, CT, F])
    sn = sb("sn", [P, CT, F])
    he = sb("he", [P, CT, HX])
    hsq = sb("hsq", [P, CT, F])
    st = sb("st", [P, 8, CT])
    et = sb("et", [P, CT, F + 1])
    etT = sb("etT", [F + 1, CB, 2, P])

    s_x, s_c, s_w, s_half = sem("p0_x"), sem("p0_const"), sem("p0_weights"), sem("p0_half")
    s_cum, s_rank_d, s_tabs_mm, s_tabs = sem("p0_ranks"), sem("p0_rank_stored"), sem("p0_tabs_mm"), sem("p0_tabs")
    s_ones, s_col, s_rfr, s_rft = sem("p0_ones"), sem("p0_colsum"), sem("p0_rfr"), sem("p0_rft")
    s_ssq, s_pw, s_phn, s_pht = sem("p0_ssq"), sem("p0_pow"), sem("p0_phn"), sem("p0_pht")
    chain = sem("p0_dve_chain")
    s_cb, s_cnt, s_sin_in, s_sin = sem("enc_cb"), sem("enc_count"), sem("enc_reduced"), sem("enc_sin")
    s_kk, s_step, s_he, s_hsq = sem("enc_kk"), sem("enc_step"), sem("enc_he"), sem("enc_hsq")
    s_var, s_ve, s_rs, s_mr = sem("enc_var"), sem("enc_ve"), sem("enc_rstd"), sem("enc_mr")
    s_et, s_etT_mm, s_etT = sem("enc_et"), sem("enc_etT_mm"), sem("enc_etT")
    s_std = sem("enc_stored")
    block = ctx.enter_context(nc.Block())
    PERM = "b (q j r) -> b q r j"

    @block.sync
    def _(sp):
        sp.dma_start(xi[:, :], g["x"]).then_inc(s_x, 16)
        sp.dma_start(row[:, :, :], g["rows"]).then_inc(s_x, 16)
        sp.dma_start(small[:, 0:1], g["tok_scale"].partition_broadcast(NB)).then_inc(s_x, 16)
        sp.dma_start(cst[:, :], g["consts"]).then_inc(s_c, 16)
        for i in range(2):
            sp.dma_start(wraw[i][:, :], g["W_qkv"][i * F:(i + 1) * F, :]).then_inc(s_w, 16)
            sp.dma_start(wp[i][0:F, :], g["W_proj"][i * F:(i + 1) * F, :]).then_inc(s_w, 16)
        sp.dma_start(wp[1][F:F + 1, :], g["b_proj"].unsqueeze(0)).then_inc(s_w, 16)
        sp.dma_start(rfn[:, :], g["rf"]).then_inc(s_w, 16)
        sp.dma_start(sl[:, :], g["slots1"].rearrange("e s d -> (e s) d")).then_inc(s_w, 16)
        for dst, src in ((g["gam"], "gamma"), (g["bet"], "beta"), (g["gin"], "gamma_in")):
            sp.dma_start(dst[:, :], g[src].partition_broadcast(P)).then_inc(s_w, 16)
        for e in range(NE):
            sp.dma_start(g["g2r"][e * NS:(e + 1) * NS, :],
                         g["gamma2"][e].partition_broadcast(NS)).then_inc(s_w, 16)
        sp.wait_ge(s_cum, 1)
        sp.dma_start(g["rank_d"], cum[:, 0, :]).then_inc(s_rank_d, 16)
        sp.wait_ge(s_rank_d, 16)

        def chunk(i):
            if exists(i - 1):
                sp.wait_ge(s_cnt, 1)
                sp.wait_ge(s_cnt, i)
            sp.dma_start(cb[:, :, :], g["rank_d"][bass.ts(i, CB), :].partition_broadcast(P)).then_inc(s_cb, 16)
            sp.wait_ge(s_mr, 1)
            sp.wait_ge(s_mr, i + 1)
            sp.dma_start(g["enc_d"].rearrange("(n c) p t f -> n p c t f", c=CB)[i],
                         he[:, :, :].rearrange("p (c t) f -> p c t f", t=NT)).then_inc(s_std, 16)
            sp.wait_ge(s_etT, 1)
            sp.wait_ge(s_etT, i + 1)
            sp.dma_start(g["encT_d"].rearrange("(n c) p s -> n p c s", c=CB)[i],
                         etT[:, :, :, :].rearrange("p c r s -> p c (r s)")).then_inc(s_std, 16)

        chunk(0)
        with sp.Fori(1, NB // CB, 1) as i:
            chunk(i)
        sp.wait_ge(s_std, 32 * (NB // CB))

    @block.vector
    def _(dve):
        v = nc.vector
        links = [0]

        def link(ins):
            links[0] += 1
            ins.then_inc(chain, 1)
            dve.wait_ge(chain, links[0])

        v.memset(half[:, :], -0.5).then_inc(s_half, 1)
        v.memset(one[:, :], 1.0)
        v.memset(ones[:, :], 1.0).then_inc(s_ones, 1)
        dve.wait_ge(s_x, 48)
        link(v.tensor_copy(xf[:, :], xi[:, :]))
        link(v.tensor_scalar(tmp[:, :], xf[:, :], 0.0, None, ALU.not_equal))
        link(v.scalar_tensor_tensor(keep[:, :], xf[:, :], 1.0, tmp[:, :], ALU.not_equal, ALU.mult))
        link(v.scalar_tensor_tensor(tmp[:, :], xf[:, :], 2.0, keep[:, :], ALU.not_equal, ALU.mult))
        link(v.tensor_tensor(xf[:, :], tmp[:, :], row[:, 0, :], ALU.mult))
        link(v.reduce_max(small[:, 1:2], xf[:, :], AX.X))
        link(v.tensor_scalar(small[:, 2:3], small[:, 1:2], -1.0, 1e-6, ALU.add, ALU.add))
        link(v.reciprocal(small[:, 3:4], small[:, 2:3]))
        link(v.tensor_tensor(small[:, 1:2], small[:, 3:4], small[:, 0:1], ALU.mult))
        link(v.tensor_tensor(keep[:, :], tmp[:, :], row[:, 1, :], ALU.mult))
        link(v.tensor_tensor(xf[:, :], tmp[:, :], keep[:, :], ALU.subtract))
        v.tensor_tensor_scan(cum[:, 0, :], one[:, :], tmp[:, :], 0.0, ALU.mult, ALU.add).then_inc(s_cum, 1)
        v.tensor_tensor_scan(cum[:, 1, :], one[:, :], keep[:, :], 0.0, ALU.mult, ALU.add)
        link(v.tensor_tensor_scan(cum[:, 2, :], one[:, :], xf[:, :], 0.0, ALU.mult, ALU.add))
        for r in range(2):
            src = cum[:, 1 + r, :].rearrange(PERM, r=2, j=32)[:, :, r, :]
            v.tensor_copy(perm[:, 0, :].rearrange("b (q r j) -> b q r j", r=2, j=32)[:, :, r, :], src)
            v.tensor_copy(perm[:, 1, :].rearrange("b (q r j) -> b q r j", r=2, j=32)[:, :, r, :],
                          tmp[:, :].rearrange(PERM, r=2, j=32)[:, :, r, :])
        link(v.tensor_scalar(perm[:, 2, :], one[:, :], small[:, 1:2], None, ALU.mult))
        dve.wait_ge(s_tabs_mm, 1)
        v.tensor_copy(tabs[:, :, :].rearrange("p a (b t) -> p a t b", t=NT)[:, :, 0, :],
                      bank[0][:, 0:3 * NT * NB].rearrange("p (a t b) -> p a t b", a=3, t=NT)[:, :, 0, :])
        link(v.tensor_copy(tabs[:, :, :].rearrange("p a (b t) -> p a t b", t=NT)[:, :, 1, :],
                           bank[0][:, 0:3 * NT * NB].rearrange("p (a t b) -> p a t b", a=3, t=NT)[:, :, 1, :]))
        v.memset(r1[:, :], 0.0)
        dve.wait_ge(s_w, 16 * 18)
        dve.wait_ge(s_c, 16)
        for i in range(2):
            v.tensor_copy(wv[i][0:F, :], wraw[i][:, 2 * D:3 * D])
            for r in range(2):
                v.tensor_copy(wqk[i][0:F, :, r, :], wraw[i][:, 0:2 * D].rearrange("p (c n) -> p c n", c=2 * NC_))
        dve.wait_ge(s_col, 1)
        for i in range(2):
            v.tensor_copy(wv[i][F:F + 1, :], bank[2][F:F + 1, 0:D])
            for r in range(2):
                v.tensor_copy(wqk[i][F:F + 1, :, r, :],
                              bank[1][F:F + 1, 0:2 * D].rearrange("p (c n) -> p c n", c=2 * NC_))
        v.tensor_copy(rfr[:, :, :], rfn[:, :].unsqueeze(1).to_broadcast([M, HC, DH])).then_inc(s_rfr, 1)
        dve.wait_ge(s_rft, 1)
        v.tensor_tensor(rfa[0:64, :, :], bank[3][0:64, 0:M].unsqueeze(1).to_broadcast([64, HC, M]),
                        cst[0:64, C_MRF:C_MRF + HC * M].rearrange("p (h m) -> p h m", h=HC), ALU.mult)
        v.tensor_copy(rfa[64:128, :, :], cst[64:128, C_MRF:C_MRF + HC * M].rearrange("p (h m) -> p h m", h=HC))
        link(v.tensor_tensor(sq1[:, :], sl[:, :], sl[:, :], ALU.mult))
        link(v.reduce_sum(r1[:, 0:1], sq1[:, :], AX.X))
        v.tensor_scalar(r1[:, 1:2], r1[:, 0:1], 1.0 / D, 1e-6 / D, ALU.mult, ALU.add).then_inc(s_ssq, 1)
        dve.wait_ge(s_pw, 1)
        v.tensor_scalar(phn[:, :], sl[:, :], r1[:, 2:3], None, ALU.mult).then_inc(s_phn, 1)
        dve.wait_ge(s_pht, 1)
        v.tensor_copy(phiT[:, :, :], bank[4][0:F, 0:2 * P].rearrange("p (c n) -> p c n", c=2))

        def chunk(i):
            if exists(8 * i - 1):
                dve.wait_ge(s_step, 8 * i)
            v.tensor_scalar(kk[:, :, :], tabs[:, :, bass.ts(i, CT)], 1.0, None, ALU.mult).then_inc(s_kk, 1)
            dve.wait_ge(s_kk, i + 1)
            dve.wait_ge(s_cb, 16 * i + 16)
            for t in range(CT):
                ins = v.tensor_scalar(junk[:, t, :], cb[:, t // NT, :], kk[:, 0, t:t + 1], 0.0, ALU.is_lt, ALU.add,
                                      accum_out=cnt[:, t:t + 1])
            ins.then_inc(s_cnt, 1)
            dve.wait_ge(s_cnt, i + 1)
            v.tensor_tensor(psc[:, :], cnt[:, :], kk[:, 2, :], ALU.mult).then_inc(s_step, 1)
            dve.wait_ge(s_step, 8 * i + 1)
            for t in range(CT):
                ins = v.tensor_scalar(ang[:, t, :], cst[:, C_INV:C_INV + F], psc[:, t:t + 1],
                                      cst[:, C_QUART:C_QUART + 1], ALU.mult, ALU.add)
            ins.then_inc(s_step, 1)
            dve.wait_ge(s_step, 8 * i + 2)
            v.tensor_scalar(nr[:, :, :], ang[:, :, :], float(1.0 / TWO_PI), ROUND, ALU.mult, ALU.add).then_inc(s_step, 1)
            dve.wait_ge(s_step, 8 * i + 3)
            v.tensor_scalar(nr2[:, :, :], nr[:, :, :], -ROUND, None, ALU.add).then_inc(s_step, 1)
            dve.wait_ge(s_step, 8 * i + 4)
            v.scalar_tensor_tensor(rd[:, :, :], nr2[:, :, :], -PI_HI, ang[:, :, :], ALU.mult, ALU.add).then_inc(s_step, 1)
            dve.wait_ge(s_step, 8 * i + 5)
            v.scalar_tensor_tensor(rd2[:, :, :], nr2[:, :, :], -PI_LO, rd[:, :, :], ALU.mult, ALU.add).then_inc(s_step, 1)
            dve.wait_ge(s_step, 8 * i + 6)
            v.tensor_scalar(rd3[:, :, :], rd2[:, :, :], PI_MAX, -PI_MAX, ALU.min, ALU.max).then_inc(s_sin_in, 1)
            dve.wait_ge(s_sin, i + 1)
            if exists(2 * i - 1):
                dve.wait_ge(s_std, (2 * i) * 16)
            v.tensor_tensor(he[:, :, 0:F], sn[:, :, :], kk[:, 1, :].unsqueeze(2).to_broadcast([P, CT, F]),
                            ALU.mult).then_inc(s_he, 1)
            dve.wait_ge(s_he, i + 1)
            v.reduce_sum(st[:, 0, :], he[:, :, 0:F], AX.X).then_inc(s_step, 1)
            dve.wait_ge(s_hsq, i + 1)
            v.reduce_sum(st[:, 1, :], hsq[:, :, :], AX.X).then_inc(s_step, 1)
            dve.wait_ge(s_step, 8 * i + 8)
            v.tensor_scalar(st[:, 2, :], st[:, 0, :], -1.0 / D, None, ALU.mult).then_inc(s_var, 1)
            dve.wait_ge(s_var, 3 * i + 1)
            v.tensor_tensor(st[:, 3, :], st[:, 2, :], st[:, 2, :], ALU.mult).then_inc(s_var, 1)
            dve.wait_ge(s_var, 3 * i + 2)
            v.scalar_tensor_tensor(st[:, 4, :], st[:, 1, :], 1.0 / D, st[:, 3, :], ALU.mult,
                                   ALU.subtract).then_inc(s_var, 1)
            dve.wait_ge(s_var, 3 * i + 3)
            if exists(i - 1):
                dve.wait_ge(s_rs, i)
            v.tensor_scalar(st[:, 5, :], st[:, 4, :], 1e-5, None, ALU.add).then_inc(s_ve, 1)
            dve.wait_ge(s_mr, i + 1)
            if exists(i - 1):
                dve.wait_ge(s_etT_mm, i)
            v.tensor_tensor(et[:, :, 0:F], he[:, :, 0:F], he[:, :, F:F + 1].to_broadcast([P, CT, F]), ALU.mult)
            v.tensor_copy(et[:, :, F:F + 1], he[:, :, F + 1:F + 2]).then_inc(s_et, 1)

        chunk(0)
        with dve.Fori(1, NB // CB, 1) as i:
            chunk(i)

    @block.scalar
    def _(act):
        def chunk(i):
            act.wait_ge(s_sin_in, i + 1)
            if exists(i - 1):
                act.wait_ge(s_he, i)
            nc.scalar.activation(sn[:, :, :], rd3[:, :, :], ACT.Sin).then_inc(s_sin, 1)
            act.wait_ge(s_he, i + 1)
            nc.scalar.activation(hsq[:, :, :], he[:, :, 0:F], ACT.Square).then_inc(s_hsq, 1)
            act.wait_ge(s_etT_mm, i + 1)
            if exists(2 * i - 1):
                act.wait_ge(s_std, (2 * i) * 16)
            for h in range(2):
                for r in range(2):
                    ins = nc.scalar.activation(
                        etT[:, 2 * h:2 * h + 2, r, :].rearrange("p c (q j) -> p c q j", j=32),
                        bank[5 + h][0:F + 1, :].rearrange("p (c q r j) -> p c q r j", c=2, r=2, j=32)[:, :, :, r, :],
                        ACT.Copy)
            ins.then_inc(s_etT, 1)

        chunk(0)
        with act.Fori(1, NB // CB, 1) as i:
            chunk(i)

    @block.gpsimd
    def _(pool):
        p = nc.gpsimd
        pool.wait_ge(s_half, 1)
        pool.wait_ge(s_ssq, 1)
        p.tensor_tensor(r1[:, 2:3], r1[:, 1:2], half[:, 0:1], ALU.pow).then_inc(s_pw, 1)

        def chunk(i):
            pool.wait_ge(s_ve, i + 1)
            p.tensor_tensor(he[:, :, F], st[:, 5, :], half[:, 0:CT], ALU.pow).then_inc(s_rs, 1)
            pool.wait_ge(s_rs, i + 1)
            p.tensor_tensor(he[:, :, F + 1], st[:, 2, :], he[:, :, F], ALU.mult).then_inc(s_mr, 1)

        chunk(0)
        with pool.Fori(1, NB // CB, 1) as i:
            chunk(i)

    @block.tensor
    def _(pe):
        pe.wait_ge(s_c, 16)
        pe.wait_ge(chain, 13)
        for a in range(3):
            for t in range(NT):
                ins = nc.tensor.transpose(bank[0][:, (a * NT + t) * NB:(a * NT + t + 1) * NB],
                                          perm[:, a, t * P:(t + 1) * P], ident[0:NB, 0:NB])
        ins.then_inc(s_tabs_mm, 1)
        pe.wait_ge(s_ones, 1)
        pe.wait_ge(s_w, 16 * 18)
        for i in range(2):
            nc.tensor.matmul(bank[1][0:F + 1, 0:2 * D], ones[:, :], wraw[i][:, 0:2 * D], start=i == 0, stop=i == 1)
        for i in range(2):
            ins = nc.tensor.matmul(bank[2][0:F + 1, 0:D], ones[:, :], wraw[i][:, 2 * D:3 * D], start=i == 0, stop=i == 1)
        ins.then_inc(s_col, 1)
        pe.wait_ge(s_rfr, 1)
        nc.tensor.transpose(bank[3][0:64, 0:M], rfr[:, :, :].rearrange("p h d -> p (h d)"),
                            ident[0:M, 0:M]).then_inc(s_rft, 1)
        pe.wait_ge(s_phn, 1)
        for c in range(2):
            ins = nc.tensor.transpose(bank[4][0:F, c * P:(c + 1) * P], phn[:, c * F:(c + 1) * F], ident)
        ins.then_inc(s_pht, 1)

        def chunk(i):
            pe.wait_ge(s_et, i + 1)
            if exists(i - 1):
                pe.wait_ge(s_etT, i)
            for t in range(CT):
                ins = nc.tensor.transpose(bank[5 + t // 4][0:F + 1, (t % 4) * P:(t % 4 + 1) * P], et[:, t, :], ident)
            ins.then_inc(s_etT_mm, 1)

        chunk(0)
        with pe.Fori(1, NB // CB, 1) as i:
            chunk(i)


def attend(nc, ctx, sem, sb, bank, g):
    cst, ident, half = g["cst"], g["ident"], g["half"]
    wv, wqk, rfa, wp, phiT = g["wv"], g["wqk"], g["rfa"], g["wp"], g["phiT"]
    gam, bet, gin, g2r = g["gam"], g["bet"], g["gin"], g["g2r"]
    two = range(2)
    encT = [sb(f"encT{i}", [F + 1, S]) for i in two]
    enc = [sb(f"enc{i}", [P, NT, HX]) for i in two]
    qk = [sb(f"qk{c}", [P, 2 * S]) for c in range(NC_)]
    kp = [sb(f"kp{c}", [P, 2, HC * M]) for c in range(NC_)]
    qp = [sb(f"qp{c}", [P, 2, S]) for c in range(NC_)]
    va = [sb(f"va{i}", [P, 2, H, DH + 1]) for i in two]
    kvb = sb("kvb", [P, H // 2, 2, DH + 1])
    den = sb("den", [P, NT * H])
    rden = sb("rden", [P, NT * H])
    xa = sb("xa", [P, NT, D])
    xaT = [sb("xaT0", [F, S]), sb("xaT1", [F + 1, S])]
    hh = [sb(f"hh{i}", [P, NT, D]) for i in two]
    hb = [sb(f"hb{i}", [P, NT, D]) for i in two]
    xs = sb("xs", [P, NT, D])
    xh = [sb(f"xh{i}", [P, NT, D]) for i in two]
    y = sb("y", [P, NT, D])
    bs = sb("bs", [P, NT, 6])
    mv = sb("mv", [P, NT, 2])
    ve = sb("ve", [P, NT])
    rs = sb("rs", [P, NT])
    yg = sb("yg", [P, NT, D])
    h2 = [sb(f"h2{i}", [P, NT, D + 1]) for i in two]
    bs2 = sb("bs2", [P, NT, 6])
    mv2 = sb("mv2", [P, NT, 2])
    ve2 = sb("ve2", [P, NT])
    f2 = sb("f2", [P, NT])
    xc = sb("xc", [P, NT, D])
    xn = [sb(f"xn{i}", [P, NT, D]) for i in two]
    xnT = sb("xnT", [F, 2, S])
    mx = sb("mx", [P, NT + GQ])
    nm = sb("nm", [P, NT + GQ])
    ec = sb("ec", [P, NT, P])
    ed = sb("ed", [P, GQ, 64])
    zd = sb("zd", [P, GQ])
    cT = [sb(f"cT{i}", [P, S]) for i in two]
    dT = sb("dT", [P, NT, P])
    sqj = sb("sqj", [P, GQ, D])
    ssq = sb("ssq", [P, GQ])
    zs = sb("zs", [P, GQ])
    sse = sb("sse", [P, GQ])
    sr = sb("sr", [P, GQ])
    yn = [sb(f"yn{i}", [P, GQ, D]) for i in two]

    s_ld = [sem(f"loaded{i}") for i in two]
    s_init = sem("at_init")
    qk_mm, qk_copy, qk_sq = sem("qk_mm"), sem("qk_copy"), sem("qk_sq")
    f_mm, f_exp = sem("feat_mm"), sem("feat_exp")
    v_mm, v_ev, kv_mm, kv_ev = sem("v_mm"), sem("v_ev"), sem("kv_mm"), sem("kv_ev")
    o_mm, o_den, o_rcp, o_ev = sem("o_mm"), sem("o_den"), sem("o_rcp"), sem("o_ev")
    xaT_mm, xaT_ev, pj_mm = sem("xaT_mm"), sem("xaT_ev"), sem("pj_mm")
    prep, prep1, prep2 = sem("prep"), sem("prep1"), sem("prep2")
    y_ev, y_bs, y_mv, y_ve, y_rs, y_g, y_h2 = (sem(n) for n in ("y_ev", "y_bs", "y_mv", "y_ve", "y_rs", "y_g", "y_h2"))
    h_bs, h_mv, h_ve, h_f, h_xc, h_xn = (sem(n) for n in ("h_bs", "h_mv", "h_ve", "h_f", "h_xc", "h_xn"))
    xnT_mm, xnT_ev, lg_mm, lg_mx, lg_nm = (sem(n) for n in ("xnT_mm", "xnT_ev", "lg_mm", "lg_mx", "lg_nm"))
    e_c, e_d, cd_mm, c_ev, d_ev = (sem(n) for n in ("e_c", "e_d", "cd_mm", "c_ev", "d_ev"))
    sl_mm, sl_sq, sl_z, sl_e, sl_r, sl_y = (sem(n) for n in ("sl_mm", "sl_sq", "sl_z", "sl_e", "sl_r", "sl_y"))
    s_h2 = [sem(f"h2_stored{i}") for i in two]
    s_yn = [sem(f"yn_stored{i}") for i in two]
    block = ctx.enter_context(nc.Block())
    b_qk, b_ft = bank[0:2], bank[2:4]
    b_v, b_o, b_x, b_s = bank[4], bank[5], bank[6], bank[7]
    YN = GQ

    def pipeline(eng, iteration, last):
        def go(a, u):
            n = 2 * a + u
            if isinstance(n, int):
                iteration(a, u, n, [0 <= n - k < NB for k in range(last + 1)])
            else:
                iteration(a, u, n, [True] * (last + 1))
        for n in range(6):
            go(n // 2, n % 2)
        with eng.Fori(3, NB // 2, 1) as a:
            for u in two:
                go(a, u)
        for n in range(NB, NB + last):
            go(n // 2, n % 2)

    @block.sync
    def _(sp):
        def iteration(a, u, n, step):
            if step[0]:
                if exists(n - 2):
                    sp.wait_ge(v_mm, 1)
                    sp.wait_ge(v_mm, n - 1)
                if exists(n - 2):
                    sp.wait_ge(prep2, 1)
                    sp.wait_ge(prep2, n - 1)
                sp.dma_start(encT[u][:, :], g["encT_d"][n]).then_inc(s_ld[u], 16)
                sp.dma_start(enc[u][:, :, :], g["enc_d"][n]).then_inc(s_ld[u], 16)
            if step[3]:
                l, v = n - 3, 1 - u
                sp.wait_ge(e_c, 1)
                sp.wait_ge(e_c, l + 1)
                sp.dma_start(g["h2_d"][l], h2[v][:, :, :]).then_inc(s_h2[v], 16)
                sp.wait_ge(c_ev, 1)
                sp.wait_ge(c_ev, l + 1)
                sp.dma_start(g["combT_d"][l], cT[v][:, :]).then_inc(s_h2[v], 16)
                sp.wait_ge(sl_y, 1)
                sp.wait_ge(sl_y, l + 1)
                for q in range(GQ):
                    sp.dma_start(g["yn_d"].rearrange("e (b q) s d -> b q e s d", q=GQ)[l, q],
                                 yn[v][:, q, :]).then_inc(s_yn[v], 16)

        pipeline(sp, iteration, 3)
        for u in two:
            sp.wait_ge(s_h2[u], 32 * NB // 2)
            sp.wait_ge(s_yn[u], 16 * YN * NB // 2)

    @block.tensor
    def _(pe):
        mm, tr = nc.tensor.matmul, nc.tensor.transpose
        pe.wait_ge(s_init, 2)

        def iteration(a, u, n, step):
            m, l = n - 1, n - 2
            eT = encT[u][:, :].rearrange("p (r s) -> p r s", r=2)

            def QK(c):
                if c == 0:
                    pe.wait_ge(s_ld[u], (a + 1) * 32)
                if exists(NC_ * n + c - 2):
                    pe.wait_ge(qk_copy, NC_ * n + c - 1)
                if exists(NC_ * n + c - 2):
                    pe.wait_ge(qk_sq, NC_ * n + c - 1)
                b = b_qk[(u + c) % 2]
                for r in two:
                    mm(b[:, 0:S].rearrange("p (q r j) -> p q r j", r=2, j=32)[:, :, r, :],
                       wqk[r][:, c, :, :].rearrange("p a n -> p (a n)"), eT[:, r, :].rearrange("p (q j) -> p q j", j=32), start=True, stop=True)
                for r in two:
                    ins = mm(b[:, S + r * P:S + (r + 1) * P],
                             wqk[r][:, NC_ + c, :, :].rearrange("p a n -> p (a n)"), eT[:, r, :], start=True, stop=True)
                ins.then_inc(qk_mm, 1)

            def V():
                if exists(l - 1):
                    pe.wait_ge(sl_y, l)
                for r in two:
                    ins = mm(b_v[:, r * D:(r + 1) * D], eT[:, r, :], wv[r][:, :], start=True, stop=True)
                ins.then_inc(v_mm, 1)

            def FEAT(s):
                if exists(2 * NC_ * n + s - 2):
                    pe.wait_ge(f_exp, 2 * NC_ * n + s - 1)
                c, b = s % NC_, b_ft[s % 2]
                if s < NC_:
                    pe.wait_ge(qk_copy, NC_ * n + c + 1)
                    pe.wait_ge(qk_sq, NC_ * n + c + 1)
                for r in two:
                    if s < NC_:
                        ins = mm(b[:, r * 256:(r + 1) * 256], qk[c][:, S + r * P:S + (r + 1) * P],
                                 rfa[:, :, :].rearrange("p h m -> p (h m)"), start=True, stop=True)
                    else:
                        ins = mm(b[:, r * 256:(r + 1) * 256],
                                 rfa[:, 2 * r:2 * r + 2, :].rearrange("p h m -> p (h m)"), qk[c][:, 0:S],
                                 start=True, stop=True)
                ins.then_inc(f_mm, 1)

            def KV():
                pe.wait_ge(f_exp, 2 * NC_ * n + NC_)
                pe.wait_ge(v_ev, n + 1)
                for p in range(H // 2):
                    for r in two:
                        ins = mm(b_v[:, 34 * p:34 * p + 34], kp[p // 2][:, r, (p % 2) * P:(p % 2 + 1) * P],
                                 va[u][:, r, 2 * p:2 * p + 2, :].rearrange("p h d -> p (h d)"),
                                 start=r == 0, stop=r == 1)
                ins.then_inc(kv_mm, 1)

            def OUT():
                pe.wait_ge(kv_ev, m + 1)
                pe.wait_ge(f_exp, 2 * NC_ * m + 2 * NC_)
                if exists(m - 1):
                    pe.wait_ge(y_ev, m)
                for t in two:
                    for p in range(H // 2):
                        ins = mm(b_o[:, t * 204 + 34 * p:t * 204 + 34 * p + 34], qp[p // 2][:, p % 2, t * P:(t + 1) * P],
                                 kvb[:, p, :, :].rearrange("p h d -> p (h d)"), start=True, stop=True)
                ins.then_inc(o_mm, 1)

            def XAT():
                pe.wait_ge(o_ev, m + 1)
                for c in two:
                    for t in two:
                        ins = tr(b_o[0:F, (2 * c + t) * P:(2 * c + t + 1) * P], xa[:, t, c * F:(c + 1) * F], ident)
                ins.then_inc(xaT_mm, 1)

            def PROJ():
                pe.wait_ge(xaT_ev, m + 1)
                for t in two:
                    for c in two:
                        ins = mm(b_o[:, t * D:(t + 1) * D], xaT[c][:, t * P:(t + 1) * P], wp[c][:, :],
                                 start=c == 0, stop=c == 1)
                ins.then_inc(pj_mm, 1)

            def XNT():
                pe.wait_ge(h_xn, l + 1)
                if exists(l - 1):
                    pe.wait_ge(c_ev, l)
                if exists(l - 1):
                    pe.wait_ge(d_ev, l)
                for c in two:
                    for t in two:
                        ins = tr(b_x[0:F, (2 * c + t) * P:(2 * c + t + 1) * P], xn[u][:, t, c * F:(c + 1) * F], ident)
                ins.then_inc(xnT_mm, 1)

            def LOG():
                pe.wait_ge(xnT_ev, l + 1)
                for t in two:
                    for c in two:
                        mm(b_x[:, t * P:(t + 1) * P], xnT[:, c, t * P:(t + 1) * P], phiT[:, c, :], start=c == 0, stop=c == 1)
                for c in two:
                    ins = mm(b_x[:, S:2 * S], phiT[:, c, :], xnT[:, c, :], start=c == 0, stop=c == 1)
                ins.then_inc(lg_mm, 1)

            def CDT():
                pe.wait_ge(e_c, l + 1)
                pe.wait_ge(e_d, l + 1)
                for t in two:
                    tr(b_x[:, t * P:(t + 1) * P], ec[:, t, :], ident)
                for t in two:
                    ins = tr(b_x[:, S + t * P:S + (t + 1) * P], ed[:, 2 * t:2 * t + 2, :].rearrange("p q s -> p (q s)"), ident)
                ins.then_inc(cd_mm, 1)

            def SLOTS():
                pe.wait_ge(d_ev, l + 1)
                if exists(l - 1):
                    pe.wait_ge(sl_y, l)
                for t in two:
                    for q, b in ((0, b_s), (1, b_v)):
                        ins = mm(b[:, t * D:(t + 1) * D], dT[64 * q:64 * q + 64, t, :], xn[u][64 * q:64 * q + 64, t, :],
                                 start=True, stop=True)
                ins.then_inc(sl_mm, 1)

            A, B, C = step
            if A:
                QK(0)
            if B:
                OUT()
            if A:
                QK(1)
            if C:
                XNT()
            if A:
                QK(2)
            if C:
                LOG()
            if A:
                V()
                FEAT(0)
                FEAT(1)
            if B:
                XAT()
            if A:
                FEAT(2)
                FEAT(3)
            if B:
                PROJ()
            if A:
                KV()
                FEAT(4)
            if C:
                CDT()
            if A:
                FEAT(5)
            if C:
                if A:
                    pe.wait_ge(kv_ev, n + 1)
                SLOTS()

        pipeline(pe, iteration, 2)

    @block.vector
    def _(dve):
        v = nc.vector
        for i in two:
            v.memset(va[i][:, :, :, :], 1.0)
        v.memset(kvb[:, :, :, :], 0.0).then_inc(s_init, 1)
        v.memset(xaT[1][F:F + 1, :], 1.0).then_inc(s_init, 1)

        def iteration(a, u, n, step):
            m, l, w = n - 1, n - 2, 1 - u

            def qk_copy_(c):
                dve.wait_ge(qk_mm, NC_ * n + c + 1)
                if exists(2 * NC_ * (n - 1) + NC_ + c):
                    dve.wait_ge(f_mm, 2 * NC_ * (n - 1) + NC_ + c + 1)
                v.tensor_copy(qk[c][0:64, :], b_qk[(u + c) % 2][0:64, :]).then_inc(qk_copy, 1)

            def out_():
                dve.wait_ge(o_mm, m + 1)
                o = b_o[:, 0:NT * 204].rearrange("p (h d) -> p h d", d=DH + 1)
                v.tensor_scalar(den[:, :], o[:, :, DH], 1e-6, None, ALU.add).then_inc(o_den, 1)
                dve.wait_ge(o_den, m + 1)
                v.reciprocal(rden[:, :], den[:, :]).then_inc(o_rcp, 1)
                dve.wait_ge(o_rcp, m + 1)
                if exists(m - 1):
                    dve.wait_ge(xaT_mm, m)
                v.tensor_tensor(xa[:, :, :].rearrange("p t (h d) -> p (t h) d", d=DH), o[:, :, 0:DH],
                                rden[:, :].unsqueeze(2).to_broadcast([P, NT * H, DH]), ALU.mult).then_inc(o_ev, 1)

            def v_():
                dve.wait_ge(v_mm, n + 1)
                if exists(n - 2):
                    dve.wait_ge(kv_mm, n - 1)
                v.tensor_copy(va[u][:, :, :, 0:DH].rearrange("p r h d -> p (r h) d"),
                              b_v[:, 0:2 * D].rearrange("p (h d) -> p h d", d=DH)).then_inc(v_ev, 1)

            def kv_():
                dve.wait_ge(kv_mm, n + 1)
                if exists(m):
                    dve.wait_ge(o_mm, m + 1)
                for r in two:
                    ins = v.tensor_scalar(kvb[64 * r:64 * r + 64, :, r, :],
                                          b_v[64 * r:64 * r + 64, 0:204].rearrange("p (h r d) -> p h r d", r=2, d=DH + 1)[:, :, r, :],
                                          1.0 / M, None, ALU.mult)
                ins.then_inc(kv_ev, 1)

            def y_():
                dve.wait_ge(pj_mm, m + 1)
                dve.wait_ge(prep2, m + 1)
                v.tensor_tensor(y[:, :, :], b_o[:, 0:NT * D].rearrange("p (t d) -> p t d", t=NT), xh[w][:, :, :],
                                ALU.add).then_inc(y_ev, 1)
                dve.wait_ge(y_ev, m + 1)
                for t in two:
                    ins = v.bn_stats(bs[:, t, :], y[:, t, :])
                ins.then_inc(y_bs, 1)
                dve.wait_ge(y_bs, 1)
                dve.wait_ge(y_bs, m + 1)
                for t in two:
                    ins = v.bn_aggr(mv[:, t, :], bs[:, t, :])
                ins.then_inc(y_mv, 1)
                dve.wait_ge(y_mv, m + 1)
                if exists(m - 1):
                    dve.wait_ge(y_rs, m)
                v.tensor_scalar(ve[:, :], mv[:, :, 1], 1e-5, None, ALU.add).then_inc(y_ve, 1)

            def h2_():
                dve.wait_ge(y_mv, m + 1)
                for t in two:
                    ins = v.scalar_tensor_tensor(yg[:, t, :], y[:, t, :], mv[:, t, 0:1], gam[:, :], ALU.subtract, ALU.mult)
                ins.then_inc(y_g, 1)
                dve.wait_ge(y_g, m + 1)
                dve.wait_ge(y_rs, m + 1)
                if exists((a if u else a - 1) - 1):
                    dve.wait_ge(s_h2[w], ((a if u else a - 1)) * 32)
                for t in two:
                    ins = v.scalar_tensor_tensor(h2[w][:, t, 0:D], yg[:, t, :], rs[:, t:t + 1], hb[w][:, t, :],
                                                 ALU.mult, ALU.add)
                ins.then_inc(y_h2, 1)
                dve.wait_ge(y_h2, m + 1)
                for t in two:
                    ins = v.bn_stats(bs2[:, t, :], h2[w][:, t, 0:D])
                ins.then_inc(h_bs, 1)
                dve.wait_ge(h_bs, 1)
                dve.wait_ge(h_bs, m + 1)
                for t in two:
                    ins = v.bn_aggr(mv2[:, t, :], bs2[:, t, :])
                ins.then_inc(h_mv, 1)
                dve.wait_ge(h_mv, m + 1)
                if exists(m - 1):
                    dve.wait_ge(h_f, m)
                v.tensor_scalar(ve2[:, :], mv2[:, :, 1], 1.0 + 1e-6 / D, 1e-11 / D, ALU.mult, ALU.add).then_inc(h_ve, 1)

            def xn_():
                dve.wait_ge(h_mv, m + 1)
                dve.wait_ge(h_f, m + 1)
                if exists(m - 1):
                    dve.wait_ge(h_xn, m)
                for t in two:
                    ins = v.tensor_scalar(xc[:, t, :], h2[w][:, t, 0:D], mv2[:, t, 0:1], f2[:, t:t + 1],
                                          ALU.subtract, ALU.mult)
                ins.then_inc(h_xc, 1)

            def xnT_():
                dve.wait_ge(xnT_mm, l + 1)
                if exists(l - 1):
                    dve.wait_ge(lg_mm, l)
                v.tensor_copy(xnT[:, :, :].rearrange("p c s -> p (c s)"), b_x[0:F, :]).then_inc(xnT_ev, 1)

            def lg_():
                dve.wait_ge(lg_mm, l + 1)
                v.reduce_max(mx[:, 0:NT], b_x[:, 0:S].rearrange("p (t n) -> p t n", t=NT), AX.X)
                v.reduce_max(mx[:, NT:NT + GQ], b_x[:, S:2 * S].rearrange("p (t n) -> p t n", t=GQ), AX.X).then_inc(lg_mx, 1)
                dve.wait_ge(lg_mx, l + 1)
                if exists(l - 1):
                    dve.wait_ge(e_c, l)
                if exists(l - 1):
                    dve.wait_ge(e_d, l)
                v.tensor_scalar(nm[:, :], mx[:, :], -1.0, None, ALU.mult).then_inc(lg_nm, 1)

            def cd_():
                dve.wait_ge(cd_mm, l + 1)
                if exists(l - 1):
                    dve.wait_ge(sl_mm, l)
                v.tensor_copy(dT[:, :, :].rearrange("p t n -> p (t n)"), b_x[:, S:2 * S]).then_inc(d_ev, 1)
                if exists(a - 2):
                    dve.wait_ge(s_h2[u], (a - 1) * 32)
                v.tensor_copy(cT[u][:, :], b_x[:, 0:S]).then_inc(c_ev, 1)

            def yn0_(k):
                dve.wait_ge(e_d, k + 1)
                v.scalar_tensor_tensor(zs[:, :], zd[:, :], 1e-6 / D, zd[:, :], ALU.mult, ALU.mult).then_inc(sl_z, 1)
                dve.wait_ge(sl_z, k + 1)
                dve.wait_ge(sl_sq, k + 1)
                if exists(k - 1):
                    dve.wait_ge(sl_r, k)
                v.scalar_tensor_tensor(sse[:, :], ssq[:, :], 1.0 / D, zs[:, :], ALU.mult, ALU.add).then_inc(sl_e, 1)

            def yn_(k, j, pair):
                dve.wait_ge(sl_r, k + 1)
                if exists(pair - 1):
                    dve.wait_ge(s_yn[j], pair * 16 * YN)
                for t in two:
                    for q, b in ((0, b_s), (1, b_v)):
                        ins = v.scalar_tensor_tensor(yn[j][:, 2 * t + q, :], b[:, t * D:(t + 1) * D],
                                                     sr[:, 2 * t + q:2 * t + q + 1], g2r[:, :], ALU.mult, ALU.mult)
                ins.then_inc(sl_y, 1)

            A, B, C, E = step
            if A:
                qk_copy_(0)
            if E:
                yn0_(n - 3)
            if B:
                out_()
            if A:
                qk_copy_(1)
            if C:
                xnT_()
            if E:
                yn_(n - 3, w, a - 1 if u else a - 2)
            if A:
                qk_copy_(2)
            if C:
                lg_()
            if A:
                v_()
            if B:
                y_()
            if A:
                kv_()
            if B:
                h2_()
            if C:
                cd_()
            if B:
                xn_()

        pipeline(dve, iteration, 3)

    @block.scalar
    def _(act):
        f = nc.scalar.activation

        def iteration(a, u, n, step):
            m, l = n - 1, n - 2

            def sq_(c):
                act.wait_ge(qk_mm, NC_ * n + c + 1)
                if exists(2 * NC_ * (n - 1) + NC_ + c):
                    act.wait_ge(f_mm, 2 * NC_ * (n - 1) + NC_ + c + 1)
                f(qk[c][64:128, :], b_qk[(u + c) % 2][64:128, :], ACT.Square).then_inc(qk_sq, 1)

            def ft_(s):
                act.wait_ge(f_mm, 2 * NC_ * n + s + 1)
                if s < NC_:
                    if exists(n - 1):
                        act.wait_ge(kv_mm, n)
                    f(kp[s][:, :, :].rearrange("p r m -> p (r m)"), b_ft[s % 2][:, :], ACT.Exp).then_inc(f_exp, 1)
                else:
                    if exists(n - 1):
                        act.wait_ge(o_mm, n)
                    f(qp[s - NC_][:, :, :].rearrange("p r m -> p (r m)"), b_ft[s % 2][:, :], ACT.Exp).then_inc(f_exp, 1)

            def xaT_():
                act.wait_ge(xaT_mm, m + 1)
                if exists(m - 1):
                    act.wait_ge(pj_mm, m)
                f(xaT[0][:, :], b_o[0:F, 0:S], ACT.Copy)
                f(xaT[1][0:F, :], b_o[0:F, S:2 * S], ACT.Copy).then_inc(xaT_ev, 1)

            def ec_():
                act.wait_ge(lg_nm, l + 1)
                if exists(l - 1):
                    act.wait_ge(cd_mm, l)
                for t in two:
                    ins = f(ec[:, t, :], b_x[:, t * P:(t + 1) * P], ACT.Exp, bias=nm[:, t:t + 1],
                            accum_out=h2[u][:, t, D:D + 1])
                ins.then_inc(e_c, 1)

            def ed_(h):
                if h == 0:
                    if exists(l - 1):
                        act.wait_ge(sl_e, l)
                for q in range(2 * h, 2 * h + 2):
                    ins = f(ed[:, q, :], b_x[:, S + 64 * q:S + 64 * (q + 1)], ACT.Exp, bias=nm[:, NT + q:NT + q + 1],
                            accum_out=zd[:, q:q + 1])
                if h == 1:
                    ins.then_inc(e_d, 1)

            def ss_():
                act.wait_ge(sl_mm, l + 1)
                if exists(l - 1):
                    act.wait_ge(sl_e, l)
                for t in two:
                    for q, b in ((0, b_s), (1, b_v)):
                        ins = f(sqj[:, 2 * t + q, :], b[:, t * D:(t + 1) * D], ACT.Square, accum_out=ssq[:, 2 * t + q:2 * t + q + 1])
                ins.then_inc(sl_sq, 1)

            A, B, C = step
            if A:
                sq_(0)
                sq_(1)
                sq_(2)
                ft_(0)
                ft_(1)
            if B:
                xaT_()
            if C:
                ec_()
            if A:
                ft_(2)
            if C:
                ed_(0)
            if A:
                ft_(3)
            if C:
                ed_(1)
            if A:
                ft_(4)
                ft_(5)
            if C:
                ss_()

        pipeline(act, iteration, 2)

    @block.gpsimd
    def _(pool):
        p = nc.gpsimd

        def iteration(a, u, n, step):
            m, l, w = n - 1, n - 2, 1 - u

            def prep_():
                pool.wait_ge(s_ld[u], (a + 1) * 32)
                if exists(n - 2):
                    pool.wait_ge(y_h2, n - 1)
                for r, c in ((0, C_EVEN), (1, C_ODD)):
                    ins = p.tensor_tensor(hh[u][:, :, r * F:(r + 1) * F], enc[u][:, :, 0:F],
                                          cst[:, c:c + 1].unsqueeze(1).to_broadcast([P, NT, F]), ALU.mult)
                ins.then_inc(prep, 1)
                pool.wait_ge(prep, n + 1)
                p.tensor_tensor(xs[:, :, :], hh[u][:, :, :], enc[u][:, :, F:F + 1].to_broadcast([P, NT, D]),
                                ALU.mult).then_inc(prep1, 1)
                p.tensor_tensor(hb[u][:, :, :], hh[u][:, :, :], bet[:, :].unsqueeze(1).to_broadcast([P, NT, D]), ALU.add)
                pool.wait_ge(prep1, n + 1)
                p.tensor_tensor(xh[u][:, :, :], xs[:, :, :], enc[u][:, :, F + 1:F + 2].to_broadcast([P, NT, D]),
                                ALU.add).then_inc(prep2, 1)

            def rs_():
                pool.wait_ge(y_ve, m + 1)
                if exists(m - 1):
                    pool.wait_ge(y_h2, m)
                p.tensor_tensor(rs[:, :], ve[:, :], half[:, 0:NT], ALU.pow).then_inc(y_rs, 1)

            def f2_():
                pool.wait_ge(h_ve, m + 1)
                if exists(m - 1):
                    pool.wait_ge(h_xc, m)
                p.tensor_tensor(f2[:, :], ve2[:, :], half[:, 0:NT], ALU.pow).then_inc(h_f, 1)

            def xn_():
                pool.wait_ge(h_xc, m + 1)
                if exists(m - 2):
                    pool.wait_ge(xnT_mm, m - 1)
                if exists(m - 2):
                    pool.wait_ge(sl_mm, m - 1)
                p.tensor_tensor(xn[w][:, :, :], xc[:, :, :], gin[:, :].unsqueeze(1).to_broadcast([P, NT, D]),
                                ALU.mult).then_inc(h_xn, 1)

            def sr_(k):
                pool.wait_ge(sl_e, k + 1)
                if exists(k - 1):
                    pool.wait_ge(sl_y, k)
                p.tensor_tensor(sr[:, :], sse[:, :], half[:, 0:GQ], ALU.pow).then_inc(sl_r, 1)

            A, B, _, E = step
            if E:
                sr_(n - 3)
            if A:
                prep_()
            if B:
                rs_()
                f2_()
                xn_()

        pipeline(pool, iteration, 3)


def experts(nc, ctx, sem, sb, bank, g):
    cst, ident, half = g["cst"], g["ident"], g["half"]
    two = range(2)
    yk = sb("yk", [P, TE, D])
    ykT = sb("ykT", [F, 2, TE * P])
    mT = sb("mT", [F, 2, ROWS])
    ws = sb("ws", [F, 2, E2 * D])
    sqj = sb("sqj2", [P, E2, D])
    s_ss = sb("s_ss", [P, E2])
    s_sv = sb("s_sv", [P, E2])
    s_sr = sb("s_sr", [P, E2])
    se = [sb(f"se{i}", [P, E2, D]) for i in two]
    shared = sb("shared", [P, 2 * TE * P])
    seT = shared[0:F, :].rearrange("p (c t n) -> p c t n", c=2, t=TE)
    lm = [[sb(f"lm{o}{i}", [P, 4, P]) for i in two] for o in two]
    mx = [sb(f"mxx{o}", [P, 4]) for o in two]
    nm = [sb(f"nmm{o}", [P, 4]) for o in two]
    ex = [[sb(f"ex{o}{i}", [P, 4, P]) for i in two] for o in two]
    zc = sb("zc", [P, TE])
    rzc = sb("rzc", [P, TE])
    zi = sb("zi", [P, 4])
    rzi = sb("rzi", [P, 4])
    exn = sb("exn", [P, 4, P])
    cmT = sb("cmT", [P, TE, P])
    dm = [sb(f"dm{i}", [P, 4, P]) for i in two]
    s2T = sb("s2T", [F, 2, E2, ROWS])
    w1s = [sb(f"w1s{e}", [F, 2, 2 * HID]) for e in range(E2)]
    w2s = [sb(f"w2s{e}", [P, NHC, D]) for e in range(E2)]
    b1r = sb("b1r", [P, P])
    b1T = sb("b1T", [P, E2 * 2 * NHC])
    b2b = sb("b2b", [P, E2, D])
    gl = [sb(f"gl{i}", [P, ROWS]) for i in two]
    aT = [sb(f"aT{i}", [P, NHC, ROWS]) for i in two]
    os_ = [sb(f"os{i}", [P, ROWS // P, D]) for i in two]
    oS = sb("oS", [P, TE, D])
    o2 = shared[:, 0:TE * D].rearrange("p (t d) -> p t d", t=TE)

    s_yk, s_ws, s_b = sem("yk_loaded"), sem("ws_loaded"), sem("b_loaded")
    s_w = [sem(f"w_loaded{e}") for e in range(E2)]
    s_zero = sem("b1_cleared")
    b1_mm, b1_ev = sem("b1_mm"), sem("b1_ev")
    yT_mm, yT_ev, mean = sem("yT_mm"), sem("yT_ev"), sem("mean")
    se_mm, se_sq, se_v, se_r, se_n = (sem(n) for n in ("se_mm", "se_sq", "se_v", "se_r", "se_n"))
    seT_mm, seT_e0, seT_e1 = (sem(n) for n in ("seT_mm", "seT_e0", "seT_e1"))
    l_mm, l_add, l_max, l_neg, l_exp = (sem(n) for n in ("l_mm", "l_add", "l_max", "l_neg", "l_exp"))
    z_r, e_n, t_mm, t_c, t_d = (sem(n) for n in ("z_r", "e_n", "t_mm", "t_c", "t_d"))
    s2_mm, s2_e0, s2_e1 = (sem(n) for n in ("s2_mm", "s2_e0", "s2_e1"))
    u_mm, u_gl, u_act, o_mm, o_ev = (sem(n) for n in ("u_mm", "u_gelu", "u_act", "oo_mm", "oo_ev"))
    s_os = [sem(f"shuffled{i}") for i in two]
    x_mm, x_rz, x_ev, s_o2 = (sem(n) for n in ("x_mm", "x_rz", "x_ev", "o2_stored"))
    block = ctx.enter_context(nc.Block())
    SH = 4
    NQ = TE // 4
    NR = ROWS // P

    def each_expert(eng, body):
        body(0)
        with eng.Fori(1, NE, 1) as k:
            body(k)

    @block.sync
    def _(sp):
        def body(k):
            if isinstance(k, int):
                sp.wait_ge(s_zero, 1)
            if exists(NQ * (k - 1) + NQ - 1):
                sp.wait_ge(s2_mm, 1)
                sp.wait_ge(s2_mm, NQ * (k - 1) + NQ)
            sp.dma_start(yk[:, :, :], g["yn_d"].rearrange("e (t a) s d -> e (a s) t d", a=GT)[k]).then_inc(s_yk, 16)
            if exists(NR * (k - 1) + NR - 1):
                sp.wait_ge(se_mm, 1)
                sp.wait_ge(se_mm, NR * (k - 1) + NR)
            sp.dma_start(ws[:, :, :], g["w_slot2"].rearrange("e (c p) n -> e p c n", c=2)[k]).then_inc(s_ws, 16)
            if exists(16 * (k - 1) + 15):
                sp.wait_ge(u_act, 1)
                sp.wait_ge(u_act, 16 * (k - 1) + 16)
            sp.dma_start(b1r[0:E2 * 2 * NHC, :], g["b1"].rearrange("k e (c p) -> k (e c) p", p=P)[k]).then_inc(s_b, 16)
            if exists(8 * (k - 1) + 7):
                sp.wait_ge(o_ev, 1)
                sp.wait_ge(o_ev, 8 * (k - 1) + 8)
            sp.dma_start(b2b[:, :, :], g["b2"][k].partition_broadcast(P)).then_inc(s_b, 16)
            for e in range(E2):
                sp.dma_start(w1s[e][:, :, :], g["w1"].rearrange("k e (c p) n -> k e p c n", c=2)[k, e]).then_inc(s_w[e], 16)
                sp.dma_start(w2s[e][:, :, :], g["w2"].rearrange("k e (c p) n -> k e p c n", p=P)[k, e]).then_inc(s_w[e], 16)
            for e in range(E2):
                sp.wait_ge(o_ev, 1)
                sp.wait_ge(o_ev, 8 * k + 2 * e + 2)
                if e == 0:
                    if exists(8 * (k - 1) + 7):
                        sp.wait_ge(x_mm, 1)
                        sp.wait_ge(x_mm, 8 * (k - 1) + 8)
                for j in range(4):
                    sp.dma_start(oS[:, :, :].rearrange("p (r j) d -> p j r d", j=4)[32 * e:32 * e + 32, j, :, :],
                                 os_[e % 2][32 * j:32 * j + 32, :, :]).then_inc(s_os[e % 2], 16)
            sp.wait_ge(x_ev, 1)
            sp.wait_ge(x_ev, 8 * k + 8)
            sp.dma_start(g["o2_d"].rearrange("e (t a) s d -> e (a s) t d", a=GT)[k], o2[:, :, :]).then_inc(s_o2, 16)

        each_expert(sp, body)
        sp.wait_ge(s_o2, 16 * NE)

    @block.tensor
    def _(pe):
        mm, tr = nc.tensor.matmul, nc.tensor.transpose

        def body(k):
            pe.wait_ge(s_b, (k + 1) * 32)
            tr(bank[7][:, 0:P], b1r[:, :], ident).then_inc(b1_mm, 1)
            pe.wait_ge(s_yk, 16 * k + 16)
            for i in range(TE // 2):
                b = bank[i % 2]
                if exists(8 * k + i - 2):
                    pe.wait_ge(yT_ev, 8 * k + i - 1)
                if i < 2:
                    if exists(8 * (k - 1) + 6 + i):
                        pe.wait_ge(x_ev, 8 * (k - 1) + 6 + i + 1)
                for c in two:
                    for t in two:
                        ins = tr(b[0:F, (2 * c + t) * P:(2 * c + t + 1) * P], yk[:, 2 * i + t, c * F:(c + 1) * F], ident)
                ins.then_inc(yT_mm, 1)

            def se2(r):
                if r == 0:
                    pe.wait_ge(mean, 8 * k + 8)
                    pe.wait_ge(s_ws, 16 * k + 16)
                if exists(NR * k + r - 2):
                    pe.wait_ge(se_n, NR * k + r - 1)
                for h in two:
                    for c in two:
                        ins = mm(bank[2 + 2 * (r % 2) + h][:, 0:2 * D], mT[:, c, r * P:(r + 1) * P],
                                 ws[:, c, h * 2 * D:(h + 1) * 2 * D], start=c == 0, stop=c == 1)
                ins.then_inc(se_mm, 1)

            def seT_(r):
                pe.wait_ge(se_n, NR * k + r + 1)
                if r == 0:
                    pe.wait_ge(yT_ev, 8 * k + 8)
                else:
                    pe.wait_ge(seT_e0, NR * k + r)
                    pe.wait_ge(seT_e1, NR * k + r)
                for c in two:
                    for e in range(E2):
                        ins = tr(bank[c][0:F, e * P:(e + 1) * P], se[r % 2][:, e, c * F:(c + 1) * F], ident)
                ins.then_inc(seT_mm, 1)

            se2(0)
            se2(1)
            seT_(0)
            se2(2)
            seT_(1)
            se2(3)
            seT_(2)
            seT_(3)

            def logits(q):
                if q == 0:
                    pe.wait_ge(seT_e0, NR * k + NR)
                    pe.wait_ge(seT_e1, NR * k + NR)
                if exists(NQ * k + q - 2):
                    pe.wait_ge(l_add, NQ * k + q - 1)
                for j in range(4):
                    t = 4 * q + j
                    for c in two:
                        mm(bank[2 + q % 2][:, j * P:(j + 1) * P], ykT[:, c, t * P:(t + 1) * P],
                           seT[:, c, t, :], start=c == 0, stop=c == 1)
                for j in range(4):
                    t = 4 * q + j
                    for c in two:
                        ins = mm(bank[4 + q % 2][:, j * P:(j + 1) * P], seT[:, c, t, :],
                                 ykT[:, c, t * P:(t + 1) * P], start=c == 0, stop=c == 1)
                ins.then_inc(l_mm, 1)

            def turn(q):
                pe.wait_ge(l_exp, NQ * k + q + 1)
                pe.wait_ge(e_n, NQ * k + q + 1)
                if exists(NQ * k + q - 1):
                    pe.wait_ge(t_c, NQ * k + q)
                if exists(NQ * k + q - 1):
                    pe.wait_ge(t_d, NQ * k + q)
                for j in range(4):
                    tr(bank[0][:, j * P:(j + 1) * P], ex[0][q % 2][:, j, :], ident)
                for j in range(4):
                    ins = tr(bank[1][:, j * P:(j + 1) * P], exn[:, j, :], ident)
                ins.then_inc(t_mm, 1)

            def slots2(q):
                pe.wait_ge(t_d, NQ * k + q + 1)
                if exists(NQ * k + q - 1):
                    pe.wait_ge(s2_e0, NQ * k + q)
                if exists(NQ * k + q - 1):
                    pe.wait_ge(s2_e1, NQ * k + q)
                for c in two:
                    for j in range(4):
                        ins = mm(bank[6 + c][0:F, j * P:(j + 1) * P], yk[:, 4 * q + j, c * F:(c + 1) * F],
                                 dm[q % 2][:, j, :], start=True, stop=True)
                ins.then_inc(s2_mm, 1)

            for q in range(NQ + 2):
                if q < NQ:
                    logits(q)
                if 0 <= q - 1 < NQ:
                    turn(q - 1)
                if 0 <= q - 2:
                    slots2(q - 2)

            def up(e, h):
                i = 16 * k + NHC * e + h
                if h == 0:
                    pe.wait_ge(s_w[e], 32 * k + 32)
                if e == 0 and h == 0:
                    pe.wait_ge(s2_e0, NQ * k + NQ)
                    pe.wait_ge(s2_e1, NQ * k + NQ)
                if exists(i - 2):
                    pe.wait_ge(u_act, i - 1)
                for b, off in ((4, HID), (2, 0)):
                    for c in two:
                        ins = mm(bank[b + h % 2][:, :], w1s[e][:, c, off + h * P:off + (h + 1) * P], s2T[:, c, e, :],
                                 start=c == 0, stop=c == 1)
                ins.then_inc(u_mm, 1)

            def down(e):
                for i in two:
                    if exists(8 * k + 2 * e + i - 2):
                        pe.wait_ge(o_ev, 8 * k + 2 * e + i - 1)
                    if i == 0:
                        pe.wait_ge(u_act, 16 * k + NHC * e + NHC)
                    for r in range(2 * i, 2 * i + 2):
                        for h in range(NHC):
                            ins = mm(bank[6 + i][:, (r % 2) * D:(r % 2 + 1) * D], aT[e % 2][:, h, r * P:(r + 1) * P],
                                     w2s[e][:, h, :], start=h == 0, stop=h == NHC - 1)
                    ins.then_inc(o_mm, 1)

            for e in range(E2):
                for h in range(NHC):
                    up(e, h)
                    if h == 0 and e > 0:
                        down(e - 1)
            down(E2 - 1)
            for i in range(TE // 2):
                if i == 0:
                    for j in two:
                        pe.wait_ge(s_os[j], (2 * k + 2) * 16 * SH)
                    pe.wait_ge(t_c, NQ * k + NQ)
                    pe.wait_ge(t_d, NQ * k + NQ)
                else:
                    if i > 1:
                        pe.wait_ge(x_ev, 8 * k + i - 1)
                for t in two:
                    ins = mm(bank[i % 2][:, t * D:(t + 1) * D], cmT[:, 2 * i + t, :], oS[:, 2 * i + t, :], start=True, stop=True)
                ins.then_inc(x_mm, 1)

        each_expert(pe, body)

    @block.vector
    def _(dve):
        v = nc.vector
        v.memset(b1r[:, :], 0.0).then_inc(s_zero, 1)

        def body(k):
            dve.wait_ge(b1_mm, k + 1)
            v.tensor_copy(b1T[:, :], bank[7][:, 0:E2 * 2 * NHC]).then_inc(b1_ev, 1)
            for i in range(TE // 2):
                dve.wait_ge(yT_ev, 8 * k + i + 1)
                if i == 0:
                    if exists(NR * (k - 1) + NR - 1):
                        dve.wait_ge(se_mm, NR * (k - 1) + NR)
                v.reduce_sum(mT[:, :, 64 * i:64 * i + 64],
                             ykT[:, :, 256 * i:256 * (i + 1)].rearrange("p c (r n) -> p c r n", n=4), AX.X).then_inc(mean, 1)
            for r in range(NR):
                if r >= 1:
                    if r == 1:
                        if exists(k - 1):
                            dve.wait_ge(s_o2, k * 16)
                    dve.wait_ge(seT_mm, NR * k + r)
                    v.tensor_copy(seT[:, 1, 4 * r - 4:4 * r, :].rearrange("p t (e n) -> p t e n", e=E2),
                                  bank[1][0:F, :].rearrange("p (e t n) -> p t e n", e=E2, t=4)).then_inc(seT_e1, 1)
                dve.wait_ge(se_sq, NR * k + r + 1)
                if exists(NR * k + r - 1):
                    dve.wait_ge(se_r, NR * k + r)
                v.tensor_scalar(s_sv[:, :], s_ss[:, :], 1.0 / D, NS * 1e-6 / D, ALU.mult, ALU.add).then_inc(se_v, 1)
                dve.wait_ge(se_r, NR * k + r + 1)
                if exists(NR * k + r - 2):
                    dve.wait_ge(seT_mm, NR * k + r - 1)
                for h in two:
                    ins = v.tensor_tensor(se[r % 2][:, 2 * h:2 * h + 2, :],
                                          bank[2 + 2 * (r % 2) + h][:, 0:2 * D].rearrange("p (e d) -> p e d", e=2),
                                          s_sr[:, 2 * h:2 * h + 2].unsqueeze(2).to_broadcast([P, 2, D]), ALU.mult)
                ins.then_inc(se_n, 1)
            dve.wait_ge(seT_mm, NR * k + NR)
            v.tensor_copy(seT[:, 1, 4 * NR - 4:4 * NR, :].rearrange("p t (e n) -> p t e n", e=E2),
                              bank[1][0:F, :].rearrange("p (e t n) -> p t e n", e=E2, t=4)).then_inc(seT_e1, 1)

            def soft(q):
                i = NQ * k + q
                dve.wait_ge(l_mm, i + 1)
                if exists(i - 2):
                    dve.wait_ge(l_exp, i - 1)
                for o in two:
                    ins = v.tensor_tensor(lm[o][q % 2][:, :, :],
                                          bank[2 + 2 * o + q % 2][:, :].rearrange("p (j n) -> p j n", j=4),
                                          cst[:, C_M1 + o * P:C_M1 + (o + 1) * P].unsqueeze(1).to_broadcast([P, 4, P]), ALU.add)
                ins.then_inc(l_add, 1)
                dve.wait_ge(l_add, i + 1)
                for o in two:
                    ins = v.reduce_max(mx[o][:, :], lm[o][q % 2][:, :, :], AX.X)
                ins.then_inc(l_max, 1)
                dve.wait_ge(l_max, i + 1)
                if exists(i - 1):
                    dve.wait_ge(l_exp, i)
                for o in two:
                    ins = v.tensor_scalar(nm[o][:, :], mx[o][:, :], -1.0, None, ALU.mult)
                ins.then_inc(l_neg, 1)

            def recip(q):
                i = NQ * k + q
                dve.wait_ge(l_exp, i + 1)
                if exists(i - 1):
                    dve.wait_ge(e_n, i)
                v.reciprocal(rzi[:, :], zi[:, :]).then_inc(z_r, 1)

            def copy_c(q):
                i = NQ * k + q
                dve.wait_ge(t_mm, i + 1)
                if q == 0:
                    if exists(8 * (k - 1) + 7):
                        dve.wait_ge(x_mm, 8 * (k - 1) + 8)
                v.tensor_copy(cmT[:, 4 * q:4 * q + 4, :].rearrange("p t n -> p (t n)"), bank[0][:, :]).then_inc(t_c, 1)

            def copy_s(q):
                i = NQ * k + q
                dve.wait_ge(s2_mm, i + 1)
                if q == 0:
                    if exists(16 * (k - 1) + 15):
                        dve.wait_ge(u_mm, 16 * (k - 1) + 16)
                v.tensor_copy(s2T[:, 1, :, P * q:P * (q + 1)].rearrange("p e (j n) -> p j e n", j=4),
                              bank[7][0:F, :].rearrange("p (j e n) -> p j e n", j=4, e=E2)).then_inc(s2_e1, 1)

            for q in range(NQ + 2):
                if q < NQ:
                    soft(q)
                if 0 <= q - 1 < NQ:
                    copy_c(q - 1)
                if q < NQ:
                    recip(q)
                if 0 <= q - 2:
                    copy_s(q - 2)
            v.reciprocal(rzc[:, :], zc[:, :]).then_inc(x_rz, 1)

            def down_(e):
                for i in two:
                    dve.wait_ge(o_mm, 8 * k + 2 * e + i + 1)
                    if i == 0:
                        if exists(2 * k + e // 2 - 1):
                            dve.wait_ge(s_os[e % 2], (2 * k + e // 2) * 16 * SH)
                    v.tensor_tensor(os_[e % 2][:, 2 * i:2 * i + 2, :],
                                    bank[6 + i][:, 0:2 * D].rearrange("p (r d) -> p r d", r=2),
                                    b2b[:, e, :].unsqueeze(1).to_broadcast([P, 2, D]), ALU.add).then_inc(o_ev, 1)

            for e in range(E2):
                for h in range(NHC):
                    i = 16 * k + NHC * e + h
                    if h == 0 and e >= 2:
                        dve.wait_ge(o_mm, 8 * k + 2 * (e - 2) + 2)
                    dve.wait_ge(u_gl, i + 1)
                    c = e * 2 * NHC + h
                    v.scalar_tensor_tensor(aT[e % 2][:, h, :], bank[2 + h % 2][:, :], b1T[:, c:c + 1], gl[h % 2][:, :],
                                           ALU.add, ALU.mult).then_inc(u_act, 1)
                    if h == 0 and e > 0:
                        down_(e - 1)
            down_(E2 - 1)
            dve.wait_ge(x_rz, k + 1)
            for i in range(TE // 2):
                dve.wait_ge(x_mm, 8 * k + i + 1)
                if i == 0:
                    if exists(k - 1):
                        dve.wait_ge(s_o2, k * 16)
                v.tensor_tensor(o2[:, 2 * i:2 * i + 2, :], bank[i % 2][:, 0:2 * D].rearrange("p (t d) -> p t d", t=2),
                                rzc[:, 2 * i:2 * i + 2].unsqueeze(2).to_broadcast([P, 2, D]), ALU.mult).then_inc(x_ev, 1)

        each_expert(dve, body)

    @block.scalar
    def _(act):
        f = nc.scalar.activation

        def body(k):
            for i in range(TE // 2):
                act.wait_ge(yT_mm, 8 * k + i + 1)
                f(ykT[:, :, 256 * i:256 * (i + 1)], bank[i % 2][0:F, :].rearrange("p (c n) -> p c n", c=2),
                  ACT.Copy).then_inc(yT_ev, 1)
            for r in range(NR):
                act.wait_ge(se_mm, NR * k + r + 1)
                if exists(NR * k + r - 1):
                    act.wait_ge(se_v, NR * k + r)
                for e in range(E2):
                    ins = f(sqj[:, e, :], bank[2 + 2 * (r % 2) + e // 2][:, (e % 2) * D:(e % 2 + 1) * D], ACT.Square,
                            accum_out=s_ss[:, e:e + 1])
                ins.then_inc(se_sq, 1)
                if r >= 1:
                    if r == 1:
                        if exists(k - 1):
                            act.wait_ge(s_o2, k * 16)
                    act.wait_ge(seT_mm, NR * k + r)
                    f(seT[:, 0, 4 * r - 4:4 * r, :].rearrange("p t (e n) -> p t e n", e=E2),
                                  bank[0][0:F, :].rearrange("p (e t n) -> p t e n", e=E2, t=4), ACT.Copy).then_inc(seT_e0, 1)
            act.wait_ge(seT_mm, NR * k + NR)
            f(seT[:, 0, 4 * NR - 4:4 * NR, :].rearrange("p t (e n) -> p t e n", e=E2),
                              bank[0][0:F, :].rearrange("p (e t n) -> p t e n", e=E2, t=4), ACT.Copy).then_inc(seT_e0, 1)

            def exps(q):
                i = NQ * k + q
                act.wait_ge(l_neg, i + 1)
                if exists(i - 2):
                    act.wait_ge(t_mm, i - 1)
                if exists(i - 1):
                    act.wait_ge(e_n, i)
                if q == 0:
                    if exists(k - 1):
                        act.wait_ge(x_rz, k)
                for o in two:
                    for j in range(4):
                        z = zi[:, j:j + 1] if o else zc[:, 4 * q + j:4 * q + j + 1]
                        ins = f(ex[o][q % 2][:, j, :], lm[o][q % 2][:, j, :], ACT.Exp, bias=nm[o][:, j:j + 1], accum_out=z)
                ins.then_inc(l_exp, 1)

            def copy_d(q):
                i = NQ * k + q
                act.wait_ge(t_mm, i + 1)
                if exists(i - 2):
                    act.wait_ge(s2_mm, i - 1)
                f(dm[q % 2][:, :, :].rearrange("p j n -> p (j n)"), bank[1][:, :], ACT.Copy).then_inc(t_d, 1)

            def copy_s(q):
                act.wait_ge(s2_mm, NQ * k + q + 1)
                if q == 0:
                    if exists(16 * (k - 1) + 15):
                        act.wait_ge(u_mm, 16 * (k - 1) + 16)
                f(s2T[:, 0, :, P * q:P * (q + 1)].rearrange("p e (j n) -> p j e n", j=4),
                  bank[6][0:F, :].rearrange("p (j e n) -> p j e n", j=4, e=E2), ACT.Copy).then_inc(s2_e0, 1)

            for q in range(NQ + 2):
                if q < NQ:
                    exps(q)
                if 0 <= q - 1 < NQ:
                    copy_d(q - 1)
                if 0 <= q - 2:
                    copy_s(q - 2)
            act.wait_ge(b1_ev, k + 1)
            for e in range(E2):
                for h in range(NHC):
                    i = 16 * k + NHC * e + h
                    act.wait_ge(u_mm, i + 1)
                    if exists(i - 2):
                        act.wait_ge(u_act, i - 1)
                    c = e * 2 * NHC + NHC + h
                    f(gl[h % 2][:, :], bank[4 + h % 2][:, :], ACT.Gelu_apprx_tanh, bias=b1T[:, c:c + 1]).then_inc(u_gl, 1)

        each_expert(act, body)

    @block.gpsimd
    def _(pool):
        p = nc.gpsimd

        def body(k):
            for r in range(NR):
                i = NR * k + r
                pool.wait_ge(se_v, i + 1)
                if exists(i - 1):
                    pool.wait_ge(se_n, i)
                p.tensor_tensor(s_sr[:, :], s_sv[:, :], half[:, 0:E2], ALU.pow).then_inc(se_r, 1)
            for q in range(NQ):
                i = NQ * k + q
                pool.wait_ge(z_r, i + 1)
                if exists(i - 1):
                    pool.wait_ge(t_mm, i)
                p.tensor_tensor(exn[:, :, :], ex[1][q % 2][:, :, :], rzi[:, :].unsqueeze(2).to_broadcast([P, 4, P]),
                                ALU.mult).then_inc(e_n, 1)

        each_expert(pool, body)


def combine(nc, ctx, sem, sb, bank, g):
    two = range(2)
    o2 = [sb(f"o2b{i}", [P, GQ, D]) for i in two]
    cT = [sb(f"cTb{i}", [P, S]) for i in two]
    h2 = [sb(f"h2b{i}", [P, NT, D + 1]) for i in two]
    rz = sb("rzb", [P, 2, NT])
    ob = [sb(f"ob{i}", [P, NT, D]) for i in two]
    s_ld = [sem(f"c_loaded{i}") for i in two]
    s_st = [sem(f"c_stored{i}") for i in two]
    c_mm, c_rz, c_ev = sem("c_mm"), sem("c_rz"), sem("c_out")
    block = ctx.enter_context(nc.Block())
    LD = GQ + 2

    def each_pair(eng, body):
        for u in two:
            body(0, u)
        with eng.Fori(1, NB // 2, 1) as a:
            for u in two:
                body(a, u)

    @block.sync
    def _(sp):
        def body(a, u):
            n = 2 * a + u
            if exists(n - 2):
                sp.wait_ge(c_ev, 1)
                sp.wait_ge(c_ev, n - 1)
            for q in range(GQ):
                sp.dma_start(o2[u][:, q, :], g["o2_d"].rearrange("e (b q) s d -> b q e s d", q=GQ)[n, q]).then_inc(s_ld[u], 16)
            sp.dma_start(cT[u][:, :], g["combT_d"][n]).then_inc(s_ld[u], 16)
            sp.dma_start(h2[u][:, :, :], g["h2_d"][n]).then_inc(s_ld[u], 16)

        each_pair(sp, body)

    @block.tensor
    def _(pe):
        def body(a, u):
            n = 2 * a + u
            pe.wait_ge(s_ld[u], (a + 1) * 16 * LD)
            if exists(n - 2):
                pe.wait_ge(c_ev, n - 1)
            for t in two:
                for q in two:
                    c = t * P + 64 * q
                    ins = nc.tensor.matmul(bank[u][64 * q:64 * q + 64, t * D:(t + 1) * D], cT[u][:, c:c + 64],
                                           o2[u][:, 2 * t + q, :], start=True, stop=True)
            ins.then_inc(c_mm, 1)

        each_pair(pe, body)

    @block.vector
    def _(dve):
        def body(a, u):
            n = 2 * a + u
            dve.wait_ge(s_ld[u], (a + 1) * 16 * LD)
            if exists(n - 2):
                dve.wait_ge(c_ev, n - 1)
            nc.vector.reciprocal(rz[:, u, :], h2[u][:, :, D]).then_inc(c_rz, 1)
            dve.wait_ge(c_rz, n + 1)
            dve.wait_ge(c_mm, n + 1)
            if exists(a - 1):
                dve.wait_ge(s_st[u], a * 16 * GQ)
            for t in two:
                ins = nc.vector.scalar_tensor_tensor(ob[u][:, t, :], bank[u][:, t * D:(t + 1) * D], rz[:, u, t:t + 1],
                                                     h2[u][:, t, 0:D], ALU.mult, ALU.add)
            ins.then_inc(c_ev, 1)

        each_pair(dve, body)

    @block.scalar
    def _(act):
        def body(a, u):
            n = 2 * a + u
            act.wait_ge(c_ev, n + 1)
            for q in range(GQ):
                act.dma_start(g["out"].rearrange("b (q j r) d -> b q r j d", r=2, j=32)[n, q],
                              ob[u][64 * (q % 2):64 * (q % 2) + 64, q // 2, :]).then_inc(s_st[u], 16)

        each_pair(act, body)
        for u in two:
            act.wait_ge(s_st[u], 16 * GQ * NB // 2)


_INS = ["x", "consts", "rows", "L0_tok_scale", "L0_attn_W_qkv", "L0_attn_W_proj", "L0_attn_b_proj", "L0_attn_gamma",
        "L0_attn_beta", "L0_attn_random_features", "L0_ffn_gamma_in", "L0_ffn_slots1", "L0_ffn_gamma2",
        "L0_ffn_w_slot2", "L0_ffn_w1", "L0_ffn_b1", "L0_ffn_w2", "L0_ffn_b2"]


def kernel(**inputs):
    import concourse.bacc as _bacc
    from concourse.bass_utils import run_bass_kernel_spmd as _run

    inputs["consts"], inputs["rows"] = shape_constants()
    nc = _bacc.Bacc("TRN2", target_bir_lowering=False, num_devices=1)
    arrays, args = {}, []
    for name in _INS:
        a = np.ascontiguousarray(inputs[name])
        arrays[f"in_{name}"] = a
        args.append(nc.dram_tensor(f"in_{name}", a.shape, mybir.dt.from_np(a.dtype), kind="ExternalInput").ap())
    args.append(nc.dram_tensor("out_0", (NB, S, D), F32, kind="ExternalOutput").ap())
    build(nc, *args)
    r = _run(nc, [arrays], core_ids=[0])
    return r.results[0]["out_0"]
```

```python
import concourse.bass as bass
from concourse import mybir
from contextlib import ExitStack
import numpy as np

F32 = mybir.dt.float32
F32R = mybir.dt.float32r
I32 = mybir.dt.int32
ALU = mybir.AluOpType
ACT = mybir.ActivationFunctionType
AX = mybir.AxisListType

NB, S, D = 32, 256, 192
F = D // 2
P = 128
GQ = S // 64
NT = S // P
H, DH, M = 12, 16, 64
HC = 4
NC_ = H // HC
NG = NB * GQ
NE, NS, E2 = 8, 16, 4
M2 = NS // E2
HID = 512
NHC = HID // P
ROWS = NG * M2
TE = NG * NS // P
GT = P // NS
CB = 4
CT = CB * NT
HX = F + 2

TWO_PI = 2.0 * np.pi
ROUND = float(1.5 * 2.0**23)
PI_HI = 6.28125
PI_LO = float(np.float32(TWO_PI - PI_HI))
PI_MAX = 3.1415925

C_ID, C_MRF, C_INV, C_M1, C_EVEN, C_ODD, C_QUART, C_END = np.cumsum([0, P, HC * M, F, P, 1, 1, 1]).tolist()


def shape_constants():
    c = np.zeros((P, C_END), np.float32)
    c[:, C_ID:C_ID + P] = np.eye(P)
    for p in range(P):
        h = (p % 64) // DH
        c[p, C_MRF + h * M:C_MRF + (h + 1) * M] = 1.0 if p < 64 else -0.5
    c[:, C_INV:C_INV + F] = (1.0 / 10000.0 ** (2.0 * np.floor(np.arange(F) / 2.0) / F)).astype(np.float32)
    row = np.arange(P)
    slot_group = row // (NS * GQ) * GQ + row % GQ
    inner_group = row % (P // E2) // (M2 * GQ) * GQ + row % GQ
    other = np.where(slot_group[:, None] == inner_group[None, :], 0.0, -1e30)
    c[:, C_M1:C_M1 + P] = other
    odd = row % 2
    c[:, C_EVEN] = 1 - odd
    c[:, C_ODD] = odd
    c[:, C_QUART] = odd * (np.pi / 2)
    rows = np.zeros((NB, 2, S), np.float32)
    rows[:, 0] = np.arange(S) + 1
    rows[:, 1] = np.arange(S) % 2 == 0
    return c, rows


def exists(index):
    return not isinstance(index, int) or index >= 0


def build(nc, x, consts, rows, tok_scale, W_qkv, W_proj, b_proj, gamma, beta, rf, gamma_in, slots1,
          gamma2, w_slot2, w1, b1, w2, b2, out):
    rank_d = nc.dram_tensor("rank_d", (NB, S), F32).ap()
    enc_d = nc.dram_tensor("enc_d", (NB, P, NT, HX), F32).ap()
    encT_d = nc.dram_tensor("encT_d", (NB, F + 1, S), F32).ap()
    h2_d = nc.dram_tensor("h2_d", (NB, P, NT, D + 1), F32).ap()
    combT_d = nc.dram_tensor("combT_d", (NB, P, S), F32).ap()
    yn_d = nc.dram_tensor("yn_d", (NB, NE, NS, GQ, D), F32).ap()
    o2_d = nc.dram_tensor("o2_d", (NB, NE, NS, GQ, D), F32).ap()

    ctx = ExitStack()
    with ctx:
        def sem(name):
            return ctx.enter_context(nc.semaphore(name))

        def sb(name, shape, dt=F32, c=ctx):
            return c.enter_context(nc.sbuf_tensor(name, shape, dt))

        cst = sb("cst", [P, C_END])
        half = sb("half", [P, 8])
        ident = cst[:, C_ID:C_ID + P]
        bank = [ctx.enter_context(nc.psum_tensor(f"bank{i}", [P, 512], F32)) for i in range(8)]
        with ExitStack() as cw:
            wv = [sb(f"wv{i}", [F + 1, D], c=cw) for i in range(2)]
            wqk = [sb(f"wqk{i}", [F + 1, 2 * NC_, 2, HC * DH], c=cw) for i in range(2)]
            rfa = sb("rfa", [P, HC, M], c=cw)
            wp = [sb("wp0", [F, D], c=cw), sb("wp1", [F + 1, D], c=cw)]
            phiT = sb("phiT", [F, 2, P], c=cw)
            gam = sb("gam", [P, D], c=cw)
            bet = sb("bet", [P, D], c=cw)
            gin = sb("gin", [P, D], c=cw)
            g2r = sb("g2r", [P, D], c=cw)
            with ExitStack() as c0:
                encode(nc, c0, sem, lambda n, s, dt=F32: sb(n, s, dt, c0), bank, locals())
            with ExitStack() as c1:
                attend(nc, c1, sem, lambda n, s, dt=F32: sb(n, s, dt, c1), bank, locals())
        with ExitStack() as c2:
            experts(nc, c2, sem, lambda n, s, dt=F32: sb(n, s, dt, c2), bank, locals())
        with ExitStack() as c3:
            combine(nc, c3, sem, lambda n, s, dt=F32: sb(n, s, dt, c3), bank, locals())


def encode(nc, ctx, sem, sb, bank, g):
    cst, ident, half = g["cst"], g["ident"], g["half"]
    wv, wqk, rfa, wp, phiT = g["wv"], g["wqk"], g["rfa"], g["wp"], g["phiT"]
    xi = sb("xi", [NB, S], I32)
    row = sb("row", [NB, 2, S])
    xf = sb("xf", [NB, S])
    keep = sb("keep", [NB, S])
    tmp = sb("tmp", [NB, S])
    one = sb("one", [NB, S])
    cum = sb("cum", [NB, 3, S])
    perm = sb("perm", [NB, 3, S])
    small = sb("small", [NB, 4])
    tabs = sb("tabs", [P, 3, NB * NT])
    wraw = [sb(f"wraw{i}", [F, 3 * D]) for i in range(2)]
    ones = sb("ones", [F, F + 1])
    rfn = sb("rfn", [M, DH])
    rfr = sb("rfr", [M, HC, DH])
    sl = sb("sl", [P, D])
    sq1 = sb("sq1", [P, D])
    phn = sb("phn", [P, D])
    r1 = sb("r1", [P, 4])
    cb = sb("cb", [P, CB, S])
    kk = sb("kk", [P, 3, CT])
    kp = sb("kept", [P, CT])
    junk = sb("junk", [P, CT, S])
    cnt = sb("cnt", [P, CT])
    psc = sb("psc", [P, CT])
    ang = sb("ang", [P, CT, F])
    nr = sb("nr", [P, CT, F])
    nr2 = sb("nr2", [P, CT, F])
    rd = sb("rd", [P, CT, F])
    rd2 = sb("rd2", [P, CT, F])
    rd3 = sb("rd3", [P, CT, F])
    sn = sb("sn", [P, CT, F])
    he = sb("he", [P, CT, HX])
    hsq = sb("hsq", [P, CT, F])
    st = sb("st", [P, 8, CT])
    et = sb("et", [P, CT, F + 1])
    etT = sb("etT", [F + 1, CB, 2, P])

    s_x, s_c, s_w, s_half = sem("p0_x"), sem("p0_const"), sem("p0_weights"), sem("p0_half")
    s_cum, s_rank_d = sem("p0_ranks"), sem("p0_rank_stored")
    s_pe = sem("p0_products")
    s_ones, s_rfr = sem("p0_ones"), sem("p0_rfr")
    s_ssq, s_pw, s_phn = sem("p0_ssq"), sem("p0_pow"), sem("p0_phn")
    chain = sem("p0_dve_chain")
    s_cb, s_pos, s_ang = sem("enc_cb"), sem("enc_position"), sem("enc_angle")
    s_red, s_sin_in, s_sin = sem("enc_reduce"), sem("enc_reduced"), sem("enc_sin")
    s_he, s_hsq = sem("enc_he"), sem("enc_squares")
    s_var, s_ve, s_rs, s_mr = sem("enc_var"), sem("enc_ve"), sem("enc_rstd"), sem("enc_mr")
    s_et, s_etT_mm, s_etT = sem("enc_et"), sem("enc_etT_mm"), sem("enc_etT")
    s_std, s_stdT = sem("enc_stored"), sem("encT_stored")
    block = ctx.enter_context(nc.Block())

    def chunks(eng, head, tail):
        n = NB // CB

        def step(i):
            head(i)
            tail(i - 1)

        head(0)
        step(1)
        with eng.Fori(2, n, 1) as i:
            step(i)
        tail(n - 1)

    @block.sync
    def _(sp):
        sp.dma_start(xi[:, :], g["x"]).then_inc(s_x, 16)
        sp.dma_start(row[:, :, :], g["rows"]).then_inc(s_x, 16)
        sp.dma_start(small[:, 0:1], g["tok_scale"].partition_broadcast(NB)).then_inc(s_x, 16)
        sp.dma_start(cst[:, :], g["consts"]).then_inc(s_c, 16)
        for i in range(2):
            sp.dma_start(wraw[i][:, :], g["W_qkv"][i * F:(i + 1) * F, :]).then_inc(s_w, 16)
            sp.dma_start(wp[i][0:F, :], g["W_proj"][i * F:(i + 1) * F, :]).then_inc(s_w, 16)
        sp.dma_start(wp[1][F:F + 1, :], g["b_proj"].unsqueeze(0)).then_inc(s_w, 16)
        sp.dma_start(rfn[:, :], g["rf"]).then_inc(s_w, 16)
        sp.dma_start(sl[:, :], g["slots1"].rearrange("e s d -> (e s) d")).then_inc(s_w, 16)
        for dst, src in ((g["gam"], "gamma"), (g["bet"], "beta"), (g["gin"], "gamma_in")):
            sp.dma_start(dst[:, :], g[src].partition_broadcast(P)).then_inc(s_w, 16)
        for e in range(NE):
            sp.dma_start(g["g2r"][e * NS:(e + 1) * NS, :],
                         g["gamma2"][e].partition_broadcast(NS)).then_inc(s_w, 16)
        sp.wait_ge(s_cum, 1)
        sp.dma_start(g["rank_d"], cum[:, 0, :]).then_inc(s_rank_d, 16)
        sp.wait_ge(s_rank_d, 16)

        def head(i):
            if exists(3 * i - 2):
                sp.wait_ge(s_pos, 1)
                sp.wait_ge(s_pos, 3 * i - 1)
            sp.dma_start(cb[:, :, :], g["rank_d"][bass.ts(i, CB), :].partition_broadcast(P)).then_inc(s_cb, 16)

        def tail(i):
            sp.wait_ge(s_mr, 1)
            sp.wait_ge(s_mr, i + 1)
            sp.dma_start(g["enc_d"].rearrange("(n c) p t f -> n p c t f", c=CB)[i],
                         he[:, :, :].rearrange("p (c t) f -> p c t f", t=NT)).then_inc(s_std, 16)
            sp.wait_ge(s_etT, 1)
            sp.wait_ge(s_etT, i + 1)
            sp.dma_start(g["encT_d"].rearrange("(n c) p s -> n p c s", c=CB)[i],
                         etT[:, :, :, :].rearrange("p c r s -> p c (r s)")).then_inc(s_stdT, 16)

        chunks(sp, head, tail)
        sp.wait_ge(s_std, 16 * (NB // CB))
        sp.wait_ge(s_stdT, 16 * (NB // CB))

    @block.vector
    def _(dve):
        v = nc.vector
        links = [0]

        def link(ins):
            links[0] += 1
            ins.then_inc(chain, 1)
            dve.wait_ge(chain, links[0])

        v.memset(half[:, :], -0.5).then_inc(s_half, 1)
        v.memset(one[:, :], 1.0)
        v.memset(ones[:, :], 1.0).then_inc(s_ones, 1)
        dve.wait_ge(s_x, 48)
        link(v.tensor_copy(xf[:, :], xi[:, :]))
        link(v.tensor_scalar(tmp[:, :], xf[:, :], 0.0, None, ALU.not_equal))
        link(v.scalar_tensor_tensor(keep[:, :], xf[:, :], 1.0, tmp[:, :], ALU.not_equal, ALU.mult))
        link(v.scalar_tensor_tensor(tmp[:, :], xf[:, :], 2.0, keep[:, :], ALU.not_equal, ALU.mult))
        link(v.tensor_tensor(xf[:, :], tmp[:, :], row[:, 0, :], ALU.mult))
        link(v.reduce_max(small[:, 1:2], xf[:, :], AX.X))
        link(v.tensor_scalar(small[:, 2:3], small[:, 1:2], -1.0, 1e-6, ALU.add, ALU.add))
        link(v.reciprocal(small[:, 3:4], small[:, 2:3]))
        link(v.tensor_tensor(small[:, 1:2], small[:, 3:4], small[:, 0:1], ALU.mult))
        link(v.tensor_tensor(keep[:, :], tmp[:, :], row[:, 1, :], ALU.mult))
        link(v.tensor_tensor(xf[:, :], tmp[:, :], keep[:, :], ALU.subtract))
        v.tensor_tensor_scan(cum[:, 0, :], one[:, :], tmp[:, :], 0.0, ALU.mult, ALU.add).then_inc(s_cum, 1)
        v.tensor_tensor_scan(cum[:, 1, :], one[:, :], keep[:, :], 0.0, ALU.mult, ALU.add)
        link(v.tensor_tensor_scan(cum[:, 2, :], one[:, :], xf[:, :], 0.0, ALU.mult, ALU.add))
        for r in range(2):
            v.tensor_copy(perm[:, 0, :].rearrange("b (j r) -> b r j", r=2)[:, r, :],
                          cum[:, 1 + r, :].rearrange("b (j r) -> b r j", r=2)[:, r, :])
        v.tensor_copy(perm[:, 1, :], tmp[:, :])
        link(v.tensor_scalar(perm[:, 2, :], one[:, :], small[:, 1:2], None, ALU.mult))
        dve.wait_ge(s_pe, 1)
        v.tensor_copy(tabs[:, :, :].rearrange("p a (b t) -> p a t b", t=NT)[:, :, 0, :],
                      bank[0][:, 0:3 * NT * NB].rearrange("p (a t b) -> p a t b", a=3, t=NT)[:, :, 0, :])
        link(v.tensor_copy(tabs[:, :, :].rearrange("p a (b t) -> p a t b", t=NT)[:, :, 1, :],
                           bank[0][:, 0:3 * NT * NB].rearrange("p (a t b) -> p a t b", a=3, t=NT)[:, :, 1, :]))
        v.memset(r1[:, :], 0.0)
        dve.wait_ge(s_w, 16 * 18)
        dve.wait_ge(s_c, 16)
        for i in range(2):
            v.tensor_copy(wv[i][0:F, :], wraw[i][:, 2 * D:3 * D])
            for r in range(2):
                v.tensor_copy(wqk[i][0:F, :, r, :], wraw[i][:, 0:2 * D].rearrange("p (c n) -> p c n", c=2 * NC_))
        dve.wait_ge(s_pe, 2)
        for i in range(2):
            v.tensor_copy(wv[i][F:F + 1, :], bank[2][F:F + 1, 0:D])
            for r in range(2):
                v.tensor_copy(wqk[i][F:F + 1, :, r, :],
                              bank[1][F:F + 1, 0:2 * D].rearrange("p (c n) -> p c n", c=2 * NC_))
        v.tensor_copy(rfr[:, :, :], rfn[:, :].unsqueeze(1).to_broadcast([M, HC, DH])).then_inc(s_rfr, 1)
        dve.wait_ge(s_pe, 3)
        v.tensor_tensor(rfa[0:64, :, :], bank[3][0:64, 0:M].unsqueeze(1).to_broadcast([64, HC, M]),
                        cst[0:64, C_MRF:C_MRF + HC * M].rearrange("p (h m) -> p h m", h=HC), ALU.mult)
        v.tensor_copy(rfa[64:128, :, :], cst[64:128, C_MRF:C_MRF + HC * M].rearrange("p (h m) -> p h m", h=HC))
        link(v.tensor_tensor(sq1[:, :], sl[:, :], sl[:, :], ALU.mult))
        link(v.reduce_sum(r1[:, 0:1], sq1[:, :], AX.X))
        v.tensor_scalar(r1[:, 1:2], r1[:, 0:1], 1.0 / D, 1e-6 / D, ALU.mult, ALU.add).then_inc(s_ssq, 1)
        dve.wait_ge(s_pw, 1)
        v.tensor_scalar(phn[:, :], sl[:, :], r1[:, 2:3], None, ALU.mult).then_inc(s_phn, 1)
        dve.wait_ge(s_pe, 4)
        v.tensor_copy(phiT[:, :, :], bank[4][0:F, 0:2 * P].rearrange("p (c n) -> p c n", c=2))

        def step(i, tail):
            if exists(3 * i - 2):
                dve.wait_ge(s_pos, 3 * i - 1)
            if exists(3 * i - 1):
                dve.wait_ge(s_pos, 3 * i)
            v.tensor_scalar(kk[:, :, :], tabs[:, :, bass.ts(i, CT)], 1.0, None, ALU.mult).then_inc(s_pos, 1)
            dve.wait_ge(s_pos, 3 * i + 1)
            dve.wait_ge(s_cb, 16 * i + 16)
            for t in range(CT):
                ins = v.tensor_scalar(junk[:, t, :], cb[:, t // NT, :], kk[:, 0, t:t + 1], 0.0, ALU.is_lt, ALU.add,
                                      accum_out=cnt[:, t:t + 1])
            ins.then_inc(s_pos, 1)
            dve.wait_ge(s_pos, 3 * i + 2)
            if exists(i - 1):
                dve.wait_ge(s_ang, i)
            v.tensor_tensor(psc[:, :], cnt[:, :], kk[:, 2, :], ALU.mult).then_inc(s_pos, 1)
            if tail:
                stats(i - 1)
            if exists(i - 1):
                dve.wait_ge(s_he, i)
            v.tensor_scalar(kp[:, :], kk[:, 1, :], 1.0, None, ALU.mult).then_inc(s_red, 1)
            dve.wait_ge(s_ang, i + 1)
            v.tensor_scalar(nr[:, :, :], ang[:, :, :], float(1.0 / TWO_PI), ROUND, ALU.mult, ALU.add).then_inc(s_red, 1)
            dve.wait_ge(s_red, 5 * i + 2)
            v.tensor_scalar(nr2[:, :, :], nr[:, :, :], -ROUND, None, ALU.add).then_inc(s_red, 1)
            dve.wait_ge(s_red, 5 * i + 3)
            v.scalar_tensor_tensor(rd[:, :, :], nr2[:, :, :], -PI_HI, ang[:, :, :], ALU.mult, ALU.add).then_inc(s_red, 1)
            dve.wait_ge(s_red, 5 * i + 4)
            v.scalar_tensor_tensor(rd2[:, :, :], nr2[:, :, :], -PI_LO, rd[:, :, :], ALU.mult, ALU.add).then_inc(s_red, 1)
            dve.wait_ge(s_red, 5 * i + 5)
            if exists(i - 1):
                dve.wait_ge(s_sin, i)
            v.tensor_scalar(rd3[:, :, :], rd2[:, :, :], PI_MAX, -PI_MAX, ALU.min, ALU.max).then_inc(s_sin_in, 1)

        def stats(i):
            dve.wait_ge(s_he, i + 1)
            v.reduce_sum(st[:, 0, :], he[:, :, 0:F], AX.X).then_inc(s_var, 1)
            dve.wait_ge(s_var, 4 * i + 1)
            if exists(i - 1):
                dve.wait_ge(s_mr, i)
            v.tensor_scalar(st[:, 2, :], st[:, 0, :], -1.0 / D, None, ALU.mult).then_inc(s_var, 1)
            dve.wait_ge(s_var, 4 * i + 2)
            v.tensor_tensor(st[:, 3, :], st[:, 2, :], st[:, 2, :], ALU.mult).then_inc(s_var, 1)
            dve.wait_ge(s_var, 4 * i + 3)
            dve.wait_ge(s_hsq, i + 1)
            v.scalar_tensor_tensor(st[:, 4, :], st[:, 1, :], 1.0 / D, st[:, 3, :], ALU.mult,
                                   ALU.subtract).then_inc(s_var, 1)
            dve.wait_ge(s_var, 4 * i + 4)
            if exists(i - 1):
                dve.wait_ge(s_rs, i)
            v.tensor_scalar(st[:, 5, :], st[:, 4, :], 1e-5, None, ALU.add).then_inc(s_ve, 1)

        step(0, False)
        step(1, True)
        with dve.Fori(2, NB // CB, 1) as i:
            step(i, True)
        stats(NB // CB - 1)

    @block.scalar
    def _(act):
        def squares(i):
            act.wait_ge(s_he, i + 1)
            if exists(i - 1):
                act.wait_ge(s_ve, i)
            for t in range(CT):
                ins = nc.scalar.activation(hsq[:, t, :], he[:, t, 0:F], ACT.Square, accum_out=st[:, 1, t:t + 1])
            ins.then_inc(s_hsq, 1)

        def angles(i):
            act.wait_ge(s_pos, 3 * i + 3)
            if exists(5 * i - 2):
                act.wait_ge(s_red, 5 * i - 1)
            for t in range(CT):
                ins = nc.scalar.activation(ang[:, t, :], cst[:, C_INV:C_INV + F], ACT.Identity,
                                           bias=cst[:, C_QUART:C_QUART + 1], scale=psc[:, t:t + 1])
            ins.then_inc(s_ang, 1)

        def sines(i):
            act.wait_ge(s_sin_in, i + 1)
            if exists(i - 1):
                act.wait_ge(s_he, i)
            nc.scalar.activation(sn[:, :, :], rd3[:, :, :], ACT.Sin).then_inc(s_sin, 1)

        def turned(i):
            act.wait_ge(s_etT_mm, i + 1)
            if exists(i - 1):
                act.wait_ge(s_stdT, i * 16)
            for h in range(2):
                ins = nc.scalar.activation(etT[:, 2 * h:2 * h + 2, :, :],
                                           bank[5 + h][0:F + 1, :].rearrange("p (c j r) -> p c r j", c=2, r=2), ACT.Copy)
            ins.then_inc(s_etT, 1)

        def step(i):
            squares(i - 1)
            angles(i)
            sines(i)
            turned(i - 1)

        act.wait_ge(s_c, 16)
        angles(0)
        sines(0)
        step(1)
        with act.Fori(2, NB // CB, 1) as i:
            step(i)
        squares(NB // CB - 1)
        turned(NB // CB - 1)

    @block.gpsimd
    def _(pool):
        p = nc.gpsimd
        pool.wait_ge(s_half, 1)
        pool.wait_ge(s_ssq, 1)
        p.tensor_tensor(r1[:, 2:3], r1[:, 1:2], half[:, 0:1], ALU.pow).then_inc(s_pw, 1)

        def kept(i):
            pool.wait_ge(s_red, 5 * i + 1)
            pool.wait_ge(s_sin, i + 1)
            if exists(i - 1):
                pool.wait_ge(s_std, i * 16)
            if exists(i - 1):
                pool.wait_ge(s_et, i)
            p.tensor_tensor(he[:, :, 0:F], sn[:, :, :], kp[:, :].unsqueeze(2).to_broadcast([P, CT, F]),
                            ALU.mult).then_inc(s_he, 1)

        def scaled(i):
            pool.wait_ge(s_ve, i + 1)
            p.tensor_tensor(he[:, :, F], st[:, 5, :], half[:, 0:CT], ALU.pow).then_inc(s_rs, 1)
            pool.wait_ge(s_rs, i + 1)
            p.tensor_tensor(he[:, :, F + 1], st[:, 2, :], he[:, :, F], ALU.mult).then_inc(s_mr, 1)
            pool.wait_ge(s_mr, i + 1)
            if exists(i - 1):
                pool.wait_ge(s_etT_mm, i)
            p.tensor_tensor(et[:, :, 0:F], he[:, :, 0:F], he[:, :, F:F + 1].to_broadcast([P, CT, F]), ALU.mult)
            p.tensor_tensor(et[:, :, F], st[:, 2, :], he[:, :, F], ALU.mult).then_inc(s_et, 1)

        def step(i):
            scaled(i - 1)
            kept(i)

        kept(0)
        step(1)
        with pool.Fori(2, NB // CB, 1) as i:
            step(i)
        scaled(NB // CB - 1)

    @block.tensor
    def _(pe):
        pe.wait_ge(s_c, 16)
        pe.wait_ge(chain, 13)
        for a in range(3):
            for t in range(NT):
                ins = nc.tensor.transpose(bank[0][:, (a * NT + t) * NB:(a * NT + t + 1) * NB],
                                          perm[:, a, t * P:(t + 1) * P], ident[0:NB, 0:NB])
        ins.then_inc(s_pe, 1)
        pe.wait_ge(s_ones, 1)
        pe.wait_ge(s_w, 16 * 18)
        for i in range(2):
            nc.tensor.matmul(bank[1][0:F + 1, 0:2 * D], ones[:, :], wraw[i][:, 0:2 * D], start=i == 0, stop=i == 1)
        for i in range(2):
            ins = nc.tensor.matmul(bank[2][0:F + 1, 0:D], ones[:, :], wraw[i][:, 2 * D:3 * D], start=i == 0, stop=i == 1)
        ins.then_inc(s_pe, 1)
        pe.wait_ge(s_rfr, 1)
        nc.tensor.transpose(bank[3][0:64, 0:M], rfr[:, :, :].rearrange("p h d -> p (h d)"),
                            ident[0:M, 0:M]).then_inc(s_pe, 1)
        pe.wait_ge(s_phn, 1)
        for c in range(2):
            ins = nc.tensor.transpose(bank[4][0:F, c * P:(c + 1) * P], phn[:, c * F:(c + 1) * F], ident)
        ins.then_inc(s_pe, 1)

        def chunk(i):
            pe.wait_ge(s_et, i + 1)
            if exists(i - 1):
                pe.wait_ge(s_etT, i)
            for t in range(CT):
                ins = nc.tensor.transpose(bank[5 + t // 4][0:F + 1, (t % 4) * P:(t % 4 + 1) * P], et[:, t, :], ident)
            ins.then_inc(s_etT_mm, 1)

        chunk(0)
        with pe.Fori(1, NB // CB, 1) as i:
            chunk(i)


def attend(nc, ctx, sem, sb, bank, g):
    cst, ident, half = g["cst"], g["ident"], g["half"]
    wv, wqk, rfa, wp, phiT = g["wv"], g["wqk"], g["rfa"], g["wp"], g["phiT"]
    gam, bet, gin, g2r = g["gam"], g["bet"], g["gin"], g["g2r"]
    two = range(2)
    encT = [sb(f"encT{i}", [F + 1, S]) for i in two]
    enc = [sb(f"enc{i}", [P, NT, HX]) for i in two]
    qk = [sb(f"qk{c}", [P, 2 * S]) for c in range(NC_)]
    kp = [sb(f"kp{c}", [P, 2, HC * M]) for c in range(NC_)]
    qp = [sb(f"qp{c}", [P, 2, S]) for c in range(NC_)]
    va = [sb(f"va{i}", [P, 2, H, DH + 1]) for i in two]
    kvb = sb("kvb", [P, H // 2, 2, DH + 1])
    den = sb("den", [P, NT * H])
    rden = sb("rden", [P, NT * H])
    xa = sb("xa", [P, NT, D])
    xaT = [sb("xaT0", [F, S]), sb("xaT1", [F + 1, S])]
    hh = [sb(f"hh{i}", [P, NT, D]) for i in two]
    hb = [sb(f"hb{i}", [P, NT, D]) for i in two]
    xs = sb("xs", [P, NT, D])
    xh = [sb(f"xh{i}", [P, NT, D]) for i in two]
    y = sb("y", [P, NT, D])
    bs = sb("bs", [P, NT, 6])
    mv = sb("mv", [P, NT, 2])
    ve = sb("ve", [P, NT])
    rs = sb("rs", [P, NT])
    yg = sb("yg", [P, NT, D])
    h2 = [sb(f"h2{i}", [P, NT, D + 1]) for i in two]
    bs2 = sb("bs2", [P, NT, 6])
    mv2 = sb("mv2", [P, NT, 2])
    ve2 = sb("ve2", [P, NT])
    f2 = sb("f2", [P, NT])
    xc = sb("xc", [P, NT, D])
    xn = [sb(f"xn{i}", [P, NT, D]) for i in two]
    xnT = sb("xnT", [F, 2, S])
    mx = sb("mx", [P, NT + GQ])
    nm = sb("nm", [P, NT + GQ])
    ec = sb("ec", [P, NT, P])
    ed = sb("ed", [P, GQ, 64])
    zd = sb("zd", [P, GQ])
    cT = [sb(f"cT{i}", [P, S]) for i in two]
    dT = sb("dT", [P, NT, P])
    sqj = sb("sqj", [P, GQ, D])
    ssq = sb("ssq", [P, GQ])
    zs = sb("zs", [P, GQ])
    sse = sb("sse", [P, GQ])
    sr = sb("sr", [P, GQ])
    yn = [sb(f"yn{i}", [P, GQ, D]) for i in two]

    s_ld = [sem(f"loaded{i}") for i in two]
    s_init = sem("at_init")
    qk_mm, qk_copy, qk_sq = sem("qk_mm"), sem("qk_copy"), sem("qk_sq")
    f_mm, f_exp = sem("feat_mm"), sem("feat_exp")
    v_mm, v_ev, kv_mm, kv_ev = sem("v_mm"), sem("v_ev"), sem("kv_mm"), sem("kv_ev")
    o_mm, o_den, o_rcp, o_ev = sem("o_mm"), sem("o_den"), sem("o_rcp"), sem("o_ev")
    xaT_mm, xaT_ev, pj_mm = sem("xaT_mm"), sem("xaT_ev"), sem("pj_mm")
    prep, prep1, prep2 = sem("prep"), sem("prep1"), sem("prep2")
    y_ev, y_bs, y_mv, y_ve, y_rs, y_g, y_h2 = (sem(n) for n in ("y_ev", "y_bs", "y_mv", "y_ve", "y_rs", "y_g", "y_h2"))
    h_bs, h_mv, h_ve, h_f, h_xc, h_xn = (sem(n) for n in ("h_bs", "h_mv", "h_ve", "h_f", "h_xc", "h_xn"))
    xnT_mm, xnT_ev, lg_mm, lg_mx, lg_nm = (sem(n) for n in ("xnT_mm", "xnT_ev", "lg_mm", "lg_mx", "lg_nm"))
    e_c, e_d, cd_mm, c_ev, d_ev = (sem(n) for n in ("e_c", "e_d", "cd_mm", "c_ev", "d_ev"))
    sl_mm, sl_sq, sl_z, sl_e, sl_r, sl_y = (sem(n) for n in ("sl_mm", "sl_sq", "sl_z", "sl_e", "sl_r", "sl_y"))
    s_h2 = [sem(f"h2_stored{i}") for i in two]
    s_yn = [sem(f"yn_stored{i}") for i in two]
    block = ctx.enter_context(nc.Block())
    b_qk, b_ft = bank[0:2], bank[2:4]
    b_v, b_o, b_x, b_s = bank[4], bank[5], bank[6], bank[7]

    def pipeline(eng, iteration, last):
        def go(a, u):
            n = 2 * a + u
            if isinstance(n, int):
                iteration(a, u, n, [0 <= n - k < NB for k in range(last + 1)])
            else:
                iteration(a, u, n, [True] * (last + 1))
        for n in range(6):
            go(n // 2, n % 2)
        with eng.Fori(3, NB // 2, 1) as a:
            for u in two:
                go(a, u)
        for n in range(NB, NB + last):
            go(n // 2, n % 2)

    @block.sync
    def _(sp):
        def iteration(a, u, n, step):
            if step[0]:
                if exists(n - 2):
                    sp.wait_ge(v_mm, 1)
                    sp.wait_ge(v_mm, n - 1)
                if exists(n - 2):
                    sp.wait_ge(prep2, 1)
                    sp.wait_ge(prep2, n - 1)
                sp.dma_start(encT[u][:, :], g["encT_d"][n]).then_inc(s_ld[u], 16)
                sp.dma_start(enc[u][:, :, :], g["enc_d"][n]).then_inc(s_ld[u], 16)
            if step[3]:
                l, v = n - 3, 1 - u
                sp.wait_ge(e_c, 1)
                sp.wait_ge(e_c, l + 1)
                sp.dma_start(g["h2_d"][l], h2[v][:, :, :]).then_inc(s_h2[v], 16)
                sp.wait_ge(c_ev, 1)
                sp.wait_ge(c_ev, l + 1)
                sp.dma_start(g["combT_d"][l], cT[v][:, :]).then_inc(s_h2[v], 16)
                sp.wait_ge(sl_y, 1)
                sp.wait_ge(sl_y, l + 1)
                sp.dma_start(g["yn_d"][l].rearrange("e s q d -> (e s) q d"), yn[v][:, :, :]).then_inc(s_yn[v], 16)

        pipeline(sp, iteration, 3)
        for u in two:
            sp.wait_ge(s_h2[u], 32 * NB // 2)
            sp.wait_ge(s_yn[u], 16 * NB // 2)

    @block.tensor
    def _(pe):
        mm, tr = nc.tensor.matmul, nc.tensor.transpose
        pe.wait_ge(s_init, 2)

        def iteration(a, u, n, step):
            m, l = n - 1, n - 2
            eT = encT[u][:, :].rearrange("p (r s) -> p r s", r=2)

            def QK(c):
                if c == 0:
                    pe.wait_ge(s_ld[u], (a + 1) * 32)
                if exists(NC_ * n + c - 2):
                    pe.wait_ge(qk_copy, NC_ * n + c - 1)
                if exists(NC_ * n + c - 2):
                    pe.wait_ge(qk_sq, NC_ * n + c - 1)
                b = b_qk[(u + c) % 2]
                for r in two:
                    mm(b[:, 0:S].rearrange("p (j r) -> p r j", r=2)[:, r, :],
                       wqk[r][:, c, :, :].rearrange("p a n -> p (a n)"), eT[:, r, :], start=True, stop=True)
                for r in two:
                    ins = mm(b[:, S + r * P:S + (r + 1) * P],
                             wqk[r][:, NC_ + c, :, :].rearrange("p a n -> p (a n)"), eT[:, r, :], start=True, stop=True)
                ins.then_inc(qk_mm, 1)

            def V():
                if exists(l - 1):
                    pe.wait_ge(sl_y, l)
                for r in two:
                    ins = mm(b_v[:, r * D:(r + 1) * D], eT[:, r, :], wv[r][:, :], start=True, stop=True)
                ins.then_inc(v_mm, 1)

            def FEAT(s):
                if exists(2 * NC_ * n + s - 2):
                    pe.wait_ge(f_exp, 2 * NC_ * n + s - 1)
                c, b = s % NC_, b_ft[s % 2]
                if s < NC_:
                    pe.wait_ge(qk_copy, NC_ * n + c + 1)
                    pe.wait_ge(qk_sq, NC_ * n + c + 1)
                for r in two:
                    if s < NC_:
                        ins = mm(b[:, r * 256:(r + 1) * 256], qk[c][:, S + r * P:S + (r + 1) * P],
                                 rfa[:, :, :].rearrange("p h m -> p (h m)"), start=True, stop=True)
                    else:
                        ins = mm(b[:, r * 256:(r + 1) * 256],
                                 rfa[:, 2 * r:2 * r + 2, :].rearrange("p h m -> p (h m)"), qk[c][:, 0:S],
                                 start=True, stop=True)
                ins.then_inc(f_mm, 1)

            def KV():
                pe.wait_ge(f_exp, 2 * NC_ * n + NC_)
                pe.wait_ge(v_ev, n + 1)
                for p in range(H // 2):
                    for r in two:
                        ins = mm(b_v[:, 34 * p:34 * p + 34], kp[p // 2][:, r, (p % 2) * P:(p % 2 + 1) * P],
                                 va[u][:, r, 2 * p:2 * p + 2, :].rearrange("p h d -> p (h d)"),
                                 start=r == 0, stop=r == 1)
                ins.then_inc(kv_mm, 1)

            def OUT():
                pe.wait_ge(kv_ev, m + 1)
                pe.wait_ge(f_exp, 2 * NC_ * m + 2 * NC_)
                if exists(m - 1):
                    pe.wait_ge(y_ev, m)
                for t in two:
                    for p in range(H // 2):
                        ins = mm(b_o[:, t * 204 + 34 * p:t * 204 + 34 * p + 34], qp[p // 2][:, p % 2, t * P:(t + 1) * P],
                                 kvb[:, p, :, :].rearrange("p h d -> p (h d)"), start=True, stop=True)
                ins.then_inc(o_mm, 1)

            def XAT():
                pe.wait_ge(o_ev, m + 1)
                for c in two:
                    for t in two:
                        ins = tr(b_o[0:F, (2 * c + t) * P:(2 * c + t + 1) * P], xa[:, t, c * F:(c + 1) * F], ident)
                ins.then_inc(xaT_mm, 1)

            def PROJ():
                pe.wait_ge(xaT_ev, m + 1)
                for t in two:
                    for c in two:
                        ins = mm(b_o[:, t * D:(t + 1) * D], xaT[c][:, t * P:(t + 1) * P], wp[c][:, :],
                                 start=c == 0, stop=c == 1)
                ins.then_inc(pj_mm, 1)

            def XNT():
                pe.wait_ge(h_xn, l + 1)
                if exists(l - 1):
                    pe.wait_ge(c_ev, l)
                if exists(l - 1):
                    pe.wait_ge(d_ev, l)
                for c in two:
                    for t in two:
                        ins = tr(b_x[0:F, (2 * c + t) * P:(2 * c + t + 1) * P], xn[u][:, t, c * F:(c + 1) * F], ident)
                ins.then_inc(xnT_mm, 1)

            def LOG():
                pe.wait_ge(xnT_ev, l + 1)
                for t in two:
                    for c in two:
                        mm(b_x[:, t * P:(t + 1) * P], xnT[:, c, t * P:(t + 1) * P], phiT[:, c, :], start=c == 0, stop=c == 1)
                for c in two:
                    ins = mm(b_x[:, S:2 * S], phiT[:, c, :], xnT[:, c, :], start=c == 0, stop=c == 1)
                ins.then_inc(lg_mm, 1)

            def CDT():
                pe.wait_ge(e_c, l + 1)
                pe.wait_ge(e_d, l + 1)
                for t in two:
                    tr(b_x[:, t * P:(t + 1) * P], ec[:, t, :], ident)
                for t in two:
                    ins = tr(b_x[:, S + t * P:S + (t + 1) * P], ed[:, 2 * t:2 * t + 2, :].rearrange("p q s -> p (q s)"), ident)
                ins.then_inc(cd_mm, 1)

            def SLOTS():
                pe.wait_ge(d_ev, l + 1)
                if exists(l - 1):
                    pe.wait_ge(sl_y, l)
                for t in two:
                    for q, b in ((0, b_s), (1, b_v)):
                        ins = mm(b[:, t * D:(t + 1) * D], dT[64 * q:64 * q + 64, t, :], xn[u][64 * q:64 * q + 64, t, :],
                                 start=True, stop=True)
                ins.then_inc(sl_mm, 1)

            A, B, C = step
            if A:
                QK(0)
            if B:
                OUT()
            if A:
                QK(1)
            if C:
                XNT()
            if A:
                QK(2)
            if C:
                LOG()
            if A:
                V()
                FEAT(0)
                FEAT(1)
            if B:
                XAT()
            if A:
                FEAT(2)
                FEAT(3)
            if B:
                PROJ()
            if A:
                KV()
                FEAT(4)
            if C:
                CDT()
            if A:
                FEAT(5)
            if C:
                if A:
                    pe.wait_ge(kv_ev, n + 1)
                SLOTS()

        pipeline(pe, iteration, 2)

    @block.vector
    def _(dve):
        v = nc.vector
        for i in two:
            v.memset(va[i][:, :, :, :], 1.0)
        v.memset(kvb[:, :, :, :], 0.0).then_inc(s_init, 1)
        v.memset(xaT[1][F:F + 1, :], 1.0).then_inc(s_init, 1)

        def iteration(a, u, n, step):
            m, l, w = n - 1, n - 2, 1 - u

            def qk_copy_(c):
                dve.wait_ge(qk_mm, NC_ * n + c + 1)
                if exists(2 * NC_ * (n - 1) + NC_ + c):
                    dve.wait_ge(f_mm, 2 * NC_ * (n - 1) + NC_ + c + 1)
                v.tensor_copy(qk[c][0:64, :], b_qk[(u + c) % 2][0:64, :]).then_inc(qk_copy, 1)

            def out_():
                dve.wait_ge(o_mm, m + 1)
                o = b_o[:, 0:NT * 204].rearrange("p (h d) -> p h d", d=DH + 1)
                v.tensor_scalar(den[:, :], o[:, :, DH], 1e-6, None, ALU.add).then_inc(o_den, 1)
                dve.wait_ge(o_den, m + 1)
                v.reciprocal(rden[:, :], den[:, :]).then_inc(o_rcp, 1)
                dve.wait_ge(o_rcp, m + 1)
                if exists(m - 1):
                    dve.wait_ge(xaT_mm, m)
                v.tensor_tensor(xa[:, :, :].rearrange("p t (h d) -> p (t h) d", d=DH), o[:, :, 0:DH],
                                rden[:, :].unsqueeze(2).to_broadcast([P, NT * H, DH]), ALU.mult).then_inc(o_ev, 1)

            def v_():
                dve.wait_ge(v_mm, n + 1)
                if exists(n - 2):
                    dve.wait_ge(kv_mm, n - 1)
                v.tensor_copy(va[u][:, :, :, 0:DH].rearrange("p r h d -> p (r h) d"),
                              b_v[:, 0:2 * D].rearrange("p (h d) -> p h d", d=DH)).then_inc(v_ev, 1)

            def kv_():
                dve.wait_ge(kv_mm, n + 1)
                if exists(m):
                    dve.wait_ge(o_mm, m + 1)
                for r in two:
                    ins = v.tensor_scalar(kvb[64 * r:64 * r + 64, :, r, :],
                                          b_v[64 * r:64 * r + 64, 0:204].rearrange("p (h r d) -> p h r d", r=2, d=DH + 1)[:, :, r, :],
                                          1.0 / M, None, ALU.mult)
                ins.then_inc(kv_ev, 1)

            def y_():
                dve.wait_ge(pj_mm, m + 1)
                dve.wait_ge(prep2, m + 1)
                v.tensor_tensor(y[:, :, :], b_o[:, 0:NT * D].rearrange("p (t d) -> p t d", t=NT), xh[w][:, :, :],
                                ALU.add).then_inc(y_ev, 1)
                dve.wait_ge(y_ev, m + 1)
                for t in two:
                    ins = v.bn_stats(bs[:, t, :], y[:, t, :])
                ins.then_inc(y_bs, 1)
                dve.wait_ge(y_bs, 1)
                dve.wait_ge(y_bs, m + 1)
                for t in two:
                    ins = v.bn_aggr(mv[:, t, :], bs[:, t, :])
                ins.then_inc(y_mv, 1)
                dve.wait_ge(y_mv, m + 1)
                if exists(m - 1):
                    dve.wait_ge(y_rs, m)
                v.tensor_scalar(ve[:, :], mv[:, :, 1], 1e-5, None, ALU.add).then_inc(y_ve, 1)

            def h2_():
                dve.wait_ge(y_mv, m + 1)
                for t in two:
                    ins = v.scalar_tensor_tensor(yg[:, t, :], y[:, t, :], mv[:, t, 0:1], gam[:, :], ALU.subtract, ALU.mult)
                ins.then_inc(y_g, 1)
                dve.wait_ge(y_g, m + 1)
                dve.wait_ge(y_rs, m + 1)
                if exists((a if u else a - 1) - 1):
                    dve.wait_ge(s_h2[w], ((a if u else a - 1)) * 32)
                for t in two:
                    ins = v.scalar_tensor_tensor(h2[w][:, t, 0:D], yg[:, t, :], rs[:, t:t + 1], hb[w][:, t, :],
                                                 ALU.mult, ALU.add)
                ins.then_inc(y_h2, 1)

            def f2_():
                dve.wait_ge(y_h2, m + 1)
                for t in two:
                    ins = v.bn_stats(bs2[:, t, :], h2[w][:, t, 0:D])
                ins.then_inc(h_bs, 1)
                dve.wait_ge(h_bs, 1)
                dve.wait_ge(h_bs, m + 1)
                for t in two:
                    ins = v.bn_aggr(mv2[:, t, :], bs2[:, t, :])
                ins.then_inc(h_mv, 1)
                dve.wait_ge(h_mv, m + 1)
                if exists(m - 1):
                    dve.wait_ge(h_f, m)
                v.tensor_scalar(ve2[:, :], mv2[:, :, 1], 1.0 + 1e-6 / D, 1e-11 / D, ALU.mult, ALU.add).then_inc(h_ve, 1)

            def xn_():
                dve.wait_ge(h_mv, m + 1)
                dve.wait_ge(h_f, m + 1)
                if exists(m - 1):
                    dve.wait_ge(h_xn, m)
                for t in two:
                    ins = v.tensor_scalar(xc[:, t, :], h2[w][:, t, 0:D], mv2[:, t, 0:1], f2[:, t:t + 1],
                                          ALU.subtract, ALU.mult)
                ins.then_inc(h_xc, 1)

            def xnT_():
                dve.wait_ge(xnT_mm, l + 1)
                if exists(l - 1):
                    dve.wait_ge(lg_mm, l)
                v.tensor_copy(xnT[:, :, :].rearrange("p c s -> p (c s)"), b_x[0:F, :]).then_inc(xnT_ev, 1)

            def lg_():
                dve.wait_ge(lg_mm, l + 1)
                v.reduce_max(mx[:, 0:NT], b_x[:, 0:S].rearrange("p (t n) -> p t n", t=NT), AX.X)
                v.reduce_max(mx[:, NT:NT + GQ], b_x[:, S:2 * S].rearrange("p (t n) -> p t n", t=GQ), AX.X).then_inc(lg_mx, 1)
                dve.wait_ge(lg_mx, l + 1)
                if exists(l - 1):
                    dve.wait_ge(e_c, l)
                if exists(l - 1):
                    dve.wait_ge(e_d, l)
                v.tensor_scalar(nm[:, :], mx[:, :], -1.0, None, ALU.mult).then_inc(lg_nm, 1)

            def cd_():
                dve.wait_ge(cd_mm, l + 1)
                if exists(l - 1):
                    dve.wait_ge(sl_mm, l)
                v.tensor_copy(dT[:, :, :].rearrange("p t n -> p (t n)"), b_x[:, S:2 * S]).then_inc(d_ev, 1)
                if exists(a - 2):
                    dve.wait_ge(s_h2[u], (a - 1) * 32)
                v.tensor_copy(cT[u][:, :], b_x[:, 0:S]).then_inc(c_ev, 1)

            def yn0_(k):
                dve.wait_ge(e_d, k + 1)
                v.scalar_tensor_tensor(zs[:, :], zd[:, :], 1e-6 / D, zd[:, :], ALU.mult, ALU.mult).then_inc(sl_z, 1)
                dve.wait_ge(sl_z, k + 1)
                dve.wait_ge(sl_sq, k + 1)
                if exists(k - 1):
                    dve.wait_ge(sl_r, k)
                v.scalar_tensor_tensor(sse[:, :], ssq[:, :], 1.0 / D, zs[:, :], ALU.mult, ALU.add).then_inc(sl_e, 1)

            def yn_(k, j, pair):
                dve.wait_ge(sl_r, k + 1)
                if exists(pair - 1):
                    dve.wait_ge(s_yn[j], pair * 16)
                for t in two:
                    for q, b in ((0, b_s), (1, b_v)):
                        ins = v.scalar_tensor_tensor(yn[j][:, 2 * t + q, :], b[:, t * D:(t + 1) * D],
                                                     sr[:, 2 * t + q:2 * t + q + 1], g2r[:, :], ALU.mult, ALU.mult)
                ins.then_inc(sl_y, 1)

            A, B, C, E = step
            if A:
                qk_copy_(0)
            if E:
                yn0_(n - 3)
            if B:
                out_()
            if A:
                qk_copy_(1)
            if C:
                xnT_()
            if E:
                yn_(n - 3, w, a - 1 if u else a - 2)
            if A:
                qk_copy_(2)
            if C:
                lg_()
            if A:
                v_()
            if B:
                y_()
            if A:
                kv_()
            if B:
                h2_()
            if C:
                cd_()
            if B:
                f2_()
                xn_()

        pipeline(dve, iteration, 3)

    @block.scalar
    def _(act):
        f = nc.scalar.activation

        def iteration(a, u, n, step):
            m, l = n - 1, n - 2

            def sq_(c):
                act.wait_ge(qk_mm, NC_ * n + c + 1)
                if exists(2 * NC_ * (n - 1) + NC_ + c):
                    act.wait_ge(f_mm, 2 * NC_ * (n - 1) + NC_ + c + 1)
                f(qk[c][64:128, :], b_qk[(u + c) % 2][64:128, :], ACT.Square).then_inc(qk_sq, 1)

            def ft_(s):
                act.wait_ge(f_mm, 2 * NC_ * n + s + 1)
                if s < NC_:
                    if exists(n - 1):
                        act.wait_ge(kv_mm, n)
                    f(kp[s][:, :, :].rearrange("p r m -> p (r m)"), b_ft[s % 2][:, :], ACT.Exp).then_inc(f_exp, 1)
                else:
                    if exists(n - 1):
                        act.wait_ge(o_mm, n)
                    f(qp[s - NC_][:, :, :].rearrange("p r m -> p (r m)"), b_ft[s % 2][:, :], ACT.Exp).then_inc(f_exp, 1)

            def xaT_():
                act.wait_ge(xaT_mm, m + 1)
                if exists(m - 1):
                    act.wait_ge(pj_mm, m)
                f(xaT[0][:, :], b_o[0:F, 0:S], ACT.Copy)
                f(xaT[1][0:F, :], b_o[0:F, S:2 * S], ACT.Copy).then_inc(xaT_ev, 1)

            def ec_():
                act.wait_ge(lg_nm, l + 1)
                if exists(l - 1):
                    act.wait_ge(cd_mm, l)
                for t in two:
                    ins = f(ec[:, t, :], b_x[:, t * P:(t + 1) * P], ACT.Exp, bias=nm[:, t:t + 1],
                            accum_out=h2[u][:, t, D:D + 1])
                ins.then_inc(e_c, 1)

            def ed_(h):
                if h == 0:
                    if exists(l - 1):
                        act.wait_ge(sl_e, l)
                for q in range(2 * h, 2 * h + 2):
                    ins = f(ed[:, q, :], b_x[:, S + 64 * q:S + 64 * (q + 1)], ACT.Exp, bias=nm[:, NT + q:NT + q + 1],
                            accum_out=zd[:, q:q + 1])
                if h == 1:
                    ins.then_inc(e_d, 1)

            def ss_():
                act.wait_ge(sl_mm, l + 1)
                if exists(l - 1):
                    act.wait_ge(sl_e, l)
                for t in two:
                    for q, b in ((0, b_s), (1, b_v)):
                        ins = f(sqj[:, 2 * t + q, :], b[:, t * D:(t + 1) * D], ACT.Square, accum_out=ssq[:, 2 * t + q:2 * t + q + 1])
                ins.then_inc(sl_sq, 1)

            A, B, C = step
            if A:
                sq_(0)
                sq_(1)
                sq_(2)
                ft_(0)
                ft_(1)
            if B:
                xaT_()
            if C:
                ec_()
            if A:
                ft_(2)
            if C:
                ed_(0)
            if A:
                ft_(3)
            if C:
                ed_(1)
            if A:
                ft_(4)
                ft_(5)
            if C:
                ss_()

        pipeline(act, iteration, 2)

    @block.gpsimd
    def _(pool):
        p = nc.gpsimd

        def iteration(a, u, n, step):
            m, l, w = n - 1, n - 2, 1 - u

            def prep_():
                pool.wait_ge(s_ld[u], (a + 1) * 32)
                if exists(n - 2):
                    pool.wait_ge(y_h2, n - 1)
                for r, c in ((0, C_EVEN), (1, C_ODD)):
                    ins = p.tensor_tensor(hh[u][:, :, r * F:(r + 1) * F], enc[u][:, :, 0:F],
                                          cst[:, c:c + 1].unsqueeze(1).to_broadcast([P, NT, F]), ALU.mult)
                ins.then_inc(prep, 1)
                pool.wait_ge(prep, n + 1)
                p.tensor_tensor(xs[:, :, :], hh[u][:, :, :], enc[u][:, :, F:F + 1].to_broadcast([P, NT, D]),
                                ALU.mult).then_inc(prep1, 1)
                p.tensor_tensor(hb[u][:, :, :], hh[u][:, :, :], bet[:, :].unsqueeze(1).to_broadcast([P, NT, D]), ALU.add)
                pool.wait_ge(prep1, n + 1)
                p.tensor_tensor(xh[u][:, :, :], xs[:, :, :], enc[u][:, :, F + 1:F + 2].to_broadcast([P, NT, D]),
                                ALU.add).then_inc(prep2, 1)

            def rs_():
                pool.wait_ge(y_ve, m + 1)
                if exists(m - 1):
                    pool.wait_ge(y_h2, m)
                p.tensor_tensor(rs[:, :], ve[:, :], half[:, 0:NT], ALU.pow).then_inc(y_rs, 1)

            def f2_():
                pool.wait_ge(h_ve, m + 1)
                if exists(m - 1):
                    pool.wait_ge(h_xc, m)
                p.tensor_tensor(f2[:, :], ve2[:, :], half[:, 0:NT], ALU.pow).then_inc(h_f, 1)

            def xn_():
                pool.wait_ge(h_xc, m + 1)
                if exists(m - 2):
                    pool.wait_ge(xnT_mm, m - 1)
                if exists(m - 2):
                    pool.wait_ge(sl_mm, m - 1)
                p.tensor_tensor(xn[w][:, :, :], xc[:, :, :], gin[:, :].unsqueeze(1).to_broadcast([P, NT, D]),
                                ALU.mult).then_inc(h_xn, 1)

            def sr_(k):
                pool.wait_ge(sl_e, k + 1)
                if exists(k - 1):
                    pool.wait_ge(sl_y, k)
                p.tensor_tensor(sr[:, :], sse[:, :], half[:, 0:GQ], ALU.pow).then_inc(sl_r, 1)

            A, B, _, E = step
            if E:
                sr_(n - 3)
            if A:
                prep_()
            if B:
                rs_()
                f2_()
                xn_()

        pipeline(pool, iteration, 3)


BACK = [step for e in range(E2 + 1)
        for n in range(NHC)
        for step in ([("up", NHC * e + n)] if e < E2 else []) + ([("down", 2 * (e - 1) + n)] if e and n < 2 else [])]
FRONT_AT = {
    3: [("turn_slots", 0), ("turn_slots", 1)], 4: [("turn_slots", 2), ("turn_slots", 3)],
    5: [("turn_slots", 4), ("turn_slots", 5)], 6: [("turn_slots", 6), ("turn_slots", 7), ("inner", 0)],
    8: [("turn_inner", 0), ("inner", 1)], 9: [("turn_inner", 1)],
    10: [("turn_inner", 2), ("inner", 2)], 11: [("turn_inner", 3)],
    12: [("turn_inner", 4), ("inner", 3)], 13: [("turn_inner", 5)],
    14: [("turn_inner", 6), ("logits", 0)], 15: [("turn_inner", 7), ("turn_logits", 0), ("logits", 1)],
    16: [("turn_logits", 1)], 17: [("exp", 0), ("exp", 1)], 18: [("logits", 2), ("sums", 0), ("sums", 1)],
    19: [("turn_disp", 0), ("turn_logits", 2), ("logits", 3)], 20: [("turn_disp", 1), ("turn_logits", 3)],
    21: [("slots2", 0), ("slots2", 1)], 22: [("exp", 2), ("exp", 3), ("slots2", 2)],
    23: [("sums", 2), ("sums", 3), ("slots2", 3)],
}
FRONT = [step for n in sorted(FRONT_AT) for step in FRONT_AT[n]]
BOTH = [step for n in range(len(BACK)) for step in [BACK[n]] + FRONT_AT.get(n, [])]
SLOTS2 = [("slots2", i) for i in range(2 * (TE // 4))]
TAIL = ([("turn_disp", 2)] + SLOTS2[4:5] + [("turn_disp", 3)] + SLOTS2[5:6] + [("bias", 0)] + SLOTS2[6:8] +
        [s for q in range(TE // 4) for s in (("back", 2 * q), ("back", 2 * q + 1), ("turn_comb", q))])
BOTH = BOTH + TAIL
ALONE = FRONT + [("turn_disp", 2), ("turn_disp", 3)] + SLOTS2[4:] + [("bias", 0)] + [("turn_comb", q) for q in range(TE // 4)]
LAST = BACK + [s for s in TAIL if s[0] == "back"]


def experts(nc, ctx, sem, sb, bank, g):
    cst, ident, half = g["cst"], g["ident"], g["half"]
    two = range(2)
    NQ = TE // 4
    NR = ROWS // P
    NU = 2 * E2
    UC = HID // 2
    DB = D - P
    yk = sb("yk", [P, TE, D + DB])
    ykT = sb("ykT", [F, 2, TE * P])
    mT = sb("mT", [F, 2, ROWS])
    ws = sb("ws", [F, 2, E2 * D])
    sqj = sb("sqj2", [P, E2, D])
    s_ss = sb("s_ss", [P, E2])
    s_sv = sb("s_sv", [P, E2])
    s_sr = sb("s_sr", [P, E2])
    se = [sb(f"se{i}", [P, E2, D]) for i in two]
    seT = sb("seT", [F, 2, TE, P])
    lm = [sb(f"lm{i}", [P, 4, P]) for i in two]
    mc = sb("mc", [P, 4])
    md = sb("md", [P, 4])
    exc = sb("exc", [P, TE, P])
    exd = [sb(f"exd{i}", [P, 4, P]) for i in two]
    zc = sb("zc", [P, TE])
    rzc = sb("rzc", [P, TE])
    zi = sb("zi", [P, 4])
    rzi = sb("rzi", [P, 4])
    cmT = sb("cmT", [P, TE, P])
    dm = sb("dm", [P, TE, P])
    sAh = sb("sAh", [P, E2, ROWS], F32R)
    sAl = sb("sAl", [P, E2, ROWS], F32R)
    sB = sb("sB", [P, E2, ROWS], F32R)
    w1r = [sb(f"w1r{i}", [P, 2, 2, UC]) for i in two]
    w1h = [sb(f"w1h{i}", [P, 2, 2, UC], F32R) for i in two]
    w1l = [sb(f"w1l{i}", [P, 2, 2, UC], F32R) for i in two]
    w2r = sb("w2r", [P, NHC, D])
    w2h = sb("w2h", [P, NHC, D], F32R)
    w2l = sb("w2l", [P, NHC, D], F32R)
    b1r = sb("b1r", [P, P])
    b1T = sb("b1T", [P, E2 * 2 * NHC])
    b2b = sb("b2b", [P, E2, D])
    gl = [sb(f"gl{i}", [P, ROWS]) for i in two]
    ah = sb("ah", [P, NHC + 1, ROWS], F32R)
    al = sb("al", [P, NHC + 1, ROWS], F32R)
    os_ = [sb(f"os{i}", [P, NR, D]) for i in two]
    oS = sb("oS", [P, TE, D])
    o2 = [os_[i // 2][:, 2 * (i % 2):2 * (i % 2) + 2, :] for i in range(4)]

    s_zero = sem("b1_cleared")
    yk_dup, s_ws, s_b1, s_b2 = sem("yk_doubled"), sem("ws_loaded"), sem("b1_loaded"), sem("b2_loaded")
    s_yk = [sem(f"yk_loaded{h}") for h in two]
    s_w1 = [sem(f"w1_loaded{i}") for i in two]
    s_w2 = sem("w2_loaded")
    w1_hi, w1_lo, w2_hi, w2_lo = sem("w1_hi"), sem("w1_lo"), sem("w2_hi"), sem("w2_lo")
    b1_mm, b1_ev = sem("b1_mm"), sem("b1_ev")
    yT_mm, yT_ev, mean = sem("yT_mm"), sem("yT_ev"), sem("mean")
    se_mm, se_sq, se_v, se_r, se_n = (sem(n) for n in ("se_mm", "se_sq", "se_v", "se_r", "se_n"))
    seT_mm, seT_e0, seT_e1 = (sem(n) for n in ("seT_mm", "seT_e0", "seT_e1"))
    l_mm, l_add, c_max, c_sub, lT_mm, d_max, d_sub, l_exp = (
        sem(n) for n in ("l_mm", "l_add", "c_max", "c_sub", "lT_mm", "d_max", "d_sub", "l_exp"))
    z_c, z_d, z_r, e_n, d_mm, t_d, c_mm, t_c = (
        sem(n) for n in ("z_c", "z_d", "z_r", "e_n", "d_mm", "t_d", "c_mm", "t_c"))
    s2_mm, s2_hi, s2_lo = (sem(n) for n in ("s2_mm", "s2_hi", "s2_lo"))
    u_mm, u_gl, u_act, a_hi, a_lo, o_mm, o_ev = (sem(n) for n in ("u_mm", "u_gelu", "u_act", "a_hi", "a_lo", "oo_mm", "oo_ev"))
    s_os = [sem(f"shuffled{i}") for i in two]
    s_o2 = [sem(f"o2_stored{i}") for i in range(4)]
    x_mm, x_rz, x_ev = (sem(n) for n in ("x_mm", "x_rz", "x_ev"))
    block = ctx.enter_context(nc.Block())
    S2_BANKS = (2, 5, 6, 3)
    BACK_BANKS = (4, 7, 5, 6)
    SH = 4

    def all_experts(eng, run):
        run(ALONE, None, 0)
        run(BOTH, 0, 1)
        with eng.Fori(1, NE - 1, 1) as k:
            run(BOTH, k, k + 1)
        run(LAST, NE - 1, None)

    @block.sync
    def _(sp):
        def load_front(f):
            if exists(2 * NQ * (f - 1) + 2 * NQ - 1):
                sp.wait_ge(s2_mm, 1)
                sp.wait_ge(s2_mm, 2 * NQ * (f - 1) + 2 * NQ)
            src = g["yn_d"].rearrange("(t b) e s q d -> e b (s q) t d", b=2)[f]
            for h in two:
                tiles = slice(h * TE // 2, (h + 1) * TE // 2)
                for b in two:
                    sp.dma_start(yk[64 * b:64 * b + 64, tiles, 0:D], src[b][:, tiles, :]).then_inc(s_yk[h], 16)
            if exists(NR * (f - 1) + NR - 1):
                sp.wait_ge(se_mm, 1)
                sp.wait_ge(se_mm, NR * (f - 1) + NR)
            sp.dma_start(ws[:, :, :], g["w_slot2"].rearrange("e (c p) n -> e p c n", c=2)[f]).then_inc(s_ws, 16)
            if isinstance(f, int) and f == 0:
                sp.wait_ge(s_zero, 1)
            if exists(f - 1):
                sp.wait_ge(b1_mm, 1)
                sp.wait_ge(b1_mm, f)
            sp.dma_start(b1r[0:E2 * 2 * NHC, :], g["b1"].rearrange("k e (c p) -> k (e c) p", p=P)[f]).then_inc(s_b1, 16)

        def load_b2(k):
            if exists(2 * E2 * (k - 1) + 2 * E2 - 1):
                sp.wait_ge(o_ev, 1)
                sp.wait_ge(o_ev, 2 * E2 * (k - 1) + 2 * E2)
            sp.dma_start(b2b[:, :, :], g["b2"][k].partition_broadcast(P)).then_inc(s_b2, 16)

        def load_w1(k, j):
            if exists(NU * k + j - 2):
                sp.wait_ge(w1_lo, 1)
                sp.wait_ge(w1_lo, NU * k + j - 1)
            src = g["w1"].rearrange("k e d (c u n) -> k e u d c n", c=2, u=2)[k, j // 2, j % 2]
            sp.dma_start(w1r[j % 2][:, 0, :, :], src[0:P]).then_inc(s_w1[j % 2], 16)
            for r in two:
                sp.dma_start(w1r[j % 2][r * DB:(r + 1) * DB, 1, :, :], src[P:D]).then_inc(s_w1[j % 2], 16)

        def load_w2(k, e):
            if exists(E2 * k + e - 1):
                sp.wait_ge(w2_lo, 1)
                sp.wait_ge(w2_lo, E2 * k + e)
            sp.dma_start(w2r[:, :, :], g["w2"].rearrange("k e (c p) n -> k e p c n", p=P)[k, e]).then_inc(s_w2, 16)

        def run(order, k, f):
            if k is None:
                load_front(f)
                load_w1(0, 0)
                load_w1(0, 1)
                load_w2(0, 0)
                load_b2(0)
                load_w1(0, 2)
                return
            if f is not None:
                load_front(f)
            for name, i in order:
                if name == "up" and i % 2 == 1:
                    j = i // 2 + 3
                    if j < NU:
                        load_w1(k, j)
                    elif f is not None:
                        load_w1(f, j - NU)
                    if i % NHC == 3:
                        if i // NHC + 1 < E2:
                            load_w2(k, i // NHC + 1)
                        elif f is not None:
                            load_w2(f, 0)
                elif name == "down" and i % 2 == 1:
                    e = i // 2
                    sp.wait_ge(o_ev, 1)
                    sp.wait_ge(o_ev, 2 * E2 * k + i + 1)
                    if e == 0:
                        if exists(8 * (k - 1) + 7):
                            sp.wait_ge(x_mm, 1)
                            sp.wait_ge(x_mm, 8 * (k - 1) + 8)
                    for j in range(4):
                        sp.dma_start(oS[:, :, :].rearrange("p (r j) d -> p j r d", j=4)[32 * e:32 * e + 32, j, :, :],
                                     os_[e % 2][32 * j:32 * j + 32, :, :]).then_inc(s_os[e % 2], 16)
                    if e == E2 - 1 and f is not None:
                        load_b2(f)
                elif name == "back":
                    sp.wait_ge(x_ev, 1)
                    sp.wait_ge(x_ev, 8 * k + i + 1)
                    dst = g["o2_d"].rearrange("(t b) e s q d -> e b (s q) t d", b=2)[k]
                    for b in two:
                        sp.dma_start(dst[b][:, 2 * i:2 * i + 2, :], o2[i % 4][64 * b:64 * b + 64, :, :]).then_inc(s_o2[i % 4], 16)

        all_experts(sp, run)
        for i in range(4):
            sp.wait_ge(s_o2[i], 32 * 2 * NE)

    @block.tensor
    def _(pe):
        mm, tr = nc.tensor.matmul, nc.tensor.transpose

        def turn_slots(f, i):
            if i == 0:
                pe.wait_ge(s_yk[0], (f + 1) * 32)
                if exists(8 * (f - 2) + 7):
                    pe.wait_ge(x_ev, 8 * (f - 2) + 8)
                if exists(f - 1):
                    pe.wait_ge(b1_ev, f)
            if i == 4:
                pe.wait_ge(s_yk[1], (f + 1) * 32)
            if i < 2:
                if exists(2 * NQ * (f - 1) + 2 * NQ - 1):
                    pe.wait_ge(s2_lo, 2 * NQ * (f - 1) + 2 * NQ)
            if exists(8 * f + i - 2):
                pe.wait_ge(yT_ev, 8 * f + i - 1)
            for c in two:
                for t in two:
                    ins = tr(bank[5 + i % 2][0:F, (2 * c + t) * P:(2 * c + t + 1) * P], yk[:, 2 * i + t, c * F:(c + 1) * F], ident)
            ins.then_inc(yT_mm, 1)

        def inner(f, r):
            if r == 0:
                pe.wait_ge(s_ws, 16 * f + 16)
                pe.wait_ge(yT_ev, 8 * f + 8)
            pe.wait_ge(mean, NR * f + r + 1)
            if exists(NR * f + r - 1):
                pe.wait_ge(se_n, NR * f + r)
            for h in two:
                for c in two:
                    ins = mm(bank[5 + h][:, 0:2 * D], mT[:, c, r * P:(r + 1) * P], ws[:, c, h * 2 * D:(h + 1) * 2 * D],
                             start=c == 0, stop=c == 1)
            ins.then_inc(se_mm, 1)

        def turn_inner(f, i):
            r, c = i // 2, i % 2
            pe.wait_ge(se_n, NR * f + r + 1)
            if exists(NR * f + r - (1 - c)):
                pe.wait_ge(seT_e0 if c else seT_e1, NR * f + r - (1 - c) + 1)
            for e in range(E2):
                ins = tr(bank[7][0:F, e * P:(e + 1) * P], se[r % 2][:, e, c * F:(c + 1) * F], ident)
            ins.then_inc(seT_mm, 1)

        def logits(f, q):
            pe.wait_ge(seT_e0, NR * f + q + 1)
            pe.wait_ge(seT_e1, NR * f + q + 1)
            if exists(NQ * f + q - 1):
                pe.wait_ge(l_add, NQ * f + q)
            for j in range(4):
                t = 4 * q + j
                for c in two:
                    ins = mm(bank[5][:, j * P:(j + 1) * P], ykT[:, c, t * P:(t + 1) * P], seT[:, c, t, :],
                             start=c == 0, stop=c == 1)
            ins.then_inc(l_mm, 1)

        def turn_logits(f, q):
            pe.wait_ge(l_add, NQ * f + q + 1)
            if exists(NQ * f + q - 1):
                pe.wait_ge(d_sub, NQ * f + q)
            for j in range(4):
                ins = tr(bank[6][:, j * P:(j + 1) * P], lm[q % 2][:, j, :], ident)
            ins.then_inc(lT_mm, 1)

        def turn_disp(f, q):
            pe.wait_ge(e_n, NQ * f + q + 1)
            if exists(NQ * f + q - 1):
                pe.wait_ge(t_d, NQ * f + q)
            if q == 0:
                pe.wait_ge(seT_e1, NR * f + NR)
            for j in range(4):
                ins = tr(bank[7][:, j * P:(j + 1) * P], exd[q % 2][:, j, :], ident)
            ins.then_inc(d_mm, 1)

        def slots2(f, k, i):
            q, c = i // 2, i % 2
            pe.wait_ge(t_d, NQ * f + q + 1)
            if i == 0:
                pe.wait_ge(yk_dup, f + 1)
            if i == 0:
                if k is not None:
                    pe.wait_ge(u_act, 16 * k + 15)
            elif i < 3:
                pe.wait_ge(d_sub, NQ * f + NQ)
            elif i == 3:
                if k is not None:
                    pe.wait_ge(u_act, 16 * k + 16)
            else:
                pe.wait_ge(s2_lo, 2 * NQ * f + i - 3)
            for j in range(4):
                ins = mm(bank[S2_BANKS[i % 4]][:, j * P:(j + 1) * P], yk[:, 4 * q + j, c * P:(c + 1) * P], dm[:, 4 * q + j, :],
                         start=True, stop=True)
            ins.then_inc(s2_mm, 1)

        def bias(f):
            pe.wait_ge(s_b1, 16 * f + 16)
            pe.wait_ge(t_d, NQ * f + NQ)
            tr(bank[7][:, 0:P], b1r[:, :], ident).then_inc(b1_mm, 1)

        def turn_comb(f, k, q):
            pe.wait_ge(l_exp, NQ * f + q + 1)
            if q > 1:
                pe.wait_ge(t_c, NQ * f + q - 1)
            elif k is not None:
                pe.wait_ge(u_act, 16 * k + 16)
            for j in range(4):
                ins = tr(bank[q % 2][:, j * P:(j + 1) * P], exc[:, 4 * q + j, :], ident)
            ins.then_inc(c_mm, 1)

        def up(k, n):
            e, h = n // NHC, n % NHC
            j = n // 2
            cols = slice((n % 2) * P, (n % 2 + 1) * P)
            if n % 2 == 0:
                pe.wait_ge(w1_lo, NU * k + j + 1)
            if n == 0:
                pe.wait_ge(s2_lo, 2 * NQ * k + 2 * NQ)
                pe.wait_ge(t_c, NQ * k + NQ - 1)
            if n == 1:
                pe.wait_ge(t_c, NQ * k + NQ)
            if n > 1:
                pe.wait_ge(u_act, 16 * k + n - 1)
            wh, wl = w1h[j % 2], w1l[j % 2]
            for c, b in ((1, 2), (0, 0)):
                out = bank[b + n % 2][:, :]
                mm(out, wh[:, 0, c, cols], sAh[:, e, :], start=True, stop=False)
                mm(out, wh[:, 0, c, cols], sAl[:, e, :], start=False, stop=False)
                mm(out, wl[:, 0, c, cols], sAh[:, e, :], start=False, stop=False)
                mm(out, wh[:, 1, c, cols], sB[:, e, :], start=False, stop=False)
                ins = mm(out, wl[0:DB, 1, c, cols], sB[0:DB, e, :], start=False, stop=True)
            ins.then_inc(u_mm, 1)

        def down(k, n):
            e, i = n // 2, n % 2
            if i == 0:
                pe.wait_ge(a_lo, 16 * k + NHC * e + NHC)
                pe.wait_ge(w2_lo, E2 * k + e + 1)
            if n == 0:
                if exists(8 * (k - 1) + 7):
                    pe.wait_ge(x_ev, 8 * (k - 1) + 8)
            else:
                pe.wait_ge(o_ev, 2 * E2 * k + n)
            for r in range(2 * i, 2 * i + 2):
                out, cols = bank[4][:, (r % 2) * D:(r % 2 + 1) * D], slice(r * P, (r + 1) * P)
                for h in range(NHC):
                    mm(out, ah[:, (NHC * e + h) % (NHC + 1), cols], w2h[:, h, :], start=h == 0, stop=False)
                    mm(out, ah[:, (NHC * e + h) % (NHC + 1), cols], w2l[:, h, :], start=False, stop=False)
                    ins = mm(out, al[:, (NHC * e + h) % (NHC + 1), cols], w2h[:, h, :], start=False, stop=h == NHC - 1)
            ins.then_inc(o_mm, 1)

        def back(k, f, i):
            if i == 0:
                for j in two:
                    pe.wait_ge(s_os[j], (2 * k + 2) * 16 * SH)
                pe.wait_ge(o_ev, 2 * E2 * k + 2 * E2)
                pe.wait_ge(t_c, NQ * k + NQ)
            elif i >= 4:
                pe.wait_ge(x_ev, 8 * k + i - 3)
            elif f is not None:
                if i == 1:
                    pe.wait_ge(b1_ev, f + 1)
                else:
                    pe.wait_ge(s2_lo, 2 * NQ * f + i + 4)
            for t in two:
                ins = mm(bank[BACK_BANKS[i % 4]][:, t * D:(t + 1) * D], cmT[:, 2 * i + t, :], oS[:, 2 * i + t, :], start=True, stop=True)
            ins.then_inc(x_mm, 1)

        def run(order, k, f):
            for name, i in order:
                if name == "turn_slots":
                    turn_slots(f, i)
                elif name == "inner":
                    inner(f, i)
                elif name == "turn_inner":
                    turn_inner(f, i)
                elif name == "logits":
                    logits(f, i)
                elif name == "turn_logits":
                    turn_logits(f, i)
                elif name == "turn_disp":
                    turn_disp(f, i)
                elif name == "slots2":
                    slots2(f, k, i)
                elif name == "bias":
                    bias(f)
                elif name == "turn_comb":
                    turn_comb(f, k, i)
                elif name == "up":
                    up(k, i)
                elif name == "down":
                    down(k, i)
                elif name == "back":
                    back(k, f, i)

        all_experts(pe, run)

    @block.vector
    def _(dve):
        v = nc.vector
        v.memset(b1r[:, :], 0.0).then_inc(s_zero, 1)

        def means(f, r):
            dve.wait_ge(yT_ev, 8 * f + 2 * r + 2)
            for c in two:
                ins = v.reduce_sum(mT[:, c, r * P:(r + 1) * P].rearrange("p (m q) -> p m q", q=GQ),
                                   ykT[:, c, 512 * r:512 * (r + 1)].rearrange("p (m n q) -> p m q n", n=4, q=GQ), AX.X)
            ins.then_inc(mean, 1)

        def inner(f, r):
            i = NR * f + r
            dve.wait_ge(se_sq, i + 1)
            if exists(i - 1):
                dve.wait_ge(se_r, i)
            v.tensor_scalar(s_sv[:, :], s_ss[:, :], 1.0 / D, NS * 1e-6 / D, ALU.mult, ALU.add).then_inc(se_v, 1)
            dve.wait_ge(se_r, i + 1)
            if exists(2 * (i - 2) + 1):
                dve.wait_ge(seT_mm, 2 * (i - 2) + 2)
            for h in two:
                ins = v.tensor_tensor(se[r % 2][:, 2 * h:2 * h + 2, :], bank[5 + h][:, 0:2 * D].rearrange("p (e d) -> p e d", e=2),
                                      s_sr[:, 2 * h:2 * h + 2].unsqueeze(2).to_broadcast([P, 2, D]), ALU.mult)
            ins.then_inc(se_n, 1)

        def turn_inner(f, i):
            if i % 2:
                r = i // 2
                dve.wait_ge(seT_mm, 2 * (NR * f + r) + 2)
                v.tensor_copy(seT[:, 1, 4 * r:4 * r + 4, :].rearrange("p t (e n) -> p t e n", e=E2),
                              bank[7][0:F, :].rearrange("p (e t n) -> p t e n", e=E2, t=4)).then_inc(seT_e1, 1)

        def logits(f, q):
            i = NQ * f + q
            dve.wait_ge(l_mm, i + 1)
            if exists(i - 2):
                dve.wait_ge(lT_mm, i - 1)
            if exists(i - 2):
                dve.wait_ge(c_sub, i - 1)
            v.tensor_tensor(lm[q % 2][:, :, :], bank[5][:, :].rearrange("p (j n) -> p j n", j=4),
                            cst[:, C_M1:C_M1 + P].unsqueeze(1).to_broadcast([P, 4, P]), ALU.add).then_inc(l_add, 1)
            dve.wait_ge(l_add, i + 1)
            v.reduce_max(mc[:, :], lm[q % 2][:, :, :], AX.X).then_inc(c_max, 1)
            dve.wait_ge(c_max, i + 1)
            if exists(NQ * (f - 1) + q):
                dve.wait_ge(c_mm, NQ * (f - 1) + q + 1)
            v.tensor_tensor(exc[:, 4 * q:4 * q + 4, :], lm[q % 2][:, :, :], mc[:, :].unsqueeze(2).to_broadcast([P, 4, P]),
                            ALU.subtract).then_inc(c_sub, 1)

        def turn_logits(f, q):
            i = NQ * f + q
            dve.wait_ge(lT_mm, i + 1)
            if exists(i - 1):
                dve.wait_ge(d_sub, i)
            b = bank[6][:, :].rearrange("p (j n) -> p j n", j=4)
            v.reduce_max(md[:, :], b, AX.X).then_inc(d_max, 1)
            dve.wait_ge(d_max, i + 1)
            if exists(i - 2):
                dve.wait_ge(d_mm, i - 1)
            v.tensor_tensor(exd[q % 2][:, :, :], b, md[:, :].unsqueeze(2).to_broadcast([P, 4, P]), ALU.subtract).then_inc(d_sub, 1)

        def sums(f, q):
            i = NQ * f + q
            dve.wait_ge(l_exp, i + 1)
            if exists(i - 1):
                dve.wait_ge(z_r, i)
            v.reduce_sum(zi[:, :], exd[q % 2][:, :, :], AX.X).then_inc(z_d, 1)
            dve.wait_ge(z_d, i + 1)
            if exists(i - 1):
                dve.wait_ge(e_n, i)
            v.reciprocal(rzi[:, :], zi[:, :]).then_inc(z_r, 1)
            if q == 0:
                if exists(f - 1):
                    dve.wait_ge(x_rz, f)
            v.reduce_sum(zc[:, 4 * q:4 * q + 4], exc[:, 4 * q:4 * q + 4, :], AX.X).then_inc(z_c, 1)

        def slots2(f, i):
            q, c = i // 2, i % 2
            dve.wait_ge(s2_hi, 2 * NQ * f + i + 1)
            lo, hi = (slice(0, P), sAh) if c == 0 else (slice(DB, P), sB)
            out = sAl if c == 0 else sB
            v.tensor_tensor(out[lo, :, P * q:P * (q + 1)].rearrange("p e (j n) -> p j e n", j=4),
                            bank[S2_BANKS[i % 4]][lo, :].rearrange("p (j e n) -> p j e n", j=4, e=E2),
                            hi[lo, :, P * q:P * (q + 1)].rearrange("p e (j n) -> p j e n", j=4).bitcast(F32),
                            ALU.subtract).then_inc(s2_lo, 1)

        def bias(f):
            dve.wait_ge(b1_mm, f + 1)
            v.tensor_copy(b1T[:, :], bank[7][:, 0:E2 * 2 * NHC]).then_inc(b1_ev, 1)

        def low(k, n):
            dve.wait_ge(a_hi, 16 * k + n + 1)
            v.tensor_tensor(al[:, n % (NHC + 1), :], gl[n % 2][:, :], ah[:, n % (NHC + 1), :].bitcast(F32), ALU.subtract).then_inc(a_lo, 1)

        def up(k, n):
            dve.wait_ge(u_gl, 16 * k + n + 1)
            c = n // NHC * 2 * NHC + n % NHC
            v.scalar_tensor_tensor(gl[n % 2][:, :], bank[n % 2][:, :], b1T[:, c:c + 1], gl[n % 2][:, :],
                                   ALU.add, ALU.mult).then_inc(u_act, 1)

        def down(k, n):
            e, i = n // 2, n % 2
            dve.wait_ge(o_mm, 2 * E2 * k + n + 1)
            if n == 0:
                dve.wait_ge(s_b2, 16 * k + 16)
            if i == 0:
                if exists(2 * k + e // 2 - 1):
                    dve.wait_ge(s_os[e % 2], (2 * k + e // 2) * 16 * SH)
                if e < 2:
                    for j in two:
                        if exists(2 * k - 1):
                            dve.wait_ge(s_o2[2 * e + j], (2 * k) * 32)
            v.tensor_tensor(os_[e % 2][:, 2 * i:2 * i + 2, :], bank[4][:, 0:2 * D].rearrange("p (r d) -> p r d", r=2),
                            b2b[:, e, :].unsqueeze(1).to_broadcast([P, 2, D]), ALU.add).then_inc(o_ev, 1)

        def back(k, i):
            dve.wait_ge(x_mm, 8 * k + i + 1)
            if i == 0:
                dve.wait_ge(x_rz, k + 1)
            if i >= 4:
                dve.wait_ge(s_o2[i % 4], (2 * k + 1) * 32)
            v.tensor_tensor(o2[i % 4], bank[BACK_BANKS[i % 4]][:, 0:2 * D].rearrange("p (t d) -> p t d", t=2),
                            rzc[:, 2 * i:2 * i + 2].unsqueeze(2).to_broadcast([P, 2, D]), ALU.mult).then_inc(x_ev, 1)

        def run(order, k, f):
            for name, i in order:
                if name == "turn_slots":
                    if i % 2:
                        means(f, i // 2)
                elif name == "inner":
                    inner(f, i)
                elif name == "turn_inner":
                    turn_inner(f, i)
                elif name == "logits":
                    logits(f, i)
                elif name == "turn_logits":
                    turn_logits(f, i)
                elif name == "sums":
                    sums(f, i)
                elif name == "slots2":
                    slots2(f, i)
                elif name == "bias":
                    bias(f)
                elif name == "up":
                    if i > 0:
                        low(k, i - 1)
                    up(k, i)
                    if i == 15:
                        low(k, i)
                elif name == "down":
                    down(k, i)
                elif name == "back":
                    back(k, i)
            if f is not None:
                dve.wait_ge(z_c, NQ * f + NQ)
                if exists(8 * (f - 1) + 7):
                    dve.wait_ge(x_ev, 8 * (f - 1) + 8)
                v.reciprocal(rzc[:, :], zc[:, :]).then_inc(x_rz, 1)

        all_experts(dve, run)

    @block.scalar
    def _(act):
        f_ = nc.scalar.activation

        def split_w1(k, j):
            act.wait_ge(s_w1[j % 2], (4 * k + j // 2 + 1) * 48)
            if exists(16 * k + 2 * (j - 2) + 1):
                act.wait_ge(u_mm, 16 * k + 2 * (j - 2) + 2)
            f_(w1h[j % 2][:, :, :, :], w1r[j % 2][:, :, :, :], ACT.Copy).then_inc(w1_hi, 1)

        def split_w2(k, e):
            act.wait_ge(s_w2, (E2 * k + e + 1) * 16)
            if exists(2 * (E2 * k + e - 1) + 1):
                act.wait_ge(o_mm, 2 * (E2 * k + e - 1) + 2)
            f_(w2h[:, :, :], w2r[:, :, :], ACT.Copy).then_inc(w2_hi, 1)

        def turn_slots(f, i):
            act.wait_ge(yT_mm, 8 * f + i + 1)
            f_(ykT[:, :, 256 * i:256 * (i + 1)], bank[5 + i % 2][0:F, :].rearrange("p (c n) -> p c n", c=2),
               ACT.Copy).then_inc(yT_ev, 1)
            if i == 7:
                for h in two:
                    act.wait_ge(s_yk[h], (f + 1) * 32)
                f_(yk[:, :, D:D + DB], yk[:, :, P:D], ACT.Copy).then_inc(yk_dup, 1)

        def inner(f, r):
            act.wait_ge(se_mm, NR * f + r + 1)
            if exists(NR * f + r - 1):
                act.wait_ge(se_v, NR * f + r)
            for e in range(E2):
                ins = f_(sqj[:, e, :], bank[5 + e // 2][:, (e % 2) * D:(e % 2 + 1) * D], ACT.Square, accum_out=s_ss[:, e:e + 1])
            ins.then_inc(se_sq, 1)

        def turn_inner(f, i):
            if i % 2 == 0:
                r = i // 2
                act.wait_ge(seT_mm, 2 * (NR * f + r) + 1)
                f_(seT[:, 0, 4 * r:4 * r + 4, :].rearrange("p t (e n) -> p t e n", e=E2),
                   bank[7][0:F, :].rearrange("p (e t n) -> p t e n", e=E2, t=4), ACT.Copy).then_inc(seT_e0, 1)

        def exp(f, q):
            i = NQ * f + q
            act.wait_ge(c_sub, i + 1)
            f_(exc[:, 4 * q:4 * q + 4, :], exc[:, 4 * q:4 * q + 4, :], ACT.Exp)
            act.wait_ge(d_sub, i + 1)
            f_(exd[q % 2][:, :, :], exd[q % 2][:, :, :], ACT.Exp).then_inc(l_exp, 1)

        def turn_disp(f, q):
            act.wait_ge(d_mm, NQ * f + q + 1)
            f_(dm[:, 4 * q:4 * q + 4, :].rearrange("p t n -> p (t n)"), bank[7][:, :], ACT.Copy).then_inc(t_d, 1)

        def slots2(f, i):
            q, c = i // 2, i % 2
            act.wait_ge(s2_mm, 2 * NQ * f + i + 1)
            f_((sB if c else sAh)[:, :, P * q:P * (q + 1)].rearrange("p e (j n) -> p j e n", j=4),
               bank[S2_BANKS[i % 4]][:, :].rearrange("p (j e n) -> p j e n", j=4, e=E2), ACT.Copy).then_inc(s2_hi, 1)

        def turn_comb(f, q):
            act.wait_ge(c_mm, NQ * f + q + 1)
            if exists(8 * (f - 1) + 2 * q + 1):
                act.wait_ge(x_mm, 8 * (f - 1) + 2 * q + 2)
            f_(cmT[:, 4 * q:4 * q + 4, :].rearrange("p t n -> p (t n)"), bank[q % 2][:, :], ACT.Copy).then_inc(t_c, 1)

        def high(k, n):
            act.wait_ge(u_act, 16 * k + n + 1)
            if n < NHC + 1:
                if exists(2 * E2 * (k - 1) + 2 * E2 - 1):
                    act.wait_ge(o_mm, 2 * E2 * (k - 1) + 2 * E2)
            else:
                act.wait_ge(o_mm, 2 * (E2 * k + (n - NHC - 1) // NHC) + 2)
            f_(ah[:, n % (NHC + 1), :], gl[n % 2][:, :], ACT.Copy).then_inc(a_hi, 1)

        def up(k, n):
            i = 16 * k + n
            act.wait_ge(u_mm, i + 1)
            if n == 0:
                act.wait_ge(b1_ev, k + 1)
            if exists(i - 2):
                act.wait_ge(a_lo, i - 1)
            c = n // NHC * 2 * NHC + NHC + n % NHC
            f_(gl[n % 2][:, :], bank[2 + n % 2][:, :], ACT.Gelu_apprx_tanh, bias=b1T[:, c:c + 1]).then_inc(u_gl, 1)

        def run(order, k, f):
            if k is None:
                split_w1(0, 0)
            for name, i in order:
                if name == "turn_slots":
                    turn_slots(f, i)
                elif name == "inner":
                    inner(f, i)
                elif name == "turn_inner":
                    turn_inner(f, i)
                elif name == "exp":
                    exp(f, i)
                elif name == "turn_disp":
                    turn_disp(f, i)
                elif name == "slots2":
                    slots2(f, i)
                elif name == "turn_comb":
                    turn_comb(f, i)
                elif name == "up":
                    if i % 2 == 0:
                        if i // 2 + 1 < NU:
                            split_w1(k, i // 2 + 1)
                        elif f is not None:
                            split_w1(f, 0)
                    if i > 0:
                        high(k, i - 1)
                    up(k, i)
                    if i % NHC == 2:
                        split_w2(k, i // NHC)
                    if i == 15:
                        high(k, i)

        all_experts(act, run)

    @block.gpsimd
    def _(pool):
        p = nc.gpsimd

        def split_w1(k, j):
            pool.wait_ge(w1_hi, NU * k + j + 1)
            p.tensor_tensor(w1l[j % 2][:, :, :, :].rearrange("p a c n -> p (a c n)"),
                            w1r[j % 2][:, :, :, :].rearrange("p a c n -> p (a c n)"),
                            w1h[j % 2][:, :, :, :].rearrange("p a c n -> p (a c n)").bitcast(F32), ALU.subtract).then_inc(w1_lo, 1)

        def run(order, k, f):
            if k is None:
                split_w1(0, 0)
            for name, n in order:
                if name == "inner":
                    i = NR * f + n
                    pool.wait_ge(se_v, i + 1)
                    if exists(i - 1):
                        pool.wait_ge(se_n, i)
                    p.tensor_tensor(s_sr[:, :], s_sv[:, :], half[:, 0:E2], ALU.pow).then_inc(se_r, 1)
                elif name == "sums":
                    pool.wait_ge(z_r, NQ * f + n + 1)
                    p.tensor_tensor(exd[n % 2][:, :, :], exd[n % 2][:, :, :], rzi[:, :].unsqueeze(2).to_broadcast([P, 4, P]),
                                    ALU.mult).then_inc(e_n, 1)
                elif name == "up":
                    if n % 2 == 0:
                        if n // 2 + 1 < NU:
                            split_w1(k, n // 2 + 1)
                        elif f is not None:
                            split_w1(f, 0)
                    if n % NHC == 2:
                        pool.wait_ge(w2_hi, E2 * k + n // NHC + 1)
                        p.tensor_tensor(w2l[:, :, :], w2r[:, :, :], w2h[:, :, :].bitcast(F32), ALU.subtract).then_inc(w2_lo, 1)

        all_experts(pool, run)


def combine(nc, ctx, sem, sb, bank, g):
    two = range(2)
    o2 = [sb(f"o2b{i}", [P, GQ, D]) for i in two]
    cT = [sb(f"cTb{i}", [P, S]) for i in two]
    h2 = [sb(f"h2b{i}", [P, NT, D + 1]) for i in two]
    rz = sb("rzb", [P, 2, NT])
    ob = [sb(f"ob{i}", [P, NT, D]) for i in two]
    s_ld = [sem(f"c_loaded{i}") for i in two]
    s_st = [sem(f"c_stored{i}") for i in two]
    c_mm, c_rz, c_ev = sem("tokens_mm"), sem("tokens_rz"), sem("tokens_out")
    block = ctx.enter_context(nc.Block())
    LD = 3

    def each_pair(eng, body):
        for u in two:
            body(0, u)
        with eng.Fori(1, NB // 2, 1) as a:
            for u in two:
                body(a, u)

    @block.sync
    def _(sp):
        def body(a, u):
            n = 2 * a + u
            if exists(n - 2):
                sp.wait_ge(c_ev, 1)
                sp.wait_ge(c_ev, n - 1)
            sp.dma_start(o2[u][:, :, :], g["o2_d"][n].rearrange("e s q d -> (e s) q d")).then_inc(s_ld[u], 16)
            sp.dma_start(cT[u][:, :], g["combT_d"][n]).then_inc(s_ld[u], 16)
            sp.dma_start(h2[u][:, :, :], g["h2_d"][n]).then_inc(s_ld[u], 16)

        each_pair(sp, body)

    @block.tensor
    def _(pe):
        def body(a, u):
            n = 2 * a + u
            pe.wait_ge(s_ld[u], (a + 1) * 16 * LD)
            if exists(n - 2):
                pe.wait_ge(c_ev, n - 1)
            for t in two:
                for q in two:
                    c = t * P + 64 * q
                    ins = nc.tensor.matmul(bank[u][64 * q:64 * q + 64, t * D:(t + 1) * D], cT[u][:, c:c + 64],
                                           o2[u][:, 2 * t + q, :], start=True, stop=True)
            ins.then_inc(c_mm, 1)

        each_pair(pe, body)

    @block.vector
    def _(dve):
        def body(a, u):
            n = 2 * a + u
            dve.wait_ge(s_ld[u], (a + 1) * 16 * LD)
            if exists(n - 2):
                dve.wait_ge(c_ev, n - 1)
            nc.vector.reciprocal(rz[:, u, :], h2[u][:, :, D]).then_inc(c_rz, 1)
            dve.wait_ge(c_rz, n + 1)
            dve.wait_ge(c_mm, n + 1)
            if exists(a - 1):
                dve.wait_ge(s_st[u], a * 16)
            for t in two:
                ins = nc.vector.scalar_tensor_tensor(ob[u][:, t, :], bank[u][:, t * D:(t + 1) * D], rz[:, u, t:t + 1],
                                                     h2[u][:, t, 0:D], ALU.mult, ALU.add)
            ins.then_inc(c_ev, 1)

        each_pair(dve, body)

    @block.scalar
    def _(act):
        def body(a, u):
            n = 2 * a + u
            act.wait_ge(c_ev, n + 1)
            act.dma_start(g["out"][n].rearrange("(t p) d -> p t d", p=P), ob[u][:, :, :]).then_inc(s_st[u], 16)

        each_pair(act, body)
        for u in two:
            act.wait_ge(s_st[u], 16 * NB // 2)


_INS = ["x", "consts", "rows", "L0_tok_scale", "L0_attn_W_qkv", "L0_attn_W_proj", "L0_attn_b_proj", "L0_attn_gamma",
        "L0_attn_beta", "L0_attn_random_features", "L0_ffn_gamma_in", "L0_ffn_slots1", "L0_ffn_gamma2",
        "L0_ffn_w_slot2", "L0_ffn_w1", "L0_ffn_b1", "L0_ffn_w2", "L0_ffn_b2"]


def kernel(**inputs):
    import concourse.bacc as _bacc
    from concourse.bass_utils import run_bass_kernel_spmd as _run

    inputs["consts"], inputs["rows"] = shape_constants()
    nc = _bacc.Bacc("TRN2", target_bir_lowering=False, num_devices=1)
    arrays, args = {}, []
    for name in _INS:
        a = np.ascontiguousarray(inputs[name])
        arrays[f"in_{name}"] = a
        args.append(nc.dram_tensor(f"in_{name}", a.shape, mybir.dt.from_np(a.dtype), kind="ExternalInput").ap())
    args.append(nc.dram_tensor("out_0", (NB, S, D), F32, kind="ExternalOutput").ap())
    build(nc, *args)
    r = _run(nc, [arrays], core_ids=[0])
    return r.results[0]["out_0"]
```

```python
import concourse.bass as bass
from concourse import mybir
from contextlib import ExitStack
import numpy as np

F32 = mybir.dt.float32
F32R = mybir.dt.float32r
I32 = mybir.dt.int32
ALU = mybir.AluOpType
ACT = mybir.ActivationFunctionType
AX = mybir.AxisListType

NB, S, D = 32, 256, 192
F = D // 2
P = 128
GQ = S // 64
NT = S // P
H, DH, M = 12, 16, 64
HC = 4
NC_ = H // HC
NG = NB * GQ
NE, NS, E2 = 8, 16, 4
M2 = NS // E2
HID = 512
NHC = HID // P
ROWS = NG * M2
TE = NG * NS // P
GT = P // NS
CB = 4
CT = CB * NT
HX = F + 2

TWO_PI = 2.0 * np.pi
ROUND = float(1.5 * 2.0**23)
PI_HI = 6.28125
PI_LO = float(np.float32(TWO_PI - PI_HI))
PI_MAX = 3.1415925

C_ID, C_MRF, C_INV, C_M1, C_EVEN, C_ODD, C_QUART, C_END = np.cumsum([0, P, HC * M, F, P, 1, 1, 1]).tolist()


def shape_constants():
    c = np.zeros((P, C_END), np.float32)
    c[:, C_ID:C_ID + P] = np.eye(P)
    for p in range(P):
        h = (p % 64) // DH
        c[p, C_MRF + h * M:C_MRF + (h + 1) * M] = 1.0 if p < 64 else -0.5
    c[:, C_INV:C_INV + F] = (1.0 / 10000.0 ** (2.0 * np.floor(np.arange(F) / 2.0) / F)).astype(np.float32)
    row = np.arange(P)
    slot_group = inner_group = row % (2 * GQ)
    other = np.where(slot_group[:, None] == inner_group[None, :], 0.0, -1e30)
    c[:, C_M1:C_M1 + P] = other
    odd = row % 2
    c[:, C_EVEN] = 1 - odd
    c[:, C_ODD] = odd
    c[:, C_QUART] = odd * (np.pi / 2)
    rows = np.zeros((NB, 2, S), np.float32)
    rows[:, 0] = np.arange(S) + 1
    rows[:, 1] = np.arange(S) % 2 == 0
    return c, rows


def exists(index):
    return not isinstance(index, int) or index >= 0


def build(nc, x, consts, rows, tok_scale, W_qkv, W_proj, b_proj, gamma, beta, rf, gamma_in, slots1,
          gamma2, w_slot2, w1, b1, w2, b2, out):
    rank_d = nc.dram_tensor("rank_d", (NB, S), F32).ap()
    enc_d = nc.dram_tensor("enc_d", (NB, P, NT, HX), F32).ap()
    encT_d = nc.dram_tensor("encT_d", (NB, F + 1, S), F32).ap()
    h2_d = nc.dram_tensor("h2_d", (NB, P, NT, D + 1), F32).ap()
    combT_d = nc.dram_tensor("combT_d", (NB, P, S), F32).ap()
    yn_d = nc.dram_tensor("yn_d", (NB // 2, NE, NS, 2, GQ, D), F32).ap()
    o2_d = nc.dram_tensor("o2_d", (NB // 2, NE, NS, 2, GQ, D), F32).ap()

    ctx = ExitStack()
    with ctx:
        def sem(name):
            return ctx.enter_context(nc.semaphore(name))

        def sb(name, shape, dt=F32, c=ctx):
            return c.enter_context(nc.sbuf_tensor(name, shape, dt))

        cst = sb("cst", [P, C_END])
        half = sb("half", [P, 8])
        ident = cst[:, C_ID:C_ID + P]
        bank = [ctx.enter_context(nc.psum_tensor(f"bank{i}", [P, 512], F32)) for i in range(8)]
        with ExitStack() as cw:
            wv = [sb(f"wv{i}", [F + 1, D], c=cw) for i in range(2)]
            wqk = [sb(f"wqk{i}", [F + 1, 2 * NC_, 2, HC * DH], c=cw) for i in range(2)]
            rfa = sb("rfa", [P, HC, M], c=cw)
            wp = [sb("wp0", [F, D], c=cw), sb("wp1", [F + 1, D], c=cw)]
            phiT = sb("phiT", [F, 2, P], c=cw)
            gam = sb("gam", [P, D], c=cw)
            bet = sb("bet", [P, D], c=cw)
            gin = sb("gin", [P, D], c=cw)
            g2r = sb("g2r", [P, D], c=cw)
            with ExitStack() as c0:
                encode(nc, c0, sem, lambda n, s, dt=F32: sb(n, s, dt, c0), bank, locals())
            with ExitStack() as c1:
                attend(nc, c1, sem, lambda n, s, dt=F32: sb(n, s, dt, c1), bank, locals())
        with ExitStack() as c2:
            experts(nc, c2, sem, lambda n, s, dt=F32: sb(n, s, dt, c2), bank, locals())
        with ExitStack() as c3:
            combine(nc, c3, sem, lambda n, s, dt=F32: sb(n, s, dt, c3), bank, locals())


def encode(nc, ctx, sem, sb, bank, g):
    cst, ident, half = g["cst"], g["ident"], g["half"]
    wv, wqk, rfa, wp, phiT = g["wv"], g["wqk"], g["rfa"], g["wp"], g["phiT"]
    xi = sb("xi", [NB, S], I32)
    row = sb("row", [NB, 2, S])
    xf = sb("xf", [NB, S])
    keep = sb("keep", [NB, S])
    tmp = sb("tmp", [NB, S])
    one = sb("one", [NB, S])
    cum = sb("cum", [NB, 3, S])
    perm = sb("perm", [NB, 3, S])
    small = sb("small", [NB, 4])
    tabs = sb("tabs", [P, 3, NB * NT])
    wraw = [sb(f"wraw{i}", [F, 3 * D]) for i in range(2)]
    ones = sb("ones", [F, F + 1])
    rfn = sb("rfn", [M, DH])
    rfr = sb("rfr", [M, HC, DH])
    sl = sb("sl", [P, D])
    sq1 = sb("sq1", [P, D])
    phn = sb("phn", [P, D])
    r1 = sb("r1", [P, 4])
    cb = sb("cb", [P, CB, S])
    kk = sb("kk", [P, 3, CT])
    kp = sb("kept", [P, CT])
    junk = sb("junk", [P, CT, S])
    cnt = sb("cnt", [P, CT])
    psc = sb("psc", [P, CT])
    ang = sb("ang", [P, CT, F])
    nr = sb("nr", [P, CT, F])
    nr2 = sb("nr2", [P, CT, F])
    rd = sb("rd", [P, CT, F])
    rd2 = sb("rd2", [P, CT, F])
    rd3 = sb("rd3", [P, CT, F])
    sn = sb("sn", [P, CT, F])
    he = sb("he", [P, CT, HX])
    hsq = sb("hsq", [P, CT, F])
    st = sb("st", [P, 8, CT])
    et = sb("et", [P, CT, F + 1])
    etT = sb("etT", [F + 1, CB, 2, P])

    s_x, s_c, s_w, s_half = sem("p0_x"), sem("p0_const"), sem("p0_weights"), sem("p0_half")
    s_cum, s_rank_d = sem("p0_ranks"), sem("p0_rank_stored")
    s_pe = sem("p0_products")
    s_ones, s_rfr = sem("p0_ones"), sem("p0_rfr")
    s_ssq, s_pw, s_phn = sem("p0_ssq"), sem("p0_pow"), sem("p0_phn")
    chain = sem("p0_dve_chain")
    s_cb, s_pos, s_ang0, s_ang = sem("enc_cb"), sem("enc_position"), sem("enc_angle0"), sem("enc_angle")
    DT = CT // 2
    s_red, s_sin_in, s_sin = sem("enc_reduce"), sem("enc_reduced"), sem("enc_sin")
    s_he, s_hsq = sem("enc_he"), sem("enc_squares")
    s_var, s_ve, s_rs, s_mr = sem("enc_var"), sem("enc_ve"), sem("enc_rstd"), sem("enc_mr")
    s_et, s_etT_mm, s_etT = sem("enc_et"), sem("enc_etT_mm"), sem("enc_etT")
    s_std, s_stdT = sem("enc_stored"), sem("encT_stored")
    block = ctx.enter_context(nc.Block())

    @block.sync
    def _(sp):
        sp.dma_start(xi[:, :], g["x"]).then_inc(s_x, 16)
        sp.dma_start(row[:, :, :], g["rows"]).then_inc(s_x, 16)
        sp.dma_start(small[:, 0:1], g["tok_scale"].partition_broadcast(NB)).then_inc(s_x, 16)
        sp.dma_start(cst[:, :], g["consts"]).then_inc(s_c, 16)
        sp.wait_ge(s_cum, 1)
        sp.dma_start(g["rank_d"], cum[:, 0, :]).then_inc(s_rank_d, 16)
        sp.wait_ge(s_rank_d, 16)

        def head(i):
            if exists(3 * i - 2):
                sp.wait_ge(s_pos, 1)
                sp.wait_ge(s_pos, 3 * i - 1)
            sp.dma_start(cb[:, :, :], g["rank_d"][bass.ts(i, CB), :].partition_broadcast(P)).then_inc(s_cb, 16)

        def tail(i):
            sp.wait_ge(s_mr, 1)
            sp.wait_ge(s_mr, i + 1)
            sp.dma_start(g["enc_d"].rearrange("(n c) p t f -> n p c t f", c=CB)[i],
                         he[:, :, :].rearrange("p (c t) f -> p c t f", t=NT)).then_inc(s_std, 16)
            sp.wait_ge(s_etT, 1)
            sp.wait_ge(s_etT, i + 1)
            sp.dma_start(g["encT_d"].rearrange("(n c) p s -> n p c s", c=CB)[i],
                         etT[:, :, :, :].rearrange("p c r s -> p c (r s)")).then_inc(s_stdT, 16)

        n = NB // CB
        head(0)
        for i in range(2):
            sp.dma_start(wraw[i][:, :], g["W_qkv"][i * F:(i + 1) * F, :]).then_inc(s_w, 16)
            sp.dma_start(wp[i][0:F, :], g["W_proj"][i * F:(i + 1) * F, :]).then_inc(s_w, 16)
        sp.dma_start(wp[1][F:F + 1, :], g["b_proj"].unsqueeze(0)).then_inc(s_w, 16)
        sp.dma_start(rfn[:, :], g["rf"]).then_inc(s_w, 16)
        sp.dma_start(sl[:, :], g["slots1"].rearrange("e s d -> (e s) d")).then_inc(s_w, 16)
        for dst, src in ((g["gam"], "gamma"), (g["bet"], "beta"), (g["gin"], "gamma_in")):
            sp.dma_start(dst[:, :], g[src].partition_broadcast(P)).then_inc(s_w, 16)
        for e in range(NE):
            sp.dma_start(g["g2r"][e * NS:(e + 1) * NS, :],
                         g["gamma2"][e].partition_broadcast(NS)).then_inc(s_w, 16)
        head(1)
        with sp.Fori(2, n, 1) as i:
            head(i)
            tail(i - 2)
        tail(n - 2)
        tail(n - 1)
        sp.wait_ge(s_std, 16 * (NB // CB))
        sp.wait_ge(s_stdT, 16 * (NB // CB))

    @block.vector
    def _(dve):
        v = nc.vector
        links = [0]

        def link(ins):
            links[0] += 1
            ins.then_inc(chain, 1)
            dve.wait_ge(chain, links[0])

        v.memset(half[:, :], -0.5).then_inc(s_half, 1)
        v.memset(one[:, :], 1.0)
        v.memset(ones[:, :], 1.0).then_inc(s_ones, 1)
        dve.wait_ge(s_x, 48)
        link(v.tensor_copy(xf[:, :], xi[:, :]))
        link(v.tensor_scalar(tmp[:, :], xf[:, :], 0.0, None, ALU.not_equal))
        link(v.scalar_tensor_tensor(keep[:, :], xf[:, :], 1.0, tmp[:, :], ALU.not_equal, ALU.mult))
        link(v.scalar_tensor_tensor(tmp[:, :], xf[:, :], 2.0, keep[:, :], ALU.not_equal, ALU.mult))
        link(v.tensor_tensor(xf[:, :], tmp[:, :], row[:, 0, :], ALU.mult))
        link(v.reduce_max(small[:, 1:2], xf[:, :], AX.X))
        link(v.tensor_scalar(small[:, 2:3], small[:, 1:2], -1.0, 1e-6, ALU.add, ALU.add))
        link(v.reciprocal(small[:, 3:4], small[:, 2:3]))
        link(v.tensor_tensor(small[:, 1:2], small[:, 3:4], small[:, 0:1], ALU.mult))
        link(v.tensor_tensor(keep[:, :], tmp[:, :], row[:, 1, :], ALU.mult))
        link(v.tensor_tensor(xf[:, :], tmp[:, :], keep[:, :], ALU.subtract))
        v.tensor_tensor_scan(cum[:, 0, :], one[:, :], tmp[:, :], 0.0, ALU.mult, ALU.add).then_inc(s_cum, 1)
        v.tensor_tensor_scan(cum[:, 1, :], one[:, :], keep[:, :], 0.0, ALU.mult, ALU.add)
        link(v.tensor_tensor_scan(cum[:, 2, :], one[:, :], xf[:, :], 0.0, ALU.mult, ALU.add))
        for r in range(2):
            v.tensor_copy(perm[:, 0, :].rearrange("b (j r) -> b r j", r=2)[:, r, :],
                          cum[:, 1 + r, :].rearrange("b (j r) -> b r j", r=2)[:, r, :])
        v.tensor_copy(perm[:, 1, :], tmp[:, :])
        link(v.tensor_scalar(perm[:, 2, :], one[:, :], small[:, 1:2], None, ALU.mult))
        dve.wait_ge(s_pe, 1)
        v.tensor_copy(tabs[:, :, :].rearrange("p a (b t) -> p a t b", t=NT)[:, :, 0, :],
                      bank[0][:, 0:3 * NT * NB].rearrange("p (a t b) -> p a t b", a=3, t=NT)[:, :, 0, :])
        link(v.tensor_copy(tabs[:, :, :].rearrange("p a (b t) -> p a t b", t=NT)[:, :, 1, :],
                           bank[0][:, 0:3 * NT * NB].rearrange("p (a t b) -> p a t b", a=3, t=NT)[:, :, 1, :]))
        def step(i, tail):
            if exists(3 * i - 2):
                dve.wait_ge(s_pos, 3 * i - 1)
            if exists(3 * i - 1):
                dve.wait_ge(s_pos, 3 * i)
            v.tensor_scalar(kk[:, :, :], tabs[:, :, bass.ts(i, CT)], 1.0, None, ALU.mult).then_inc(s_pos, 1)
            dve.wait_ge(s_pos, 3 * i + 1)
            dve.wait_ge(s_cb, 16 * i + 16)
            for t in range(CT):
                ins = v.tensor_scalar(junk[:, t, :], cb[:, t // NT, :], kk[:, 0, t:t + 1], 0.0, ALU.is_lt, ALU.add,
                                      accum_out=cnt[:, t:t + 1])
            ins.then_inc(s_pos, 1)
            dve.wait_ge(s_pos, 3 * i + 2)
            if exists(i - 1):
                dve.wait_ge(s_ang, i)
            v.tensor_tensor(psc[:, :], cnt[:, :], kk[:, 2, :], ALU.mult).then_inc(s_pos, 1)
            dve.wait_ge(s_pos, 3 * i + 3)
            if exists(5 * i - 2):
                dve.wait_ge(s_red, 5 * i - 1)
            for t in range(DT):
                ins = v.tensor_scalar(ang[:, t, :], cst[:, C_INV:C_INV + F], psc[:, t:t + 1],
                                      cst[:, C_QUART:C_QUART + 1], ALU.mult, ALU.add)
            ins.then_inc(s_ang0, 1)
            if tail:
                stats(i - 1)
            if exists(i - 1):
                dve.wait_ge(s_he, i)
            v.tensor_scalar(kp[:, :], kk[:, 1, :], 1.0, None, ALU.mult).then_inc(s_red, 1)
            dve.wait_ge(s_ang0, i + 1)
            dve.wait_ge(s_ang, i + 1)
            v.tensor_scalar(nr[:, :, :], ang[:, :, :], float(1.0 / TWO_PI), ROUND, ALU.mult, ALU.add).then_inc(s_red, 1)
            dve.wait_ge(s_red, 5 * i + 2)
            v.tensor_scalar(nr2[:, :, :], nr[:, :, :], -ROUND, None, ALU.add).then_inc(s_red, 1)
            dve.wait_ge(s_red, 5 * i + 3)
            v.scalar_tensor_tensor(rd[:, :, :], nr2[:, :, :], -PI_HI, ang[:, :, :], ALU.mult, ALU.add).then_inc(s_red, 1)
            dve.wait_ge(s_red, 5 * i + 4)
            v.scalar_tensor_tensor(rd2[:, :, :], nr2[:, :, :], -PI_LO, rd[:, :, :], ALU.mult, ALU.add).then_inc(s_red, 1)
            dve.wait_ge(s_red, 5 * i + 5)
            if exists(i - 1):
                dve.wait_ge(s_sin, i)
            v.tensor_scalar(rd3[:, :, :], rd2[:, :, :], PI_MAX, -PI_MAX, ALU.min, ALU.max).then_inc(s_sin_in, 1)

        def stats(i):
            dve.wait_ge(s_he, i + 1)
            v.reduce_sum(st[:, 0, :], he[:, :, 0:F], AX.X).then_inc(s_var, 1)
            dve.wait_ge(s_var, 4 * i + 1)
            if exists(i - 1):
                dve.wait_ge(s_mr, i)
            v.tensor_scalar(st[:, 2, :], st[:, 0, :], -1.0 / D, None, ALU.mult).then_inc(s_var, 1)
            dve.wait_ge(s_var, 4 * i + 2)
            v.tensor_tensor(st[:, 3, :], st[:, 2, :], st[:, 2, :], ALU.mult).then_inc(s_var, 1)
            dve.wait_ge(s_var, 4 * i + 3)
            dve.wait_ge(s_hsq, i + 1)
            v.scalar_tensor_tensor(st[:, 4, :], st[:, 1, :], 1.0 / D, st[:, 3, :], ALU.mult,
                                   ALU.subtract).then_inc(s_var, 1)
            dve.wait_ge(s_var, 4 * i + 4)
            if exists(i - 1):
                dve.wait_ge(s_rs, i)
            v.tensor_scalar(st[:, 5, :], st[:, 4, :], 1e-5, None, ALU.add).then_inc(s_ve, 1)

        step(0, False)
        step(1, True)
        with dve.Fori(2, NB // CB, 1) as i:
            step(i, True)
        stats(NB // CB - 1)

        v.memset(r1[:, :], 0.0)
        dve.wait_ge(s_w, 16 * 18)
        dve.wait_ge(s_c, 16)
        for i in range(2):
            v.tensor_copy(wv[i][0:F, :], wraw[i][:, 2 * D:3 * D])
            for r in range(2):
                v.tensor_copy(wqk[i][0:F, :, r, :], wraw[i][:, 0:2 * D].rearrange("p (c n) -> p c n", c=2 * NC_))
        dve.wait_ge(s_pe, 2)
        for i in range(2):
            v.tensor_copy(wv[i][F:F + 1, :], bank[2][F:F + 1, 0:D])
            for r in range(2):
                v.tensor_copy(wqk[i][F:F + 1, :, r, :],
                              bank[1][F:F + 1, 0:2 * D].rearrange("p (c n) -> p c n", c=2 * NC_))
        v.tensor_copy(rfr[:, :, :], rfn[:, :].unsqueeze(1).to_broadcast([M, HC, DH])).then_inc(s_rfr, 1)
        dve.wait_ge(s_pe, 3)
        v.tensor_tensor(rfa[0:64, :, :], bank[3][0:64, 0:M].unsqueeze(1).to_broadcast([64, HC, M]),
                        cst[0:64, C_MRF:C_MRF + HC * M].rearrange("p (h m) -> p h m", h=HC), ALU.mult)
        v.tensor_copy(rfa[64:128, :, :], cst[64:128, C_MRF:C_MRF + HC * M].rearrange("p (h m) -> p h m", h=HC))
        link(v.tensor_tensor(sq1[:, :], sl[:, :], sl[:, :], ALU.mult))
        link(v.reduce_sum(r1[:, 0:1], sq1[:, :], AX.X))
        v.tensor_scalar(r1[:, 1:2], r1[:, 0:1], 1.0 / D, 1e-6 / D, ALU.mult, ALU.add).then_inc(s_ssq, 1)
        dve.wait_ge(s_pw, 1)
        v.tensor_scalar(phn[:, :], sl[:, :], r1[:, 2:3], None, ALU.mult).then_inc(s_phn, 1)
        dve.wait_ge(s_pe, 4)
        v.tensor_copy(phiT[:, :, :], bank[4][0:F, 0:2 * P].rearrange("p (c n) -> p c n", c=2))

    @block.scalar
    def _(act):
        def squares(i):
            act.wait_ge(s_he, i + 1)
            if exists(i - 1):
                act.wait_ge(s_ve, i)
            for t in range(CT):
                ins = nc.scalar.activation(hsq[:, t, :], he[:, t, 0:F], ACT.Square, accum_out=st[:, 1, t:t + 1])
            ins.then_inc(s_hsq, 1)

        def angles(i):
            act.wait_ge(s_pos, 3 * i + 3)
            if exists(5 * i - 2):
                act.wait_ge(s_red, 5 * i - 1)
            for t in range(DT, CT):
                ins = nc.scalar.activation(ang[:, t, :], cst[:, C_INV:C_INV + F], ACT.Identity,
                                           bias=cst[:, C_QUART:C_QUART + 1], scale=psc[:, t:t + 1])
            ins.then_inc(s_ang, 1)

        def sines(i):
            act.wait_ge(s_sin_in, i + 1)
            if exists(i - 1):
                act.wait_ge(s_he, i)
            nc.scalar.activation(sn[:, :, :], rd3[:, :, :], ACT.Sin).then_inc(s_sin, 1)

        def turned(i):
            act.wait_ge(s_etT_mm, i + 1)
            if exists(i - 1):
                act.wait_ge(s_stdT, i * 16)
            for h in range(2):
                ins = nc.scalar.activation(etT[:, 2 * h:2 * h + 2, :, :],
                                           bank[5 + h][0:F + 1, :].rearrange("p (c j r) -> p c r j", c=2, r=2), ACT.Copy)
            ins.then_inc(s_etT, 1)

        def step(i):
            squares(i - 1)
            angles(i)
            sines(i)
            turned(i - 1)

        act.wait_ge(s_c, 16)
        angles(0)
        sines(0)
        step(1)
        with act.Fori(2, NB // CB, 1) as i:
            step(i)
        squares(NB // CB - 1)
        turned(NB // CB - 1)

    @block.gpsimd
    def _(pool):
        p = nc.gpsimd
        pool.wait_ge(s_half, 1)

        def kept(i):
            pool.wait_ge(s_red, 5 * i + 1)
            pool.wait_ge(s_sin, i + 1)
            if exists(i - 1):
                pool.wait_ge(s_std, i * 16)
            if exists(i - 1):
                pool.wait_ge(s_et, i)
            p.tensor_tensor(he[:, :, 0:F], sn[:, :, :], kp[:, :].unsqueeze(2).to_broadcast([P, CT, F]),
                            ALU.mult).then_inc(s_he, 1)

        def scaled(i):
            pool.wait_ge(s_ve, i + 1)
            p.tensor_tensor(he[:, :, F], st[:, 5, :], half[:, 0:CT], ALU.pow).then_inc(s_rs, 1)
            pool.wait_ge(s_rs, i + 1)
            p.tensor_tensor(he[:, :, F + 1], st[:, 2, :], he[:, :, F], ALU.mult).then_inc(s_mr, 1)
            pool.wait_ge(s_mr, i + 1)
            if exists(i - 1):
                pool.wait_ge(s_etT_mm, i)
            p.tensor_tensor(et[:, :, 0:F], he[:, :, 0:F], he[:, :, F:F + 1].to_broadcast([P, CT, F]), ALU.mult)
            p.tensor_tensor(et[:, :, F], st[:, 2, :], he[:, :, F], ALU.mult).then_inc(s_et, 1)

        def step(i):
            scaled(i - 1)
            kept(i)

        kept(0)
        step(1)
        with pool.Fori(2, NB // CB, 1) as i:
            step(i)
        scaled(NB // CB - 1)
        pool.wait_ge(s_ssq, 1)
        p.tensor_tensor(r1[:, 2:3], r1[:, 1:2], half[:, 0:1], ALU.pow).then_inc(s_pw, 1)

    @block.tensor
    def _(pe):
        pe.wait_ge(s_c, 16)
        pe.wait_ge(chain, 13)
        for a in range(3):
            for t in range(NT):
                ins = nc.tensor.transpose(bank[0][:, (a * NT + t) * NB:(a * NT + t + 1) * NB],
                                          perm[:, a, t * P:(t + 1) * P], ident[0:NB, 0:NB])
        ins.then_inc(s_pe, 1)
        pe.wait_ge(s_ones, 1)
        pe.wait_ge(s_w, 16 * 18)
        for i in range(2):
            nc.tensor.matmul(bank[1][0:F + 1, 0:2 * D], ones[:, :], wraw[i][:, 0:2 * D], start=i == 0, stop=i == 1)
        for i in range(2):
            ins = nc.tensor.matmul(bank[2][0:F + 1, 0:D], ones[:, :], wraw[i][:, 2 * D:3 * D], start=i == 0, stop=i == 1)
        ins.then_inc(s_pe, 1)
        def chunk(i):
            pe.wait_ge(s_et, i + 1)
            if exists(i - 1):
                pe.wait_ge(s_etT, i)
            for t in range(CT):
                ins = nc.tensor.transpose(bank[5 + t // 4][0:F + 1, (t % 4) * P:(t % 4 + 1) * P], et[:, t, :], ident)
            ins.then_inc(s_etT_mm, 1)

        chunk(0)
        with pe.Fori(1, NB // CB, 1) as i:
            chunk(i)
        pe.wait_ge(s_rfr, 1)
        nc.tensor.transpose(bank[3][0:64, 0:M], rfr[:, :, :].rearrange("p h d -> p (h d)"),
                            ident[0:M, 0:M]).then_inc(s_pe, 1)
        pe.wait_ge(s_phn, 1)
        for c in range(2):
            ins = nc.tensor.transpose(bank[4][0:F, c * P:(c + 1) * P], phn[:, c * F:(c + 1) * F], ident)
        ins.then_inc(s_pe, 1)


def attend(nc, ctx, sem, sb, bank, g):
    cst, ident, half = g["cst"], g["ident"], g["half"]
    wv, wqk, rfa, wp, phiT = g["wv"], g["wqk"], g["rfa"], g["wp"], g["phiT"]
    gam, bet, gin, g2r = g["gam"], g["bet"], g["gin"], g["g2r"]
    two = range(2)
    encT = [sb(f"encT{i}", [F + 1, S]) for i in two]
    enc = [sb(f"enc{i}", [P, NT, HX]) for i in two]
    qh = [sb(f"qh{c}", [P, 2 * S], F32R) for c in range(NC_)]
    ql = [sb(f"ql{c}", [P, 2 * S], F32R) for c in range(NC_)]
    sqf = [sb(f"sqf{c}", [P, 2 * S]) for c in range(NC_)]
    rfh = sb("rfh", [P, HC * M], F32R)
    rfl = sb("rfl", [HC * DH, HC * M], F32R)
    kp = [sb(f"kp{c}", [P, 2, HC * M]) for c in range(NC_)]
    qp = [sb(f"qp{c}", [P, 2, S]) for c in range(NC_)]
    va = [sb(f"va{i}", [P, 2, H, DH + 1]) for i in two]
    kvb = sb("kvb", [P, H // 2, 2, DH + 1])
    den = sb("den", [P, NT * H])
    rden = sb("rden", [P, NT * H])
    xa = sb("xa", [P, NT, D])
    xaT = [sb("xaT0", [F, S]), sb("xaT1", [F + 1, S])]
    hh = [sb(f"hh{i}", [P, NT, D]) for i in two]
    hb = [sb(f"hb{i}", [P, NT, D]) for i in two]
    xs = sb("xs", [P, NT, D])
    xh = [sb(f"xh{i}", [P, NT, D]) for i in two]
    y = sb("y", [P, NT, D])
    bs = sb("bs", [P, NT, 6])
    mv = sb("mv", [P, NT, 2])
    ve = sb("ve", [P, NT])
    rs = sb("rs", [P, NT])
    yg = sb("yg", [P, NT, D])
    h2 = [sb(f"h2{i}", [P, NT, D + 1]) for i in two]
    bs2 = sb("bs2", [P, NT, 6])
    mv2 = sb("mv2", [P, NT, 2])
    ve2 = sb("ve2", [P, NT])
    f2 = sb("f2", [P, NT])
    xc = sb("xc", [P, NT, D])
    xn = [sb(f"xn{i}", [P, NT, D]) for i in two]
    xnT = sb("xnT", [F, 2, S])
    mx = sb("mx", [P, NT + GQ])
    nm = sb("nm", [P, NT + GQ])
    lgs = sb("lgs", [P, NT, P])
    ec = sb("ec", [P, NT, P])
    ed = sb("ed", [P, GQ, 64])
    zd = sb("zd", [P, GQ])
    cT = [sb(f"cT{i}", [P, S]) for i in two]
    dT = sb("dT", [P, NT, P])
    sqj = sb("sqj", [P, GQ, D])
    ssq = sb("ssq", [P, GQ])
    zs = sb("zs", [P, GQ])
    sse = sb("sse", [P, GQ])
    sr = sb("sr", [P, GQ])
    yn = [sb(f"yn{i}", [P, GQ, D]) for i in two]

    s_ld = [sem(f"loaded{i}") for i in two]
    s_init = sem("at_init")
    sq_lo = sem("sq_lo")
    qk_mm, qk_copy, qk_sq = sem("qk_mm"), sem("qk_copy"), sem("qk_sq")
    f_mm, f_exp = sem("feat_mm"), sem("feat_exp")
    v_mm, v_ev, kv_mm, kv_ev = sem("v_mm"), sem("v_ev"), sem("kv_mm"), sem("kv_ev")
    o_mm, o_den, o_rcp, o_ev = sem("o_mm"), sem("o_den"), sem("o_rcp"), sem("o_ev")
    xaT_mm, xaT_ev, pj_mm = sem("xaT_mm"), sem("xaT_ev"), sem("pj_mm")
    prep, prep1, prep2 = sem("prep"), sem("prep1"), sem("prep2")
    y_ev, y_bs, y_mv, y_ve, y_rs, y_g, y_h2 = (sem(n) for n in ("y_ev", "y_bs", "y_mv", "y_ve", "y_rs", "y_g", "y_h2"))
    h_bs, h_mv, h_ve, h_f, h_xc, h_xn = (sem(n) for n in ("h_bs", "h_mv", "h_ve", "h_f", "h_xc", "h_xn"))
    xnT_mm, xnT_ev, lg_mm, lg_mx, lg_nm = (sem(n) for n in ("xnT_mm", "xnT_ev", "lg_mm", "lg_mx", "lg_nm"))
    lg_cp, lgT_mm = sem("lg_copied"), sem("lgT_mm")
    e_c, e_d, cd_mm, c_ev, d_ev = (sem(n) for n in ("e_c", "e_d", "cd_mm", "c_ev", "d_ev"))
    sl_mm, sl_sq, sl_z, sl_e, sl_r, sl_y = (sem(n) for n in ("sl_mm", "sl_sq", "sl_z", "sl_e", "sl_r", "sl_y"))
    s_h2 = [sem(f"h2_stored{i}") for i in two]
    s_yn = [sem(f"yn_stored{i}") for i in two]
    block = ctx.enter_context(nc.Block())
    b_qk, b_ft = bank[0:2], bank[2:4]
    b_v, b_o, b_x, b_s = bank[4], bank[5], bank[6], bank[7]

    def pipeline(eng, iteration, last):
        def go(a, u):
            n = 2 * a + u
            if isinstance(n, int):
                iteration(a, u, n, [0 <= n - k < NB for k in range(last + 1)])
            else:
                iteration(a, u, n, [True] * (last + 1))
        for n in range(6):
            go(n // 2, n % 2)
        with eng.Fori(3, NB // 2, 1) as a:
            for u in two:
                go(a, u)
        for n in range(NB, NB + last):
            go(n // 2, n % 2)

    @block.sync
    def _(sp):
        def iteration(a, u, n, step):
            if step[0]:
                if exists(n - 2):
                    sp.wait_ge(v_mm, 1)
                    sp.wait_ge(v_mm, n - 1)
                if exists(n - 2):
                    sp.wait_ge(prep2, 1)
                    sp.wait_ge(prep2, n - 1)
                sp.dma_start(encT[u][:, :], g["encT_d"][n]).then_inc(s_ld[u], 16)
                sp.dma_start(enc[u][:, :, :], g["enc_d"][n]).then_inc(s_ld[u], 16)
            if step[3]:
                l, v = n - 3, 1 - u
                sp.wait_ge(e_c, 1)
                sp.wait_ge(e_c, l + 1)
                sp.dma_start(g["h2_d"][l], h2[v][:, :, :]).then_inc(s_h2[v], 16)
                sp.wait_ge(c_ev, 1)
                sp.wait_ge(c_ev, l + 1)
                sp.dma_start(g["combT_d"][l], cT[v][:, :]).then_inc(s_h2[v], 16)
                sp.wait_ge(sl_y, 1)
                sp.wait_ge(sl_y, l + 1)
                sp.dma_start(g["yn_d"].rearrange("t e s b q d -> t b (e s) q d")[a - 1 if u else a - 2, v], yn[v][:, :, :]).then_inc(s_yn[v], 16)

        pipeline(sp, iteration, 3)
        for u in two:
            sp.wait_ge(s_h2[u], 32 * NB // 2)
            sp.wait_ge(s_yn[u], 16 * NB // 2)

    @block.tensor
    def _(pe):
        mm, tr = nc.tensor.matmul, nc.tensor.transpose
        pe.wait_ge(s_init, 4)

        def iteration(a, u, n, step):
            m, l = n - 1, n - 2
            eT = encT[u][:, :].rearrange("p (r s) -> p r s", r=2)

            def QK(c):
                if c == 0:
                    pe.wait_ge(s_ld[u], (a + 1) * 32)
                if exists(2 * (NC_ * n + c - 2) + 1):
                    pe.wait_ge(qk_copy, 2 * (NC_ * n + c - 2) + 2)
                if exists(2 * (NC_ * n + c - 2)):
                    pe.wait_ge(qk_sq, 2 * (NC_ * n + c - 2) + 1)
                b = b_qk[(u + c) % 2]
                for r in two:
                    mm(b[:, 0:S].rearrange("p (j r) -> p r j", r=2)[:, r, :],
                       wqk[r][:, c, :, :].rearrange("p a n -> p (a n)"), eT[:, r, :], start=True, stop=True)
                for r in two:
                    ins = mm(b[:, S + r * P:S + (r + 1) * P],
                             wqk[r][:, NC_ + c, :, :].rearrange("p a n -> p (a n)"), eT[:, r, :], start=True, stop=True)
                ins.then_inc(qk_mm, 1)

            def V():
                if exists(l - 1):
                    pe.wait_ge(sl_y, l)
                for r in two:
                    ins = mm(b_v[:, r * D:(r + 1) * D], eT[:, r, :], wv[r][:, :], start=True, stop=True)
                ins.then_inc(v_mm, 1)

            def FEAT(s):
                if exists(2 * NC_ * n + s - 2):
                    pe.wait_ge(f_exp, 2 * NC_ * n + s - 1)
                c, b = s % NC_, b_ft[s % 2]
                if s < NC_:
                    pe.wait_ge(qk_copy, 2 * (NC_ * n + c) + 2)
                    pe.wait_ge(sq_lo, NC_ * n + c + 1)
                K = HC * DH
                for r in two:
                    out = b[:, r * 256:(r + 1) * 256]
                    if s < NC_:
                        cols = slice(S + r * P, S + (r + 1) * P)
                        mm(out, qh[c][:, cols], rfh[:, :], start=True, stop=False)
                        mm(out, ql[c][:, cols], rfh[:, :], start=False, stop=False)
                        ins = mm(out, qh[c][0:K, cols], rfl[:, :], start=False, stop=True)
                    else:
                        cols = slice(r * P, (r + 1) * P)
                        mm(out, rfh[:, cols], qh[c][:, 0:S], start=True, stop=False)
                        mm(out, rfh[:, cols], ql[c][:, 0:S], start=False, stop=False)
                        ins = mm(out, rfl[:, cols], qh[c][0:K, 0:S], start=False, stop=True)
                ins.then_inc(f_mm, 1)

            def KV():
                pe.wait_ge(f_exp, 2 * NC_ * n + NC_)
                pe.wait_ge(v_ev, n + 1)
                for p in range(H // 2):
                    for r in two:
                        ins = mm(b_v[:, 34 * p:34 * p + 34], kp[p // 2][:, r, (p % 2) * P:(p % 2 + 1) * P],
                                 va[u][:, r, 2 * p:2 * p + 2, :].rearrange("p h d -> p (h d)"),
                                 start=r == 0, stop=r == 1)
                ins.then_inc(kv_mm, 1)

            def OUT():
                pe.wait_ge(kv_ev, m + 1)
                pe.wait_ge(f_exp, 2 * NC_ * m + 2 * NC_)
                if exists(m - 1):
                    pe.wait_ge(y_ev, m)
                for t in two:
                    for p in range(H // 2):
                        ins = mm(b_o[:, t * 204 + 34 * p:t * 204 + 34 * p + 34], qp[p // 2][:, p % 2, t * P:(t + 1) * P],
                                 kvb[:, p, :, :].rearrange("p h d -> p (h d)"), start=True, stop=True)
                ins.then_inc(o_mm, 1)

            def XAT():
                pe.wait_ge(o_ev, m + 1)
                for c in two:
                    for t in two:
                        ins = tr(b_o[0:F, (2 * c + t) * P:(2 * c + t + 1) * P], xa[:, t, c * F:(c + 1) * F], ident)
                ins.then_inc(xaT_mm, 1)

            def PROJ():
                pe.wait_ge(xaT_ev, m + 1)
                for t in two:
                    for c in two:
                        ins = mm(b_o[:, t * D:(t + 1) * D], xaT[c][:, t * P:(t + 1) * P], wp[c][:, :],
                                 start=c == 0, stop=c == 1)
                ins.then_inc(pj_mm, 1)

            def XNT():
                pe.wait_ge(h_xn, l + 1)
                if exists(l - 1):
                    pe.wait_ge(c_ev, l)
                if exists(l - 1):
                    pe.wait_ge(d_ev, l)
                for c in two:
                    for t in two:
                        ins = tr(b_x[0:F, (2 * c + t) * P:(2 * c + t + 1) * P], xn[u][:, t, c * F:(c + 1) * F], ident)
                ins.then_inc(xnT_mm, 1)

            def LOG():
                pe.wait_ge(xnT_ev, l + 1)
                for t in two:
                    for c in two:
                        ins = mm(b_x[:, t * P:(t + 1) * P], xnT[:, c, t * P:(t + 1) * P], phiT[:, c, :],
                                 start=c == 0, stop=c == 1)
                ins.then_inc(lg_mm, 1)

            def LGT():
                pe.wait_ge(lg_cp, l + 1)
                for t in two:
                    ins = tr(b_x[:, S + t * P:S + (t + 1) * P], lgs[:, t, :], ident)
                ins.then_inc(lgT_mm, 1)

            def CDT():
                pe.wait_ge(e_c, l + 1)
                pe.wait_ge(e_d, l + 1)
                for t in two:
                    tr(b_x[:, t * P:(t + 1) * P], ec[:, t, :], ident)
                for t in two:
                    ins = tr(b_x[:, S + t * P:S + (t + 1) * P], ed[:, 2 * t:2 * t + 2, :].rearrange("p q s -> p (q s)"), ident)
                ins.then_inc(cd_mm, 1)

            def SLOTS():
                pe.wait_ge(d_ev, l + 1)
                if exists(l - 1):
                    pe.wait_ge(sl_y, l)
                for t in two:
                    for q, b in ((0, b_s), (1, b_v)):
                        ins = mm(b[:, t * D:(t + 1) * D], dT[64 * q:64 * q + 64, t, :], xn[u][64 * q:64 * q + 64, t, :],
                                 start=True, stop=True)
                ins.then_inc(sl_mm, 1)

            A, B, C = step
            if A:
                QK(0)
            if B:
                OUT()
            if A:
                QK(1)
            if C:
                XNT()
            if A:
                QK(2)
                FEAT(0)
            if C:
                LOG()
            if B:
                XAT()
            if C:
                LGT()
            if A:
                V()
                FEAT(1)
                FEAT(2)
                FEAT(3)
            if B:
                PROJ()
            if A:
                KV()
                FEAT(4)
            if C:
                CDT()
            if A:
                FEAT(5)
            if C:
                if A:
                    pe.wait_ge(kv_ev, n + 1)
                SLOTS()

        pipeline(pe, iteration, 2)

    @block.vector
    def _(dve):
        v = nc.vector
        for i in two:
            v.memset(va[i][:, :, :, :], 1.0)
        v.memset(kvb[:, :, :, :], 0.0).then_inc(s_init, 1)
        v.memset(xaT[1][F:F + 1, :], 1.0).then_inc(s_init, 1)
        K = HC * DH
        v.tensor_copy(rfh[:, :], rfa[:, :, :].rearrange("p h m -> p (h m)")).then_inc(s_init, 1)
        dve.wait_ge(s_init, 3)
        v.tensor_tensor(rfl[:, :], rfa[0:K, :, :].rearrange("p h m -> p (h m)"), rfh[0:K, :].bitcast(F32),
                        ALU.subtract).then_inc(s_init, 1)

        def iteration(a, u, n, step):
            m, l, w = n - 1, n - 2, 1 - u

            def qk_copy_(c):
                dve.wait_ge(qk_mm, NC_ * n + c + 1)
                if exists(2 * NC_ * (n - 1) + NC_ + c):
                    dve.wait_ge(f_mm, 2 * NC_ * (n - 1) + NC_ + c + 1)
                v.tensor_copy(qh[c][0:64, :], b_qk[(u + c) % 2][0:64, :]).then_inc(qk_copy, 1)
                dve.wait_ge(qk_copy, 2 * (NC_ * n + c) + 1)
                v.tensor_tensor(ql[c][0:64, :], b_qk[(u + c) % 2][0:64, :], qh[c][0:64, :].bitcast(F32),
                                ALU.subtract).then_inc(qk_copy, 1)

            def out_():
                dve.wait_ge(o_mm, m + 1)
                o = b_o[:, 0:NT * 204].rearrange("p (h d) -> p h d", d=DH + 1)
                v.tensor_scalar(den[:, :], o[:, :, DH], 1e-6, None, ALU.add).then_inc(o_den, 1)
                dve.wait_ge(o_den, m + 1)
                v.reciprocal(rden[:, :], den[:, :]).then_inc(o_rcp, 1)
                dve.wait_ge(o_rcp, m + 1)
                if exists(m - 1):
                    dve.wait_ge(xaT_mm, m)
                v.tensor_tensor(xa[:, :, :].rearrange("p t (h d) -> p (t h) d", d=DH), o[:, :, 0:DH],
                                rden[:, :].unsqueeze(2).to_broadcast([P, NT * H, DH]), ALU.mult).then_inc(o_ev, 1)

            def v_():
                dve.wait_ge(v_mm, n + 1)
                if exists(n - 2):
                    dve.wait_ge(kv_mm, n - 1)
                v.tensor_copy(va[u][:, :, :, 0:DH].rearrange("p r h d -> p (r h) d"),
                              b_v[:, 0:2 * D].rearrange("p (h d) -> p h d", d=DH)).then_inc(v_ev, 1)

            def kv_():
                dve.wait_ge(kv_mm, n + 1)
                if exists(m):
                    dve.wait_ge(o_mm, m + 1)
                for r in two:
                    ins = v.tensor_scalar(kvb[64 * r:64 * r + 64, :, r, :],
                                          b_v[64 * r:64 * r + 64, 0:204].rearrange("p (h r d) -> p h r d", r=2, d=DH + 1)[:, :, r, :],
                                          1.0 / M, None, ALU.mult)
                ins.then_inc(kv_ev, 1)

            def y_():
                dve.wait_ge(pj_mm, m + 1)
                dve.wait_ge(prep2, m + 1)
                v.tensor_tensor(y[:, :, :], b_o[:, 0:NT * D].rearrange("p (t d) -> p t d", t=NT), xh[w][:, :, :],
                                ALU.add).then_inc(y_ev, 1)
                dve.wait_ge(y_ev, m + 1)
                for t in two:
                    ins = v.bn_stats(bs[:, t, :], y[:, t, :])
                ins.then_inc(y_bs, 1)
                dve.wait_ge(y_bs, 1)
                dve.wait_ge(y_bs, m + 1)
                for t in two:
                    ins = v.bn_aggr(mv[:, t, :], bs[:, t, :])
                ins.then_inc(y_mv, 1)
                dve.wait_ge(y_mv, m + 1)
                if exists(m - 1):
                    dve.wait_ge(y_rs, m)
                v.tensor_scalar(ve[:, :], mv[:, :, 1], 1e-5, None, ALU.add).then_inc(y_ve, 1)

            def yg_():
                dve.wait_ge(y_mv, m + 1)
                for t in two:
                    ins = v.scalar_tensor_tensor(yg[:, t, :], y[:, t, :], mv[:, t, 0:1], gam[:, :], ALU.subtract, ALU.mult)
                ins.then_inc(y_g, 1)

            def h2_():
                dve.wait_ge(y_g, m + 1)
                dve.wait_ge(y_rs, m + 1)
                if exists((a if u else a - 1) - 1):
                    dve.wait_ge(s_h2[w], ((a if u else a - 1)) * 32)
                for t in two:
                    ins = v.scalar_tensor_tensor(h2[w][:, t, 0:D], yg[:, t, :], rs[:, t:t + 1], hb[w][:, t, :],
                                                 ALU.mult, ALU.add)
                ins.then_inc(y_h2, 1)

            def f2_():
                dve.wait_ge(y_h2, m + 1)
                for t in two:
                    ins = v.bn_stats(bs2[:, t, :], h2[w][:, t, 0:D])
                ins.then_inc(h_bs, 1)
                dve.wait_ge(h_bs, 1)
                dve.wait_ge(h_bs, m + 1)
                for t in two:
                    ins = v.bn_aggr(mv2[:, t, :], bs2[:, t, :])
                ins.then_inc(h_mv, 1)
                dve.wait_ge(h_mv, m + 1)
                if exists(m - 1):
                    dve.wait_ge(h_f, m)
                v.tensor_scalar(ve2[:, :], mv2[:, :, 1], 1.0 + 1e-6 / D, 1e-11 / D, ALU.mult, ALU.add).then_inc(h_ve, 1)

            def xn_():
                dve.wait_ge(h_mv, m + 1)
                dve.wait_ge(h_f, m + 1)
                if exists(m - 1):
                    dve.wait_ge(h_xn, m)
                for t in two:
                    ins = v.tensor_scalar(xc[:, t, :], h2[w][:, t, 0:D], mv2[:, t, 0:1], f2[:, t:t + 1],
                                          ALU.subtract, ALU.mult)
                ins.then_inc(h_xc, 1)

            def xnT_():
                dve.wait_ge(xnT_mm, l + 1)
                if exists(l - 1):
                    dve.wait_ge(lg_mm, l)
                v.tensor_copy(xnT[:, :, :].rearrange("p c s -> p (c s)"), b_x[0:F, :]).then_inc(xnT_ev, 1)

            def lg_():
                dve.wait_ge(lgT_mm, l + 1)
                v.reduce_max(mx[:, 0:NT], b_x[:, 0:S].rearrange("p (t n) -> p t n", t=NT), AX.X)
                v.reduce_max(mx[:, NT:NT + GQ], b_x[:, S:2 * S].rearrange("p (t n) -> p t n", t=GQ), AX.X).then_inc(lg_mx, 1)
                dve.wait_ge(lg_mx, l + 1)
                if exists(l - 1):
                    dve.wait_ge(e_c, l)
                if exists(l - 1):
                    dve.wait_ge(e_d, l)
                v.tensor_scalar(nm[:, :], mx[:, :], -1.0, None, ALU.mult).then_inc(lg_nm, 1)

            def cd_():
                dve.wait_ge(cd_mm, l + 1)
                if exists(l - 1):
                    dve.wait_ge(sl_mm, l)
                v.tensor_copy(dT[:, :, :].rearrange("p t n -> p (t n)"), b_x[:, S:2 * S]).then_inc(d_ev, 1)
                if exists(a - 2):
                    dve.wait_ge(s_h2[u], (a - 1) * 32)
                v.tensor_copy(cT[u][:, :], b_x[:, 0:S]).then_inc(c_ev, 1)

            def yn0_(k):
                dve.wait_ge(e_d, k + 1)
                v.scalar_tensor_tensor(zs[:, :], zd[:, :], 1e-6 / D, zd[:, :], ALU.mult, ALU.mult).then_inc(sl_z, 1)
                dve.wait_ge(sl_z, k + 1)
                dve.wait_ge(sl_sq, k + 1)
                if exists(k - 1):
                    dve.wait_ge(sl_r, k)
                v.scalar_tensor_tensor(sse[:, :], ssq[:, :], 1.0 / D, zs[:, :], ALU.mult, ALU.add).then_inc(sl_e, 1)

            def yn_(k, j, pair):
                dve.wait_ge(sl_r, k + 1)
                if exists(pair - 1):
                    dve.wait_ge(s_yn[j], pair * 16)
                for t in two:
                    for q, b in ((0, b_s), (1, b_v)):
                        ins = v.scalar_tensor_tensor(yn[j][:, 2 * t + q, :], b[:, t * D:(t + 1) * D],
                                                     sr[:, 2 * t + q:2 * t + q + 1], g2r[:, :], ALU.mult, ALU.mult)
                ins.then_inc(sl_y, 1)

            A, B, C, E = step
            if A:
                qk_copy_(0)
            if E:
                yn0_(n - 3)
            if B:
                out_()
            if C:
                xnT_()
            if E:
                yn_(n - 3, w, a - 1 if u else a - 2)
            if A:
                qk_copy_(1)
            if A:
                qk_copy_(2)
            if C:
                lg_()
            if A:
                v_()
            if B:
                y_()
            if A:
                kv_()
            if B:
                yg_()
            if C:
                cd_()
            if B:
                h2_()
                f2_()
                xn_()

        pipeline(dve, iteration, 3)

    @block.scalar
    def _(act):
        f = nc.scalar.activation

        def iteration(a, u, n, step):
            m, l = n - 1, n - 2

            def sq_(c):
                act.wait_ge(qk_mm, NC_ * n + c + 1)
                if exists(2 * NC_ * (n - 1) + NC_ + c):
                    act.wait_ge(f_mm, 2 * NC_ * (n - 1) + NC_ + c + 1)
                if exists(NC_ * (n - 1) + c):
                    act.wait_ge(sq_lo, NC_ * (n - 1) + c + 1)
                f(sqf[c][64:128, :], b_qk[(u + c) % 2][64:128, :], ACT.Square).then_inc(qk_sq, 1)
                act.wait_ge(qk_sq, 2 * (NC_ * n + c) + 1)
                f(qh[c][64:128, :], sqf[c][64:128, :], ACT.Copy).then_inc(qk_sq, 1)

            def ft_(s):
                act.wait_ge(f_mm, 2 * NC_ * n + s + 1)
                if s < NC_:
                    if exists(n - 1):
                        act.wait_ge(kv_mm, n)
                    f(kp[s][:, :, :].rearrange("p r m -> p (r m)"), b_ft[s % 2][:, :], ACT.Exp).then_inc(f_exp, 1)
                else:
                    if exists(n - 1):
                        act.wait_ge(o_mm, n)
                    f(qp[s - NC_][:, :, :].rearrange("p r m -> p (r m)"), b_ft[s % 2][:, :], ACT.Exp).then_inc(f_exp, 1)

            def xaT_():
                act.wait_ge(xaT_mm, m + 1)
                if exists(m - 1):
                    act.wait_ge(pj_mm, m)
                f(xaT[0][:, :], b_o[0:F, 0:S], ACT.Copy)
                f(xaT[1][0:F, :], b_o[0:F, S:2 * S], ACT.Copy).then_inc(xaT_ev, 1)

            def lgs_():
                act.wait_ge(lg_mm, l + 1)
                if exists(l - 1):
                    act.wait_ge(lgT_mm, l)
                f(lgs[:, :, :].rearrange("p t n -> p (t n)"), b_x[:, 0:S], ACT.Copy).then_inc(lg_cp, 1)

            def ec_():
                act.wait_ge(lg_nm, l + 1)
                if exists(l - 1):
                    act.wait_ge(cd_mm, l)
                for t in two:
                    ins = f(ec[:, t, :], b_x[:, t * P:(t + 1) * P], ACT.Exp, bias=nm[:, t:t + 1],
                            accum_out=h2[u][:, t, D:D + 1])
                ins.then_inc(e_c, 1)

            def ed_(h):
                if h == 0:
                    if exists(l - 1):
                        act.wait_ge(sl_e, l)
                for q in range(2 * h, 2 * h + 2):
                    ins = f(ed[:, q, :], b_x[:, S + 64 * q:S + 64 * (q + 1)], ACT.Exp, bias=nm[:, NT + q:NT + q + 1],
                            accum_out=zd[:, q:q + 1])
                if h == 1:
                    ins.then_inc(e_d, 1)

            def ss_():
                act.wait_ge(sl_mm, l + 1)
                if exists(l - 1):
                    act.wait_ge(sl_e, l)
                for t in two:
                    for q, b in ((0, b_s), (1, b_v)):
                        ins = f(sqj[:, 2 * t + q, :], b[:, t * D:(t + 1) * D], ACT.Square, accum_out=ssq[:, 2 * t + q:2 * t + q + 1])
                ins.then_inc(sl_sq, 1)

            A, B, C = step
            if A:
                sq_(0)
                sq_(1)
                sq_(2)
                ft_(0)
            if C:
                lgs_()
            if A:
                ft_(1)
            if B:
                xaT_()
            if C:
                ec_()
            if A:
                ft_(2)
            if C:
                ed_(0)
            if A:
                ft_(3)
            if C:
                ed_(1)
            if A:
                ft_(4)
                ft_(5)
            if C:
                ss_()

        pipeline(act, iteration, 2)

    @block.gpsimd
    def _(pool):
        p = nc.gpsimd

        def iteration(a, u, n, step):
            m, l, w = n - 1, n - 2, 1 - u

            def prep_():
                pool.wait_ge(s_ld[u], (a + 1) * 32)
                if exists(n - 2):
                    pool.wait_ge(y_h2, n - 1)
                for r, c in ((0, C_EVEN), (1, C_ODD)):
                    ins = p.tensor_tensor(hh[u][:, :, r * F:(r + 1) * F], enc[u][:, :, 0:F],
                                          cst[:, c:c + 1].unsqueeze(1).to_broadcast([P, NT, F]), ALU.mult)
                ins.then_inc(prep, 1)
                pool.wait_ge(prep, n + 1)
                p.tensor_tensor(xs[:, :, :], hh[u][:, :, :], enc[u][:, :, F:F + 1].to_broadcast([P, NT, D]),
                                ALU.mult).then_inc(prep1, 1)
                p.tensor_tensor(hb[u][:, :, :], hh[u][:, :, :], bet[:, :].unsqueeze(1).to_broadcast([P, NT, D]), ALU.add)
                pool.wait_ge(prep1, n + 1)
                p.tensor_tensor(xh[u][:, :, :], xs[:, :, :], enc[u][:, :, F + 1:F + 2].to_broadcast([P, NT, D]),
                                ALU.add).then_inc(prep2, 1)

            def sq_(c):
                pool.wait_ge(qk_sq, 2 * (NC_ * n + c) + 2)
                p.tensor_tensor(ql[c][64:128, :], sqf[c][64:128, :], qh[c][64:128, :].bitcast(F32),
                                ALU.subtract).then_inc(sq_lo, 1)

            def rs_():
                pool.wait_ge(y_ve, m + 1)
                if exists(m - 1):
                    pool.wait_ge(y_h2, m)
                p.tensor_tensor(rs[:, :], ve[:, :], half[:, 0:NT], ALU.pow).then_inc(y_rs, 1)

            def f2_():
                pool.wait_ge(h_ve, m + 1)
                if exists(m - 1):
                    pool.wait_ge(h_xc, m)
                p.tensor_tensor(f2[:, :], ve2[:, :], half[:, 0:NT], ALU.pow).then_inc(h_f, 1)

            def xn_():
                pool.wait_ge(h_xc, m + 1)
                if exists(m - 2):
                    pool.wait_ge(xnT_mm, m - 1)
                if exists(m - 2):
                    pool.wait_ge(sl_mm, m - 1)
                p.tensor_tensor(xn[w][:, :, :], xc[:, :, :], gin[:, :].unsqueeze(1).to_broadcast([P, NT, D]),
                                ALU.mult).then_inc(h_xn, 1)

            def sr_(k):
                pool.wait_ge(sl_e, k + 1)
                if exists(k - 1):
                    pool.wait_ge(sl_y, k)
                p.tensor_tensor(sr[:, :], sse[:, :], half[:, 0:GQ], ALU.pow).then_inc(sl_r, 1)

            A, B, _, E = step
            if A:
                if exists(n - 2):
                    pool.wait_ge(h_xn, n - 1)
                if exists(n - 1):
                    pool.wait_ge(prep2, n)
                sq_(0)
                pool.wait_ge(sq_lo, NC_ * n + 1)
            if E:
                sr_(n - 3)
            if A:
                if E:
                    pool.wait_ge(sl_r, n - 2)
                sq_(1)
                sq_(2)
                pool.wait_ge(sq_lo, NC_ * n + NC_)
                prep_()
            if B:
                rs_()
                f2_()
                xn_()

        pipeline(pool, iteration, 3)


BACK = [step for e in range(E2 + 1)
        for n in range(NHC)
        for step in ([("up", NHC * e + n)] if e < E2 else []) + ([("down", 2 * (e - 1) + n)] if e and n < 2 else [])]
FRONT_AT = {
    1: [("turn_slots", 0)],
    2: [("turn_slots", 1), ("turn_slots", 2)],
    3: [("turn_slots", 3), ("turn_slots", 4)],
    4: [("turn_slots", 5)],
    5: [("turn_slots", 6), ("turn_slots", 7)],
    6: [("inner", 0)],
    8: [("turn_inner", 0), ("inner", 1)],
    9: [("turn_inner", 1)],
    10: [("turn_inner", 2), ("inner", 2)],
    11: [("turn_inner", 3)],
    12: [("turn_inner", 4), ("inner", 3)],
    13: [("turn_inner", 5)],
    14: [("turn_inner", 6), ("logits", 0)],
    15: [("turn_inner", 7), ("turn_logits", 0), ("logits", 1)],
    16: [("turn_logits", 1)],
    17: [("exp", 0), ("exp", 1)],
    18: [("logits", 2), ("sums", 0), ("sums", 1)],
    19: [("turn_logits", 2), ("logits", 3), ("turn_disp", 0)],
    20: [("turn_disp", 1), ("turn_logits", 3)],
    21: [("exp", 2), ("exp", 3), ("slots2", 0)],
    22: [("slots2", 1), ("slots2", 2), ("sums", 2), ("sums", 3)],
    23: [("slots2", 3)],
}
FRONT = [step for n in sorted(FRONT_AT) for step in FRONT_AT[n]]
BOTH = [step for n in range(len(BACK)) for step in [BACK[n]] + FRONT_AT.get(n, [])]
SLOTS2 = [("slots2", i) for i in range(2 * (TE // 4))]
TAIL = ([("turn_disp", 2)] + SLOTS2[4:5] + [("turn_disp", 3)] + SLOTS2[5:6] + [("bias", 0)] + SLOTS2[6:8] +
        [s for q in range(TE // 4) for s in (("back", 2 * q), ("back", 2 * q + 1), ("turn_comb", q))])
BOTH = BOTH + TAIL
INNER = [("inner", 0), ("inner", 1), ("turn_inner", 0), ("turn_inner", 1), ("inner", 2), ("turn_inner", 2),
         ("turn_inner", 3), ("inner", 3), ("turn_inner", 4), ("turn_inner", 5), ("turn_inner", 6), ("turn_inner", 7)]
ALONE = [s for s in FRONT if s[0] == "turn_slots"] + INNER
ALONE = ALONE + [s for s in FRONT if s not in ALONE] + [("turn_disp", 2), ("turn_disp", 3)] + SLOTS2[4:]
ALONE = ALONE + [("bias", 0)] + [("turn_comb", q) for q in range(TE // 4)]
LAST = BACK + [s for s in TAIL if s[0] == "back"]


def experts(nc, ctx, sem, sb, bank, g):
    cst, ident, half = g["cst"], g["ident"], g["half"]
    two = range(2)
    NQ = TE // 4
    NR = ROWS // P
    NU = 2 * E2
    UC = HID // 2
    DB = D - P
    yk = sb("yk", [P, TE, D + DB])
    ykT = sb("ykT", [F, 2, TE * P])
    mT = sb("mT", [F, 2, ROWS])
    ws = sb("ws", [F, 2, E2 * D])
    sqj = sb("sqj2", [P, E2, D])
    s_ss = sb("s_ss", [P, E2])
    s_sv = sb("s_sv", [P, E2])
    s_sr = sb("s_sr", [P, E2])
    se = [sb(f"se{i}", [P, E2, D]) for i in two]
    seT = sb("seT", [F, 2, TE, P])
    lm = [sb(f"lm{i}", [P, 4, P]) for i in two]
    mc = sb("mc", [P, 4])
    md = sb("md", [P, 4])
    exc = sb("exc", [P, TE, P])
    exd = [sb(f"exd{i}", [P, 4, P]) for i in two]
    zc = sb("zc", [P, TE])
    rzc = sb("rzc", [P, TE])
    zi = sb("zi", [P, 4])
    rzi = sb("rzi", [P, 4])
    cmT = sb("cmT", [P, TE, P])
    dm = sb("dm", [P, TE, P])
    sAh = sb("sAh", [P, E2, ROWS], F32R)
    sAl = sb("sAl", [P, E2, ROWS], F32R)
    sB = sb("sB", [P, E2, ROWS], F32R)
    w1r = [sb(f"w1r{i}", [P, 2, 2, UC]) for i in two]
    w1h = [sb(f"w1h{i}", [P, 2, 2, UC], F32R) for i in two]
    w1l = [sb(f"w1l{i}", [P, 2, 2, UC], F32R) for i in two]
    w2r = [sb(f"w2r{i}", [P, NHC, D]) for i in two]
    b1r = sb("b1r", [P, P])
    b1T = sb("b1T", [P, E2 * 2 * NHC])
    b2b = sb("b2b", [P, E2, D])
    gl = [sb(f"gl{i}", [P, ROWS]) for i in two]
    av = sb("av", [P, NHC + 2, ROWS])
    os_ = [sb(f"os{i}", [P, NR, D]) for i in two]
    oS = sb("oS", [P, TE, D])
    o2 = [os_[i // 2][:, 2 * (i % 2):2 * (i % 2) + 2, :] for i in range(4)]

    s_zero = sem("b1_cleared")
    yk_dup, s_ws, s_b1, s_b2 = sem("yk_doubled"), sem("ws_loaded"), sem("b1_loaded"), sem("b2_loaded")
    s_yk = [sem(f"yk_loaded{h}") for h in two]
    s_w1 = [sem(f"w1_loaded{i}") for i in two]
    s_w2 = [sem(f"w2_loaded{i}") for i in two]
    w1_hi, w1_lo = sem("w1_hi"), sem("w1_lo")
    b1_mm, b1_ev = sem("b1_mm"), sem("b1_ev")
    yT_mm, yT_ev, mean = sem("yT_mm"), sem("yT_ev"), sem("mean")
    se_mm, se_sq, se_v, se_r, se_n = (sem(n) for n in ("se_mm", "se_sq", "se_v", "se_r", "se_n"))
    seT_mm, seT_e0, seT_e1 = (sem(n) for n in ("seT_mm", "seT_e0", "seT_e1"))
    l_mm, l_add, c_max, c_sub, lT_mm, d_max, d_sub, l_exp = (
        sem(n) for n in ("l_mm", "l_add", "c_max", "c_sub", "lT_mm", "d_max", "d_sub", "l_exp"))
    z_c, z_d, z_r, e_n, d_mm, t_d, c_mm, t_c = (
        sem(n) for n in ("z_c", "z_d", "z_r", "e_n", "d_mm", "t_d", "c_mm", "t_c"))
    s2_mm, s2_hi, s2_lo = (sem(n) for n in ("s2_mm", "s2_hi", "s2_lo"))
    u_mm, u_gl, u_act, o_mm, o_ev = (sem(n) for n in ("u_mm", "u_gelu", "u_act", "oo_mm", "oo_ev"))
    s_os = [sem(f"shuffled{i}") for i in two]
    s_o2 = [sem(f"o2_stored{i}") for i in range(4)]
    x_mm, x_rz, x_ev = (sem(n) for n in ("x_mm", "x_rz", "x_ev"))
    block = ctx.enter_context(nc.Block())
    S2_BANKS = (2, 5, 6, 3)
    INNER_BANKS = ((5, 6), (0, 1))
    BACK_BANKS = (4, 7, 5, 6)
    SH = 4

    def all_experts(eng, run):
        run(ALONE, None, 0)
        run(BOTH, 0, 1)
        with eng.Fori(1, NE - 1, 1) as k:
            run(BOTH, k, k + 1)
        run(LAST, NE - 1, None)

    @block.sync
    def _(sp):
        def load_front(f):
            if exists(2 * NQ * (f - 1) + 2 * NQ - 1):
                sp.wait_ge(s2_mm, 1)
                sp.wait_ge(s2_mm, 2 * NQ * (f - 1) + 2 * NQ)
            src = g["yn_d"].rearrange("t e s b q d -> e (s b q) t d")[f]
            for h in two:
                tiles = slice(h * TE // 2, (h + 1) * TE // 2)
                sp.dma_start(yk[:, tiles, 0:D], src[:, tiles, :]).then_inc(s_yk[h], 16)
            if exists(NR * (f - 1) + NR - 1):
                sp.wait_ge(se_mm, 1)
                sp.wait_ge(se_mm, NR * (f - 1) + NR)
            sp.dma_start(ws[:, :, :], g["w_slot2"].rearrange("e (c p) n -> e p c n", c=2)[f]).then_inc(s_ws, 16)
            if isinstance(f, int) and f == 0:
                sp.wait_ge(s_zero, 1)
            if exists(f - 1):
                sp.wait_ge(b1_mm, 1)
                sp.wait_ge(b1_mm, f)
            sp.dma_start(b1r[0:E2 * 2 * NHC, :], g["b1"].rearrange("k e (c p) -> k (e c) p", p=P)[f]).then_inc(s_b1, 16)

        def load_b2(k):
            if exists(2 * E2 * (k - 1) + 2 * E2 - 1):
                sp.wait_ge(o_ev, 1)
                sp.wait_ge(o_ev, 2 * E2 * (k - 1) + 2 * E2)
            sp.dma_start(b2b[:, :, :], g["b2"][k].partition_broadcast(P)).then_inc(s_b2, 16)

        def load_w1(k, j):
            if exists(NU * k + j - 2):
                sp.wait_ge(w1_lo, 1)
                sp.wait_ge(w1_lo, NU * k + j - 1)
            src = g["w1"].rearrange("k e d (c u n) -> k e u d c n", c=2, u=2)[k, j // 2, j % 2]
            sp.dma_start(w1r[j % 2][:, 0, :, :], src[0:P]).then_inc(s_w1[j % 2], 16)
            for r in two:
                sp.dma_start(w1r[j % 2][r * DB:(r + 1) * DB, 1, :, :], src[P:D]).then_inc(s_w1[j % 2], 16)

        def load_w2(k, e):
            if exists(2 * (E2 * k + e - 2) + 1):
                sp.wait_ge(o_mm, 1)
                sp.wait_ge(o_mm, 2 * (E2 * k + e - 2) + 2)
            sp.dma_start(w2r[e % 2][:, :, :], g["w2"].rearrange("k e (c p) n -> k e p c n", p=P)[k, e]).then_inc(s_w2[e % 2], 16)

        def run(order, k, f, more):
            if k is None:
                load_front(f)
                load_w1(0, 0)
                load_w1(0, 1)
                load_w2(0, 0)
                load_w2(0, 1)
                load_b2(0)
                load_w1(0, 2)
                load_front(1)
                return
            for name, i in order:
                if name == "up" and i % 2 == 1:
                    j = i // 2 + 3
                    if j < NU:
                        load_w1(k, j)
                    elif f is not None:
                        load_w1(f, j - NU)
                elif name == "down" and i % 2 == 1:
                    e = i // 2
                    if e + 2 < E2:
                        load_w2(k, e + 2)
                    elif f is not None:
                        load_w2(f, e + 2 - E2)
                    sp.wait_ge(o_ev, 1)
                    sp.wait_ge(o_ev, 2 * E2 * k + i + 1)
                    if e == 0:
                        if exists(8 * (k - 1) + 7):
                            sp.wait_ge(x_mm, 1)
                            sp.wait_ge(x_mm, 8 * (k - 1) + 8)
                    for j in range(4):
                        sp.dma_start(oS[:, :, :].rearrange("p (r j) d -> p j r d", j=4)[32 * e:32 * e + 32, j, :, :],
                                     os_[e % 2][32 * j:32 * j + 32, :, :]).then_inc(s_os[e % 2], 16)
                    if e == E2 - 1 and f is not None:
                        load_b2(f)
                elif name == "slots2" and i == 2 * NQ - 1 and more:
                    load_front(f + 1)
                elif name == "back":
                    sp.wait_ge(x_ev, 1)
                    sp.wait_ge(x_ev, 8 * k + i + 1)
                    dst = g["o2_d"].rearrange("t e s b q d -> e (s b q) t d")[k]
                    sp.dma_start(dst[:, 2 * i:2 * i + 2, :], o2[i % 4]).then_inc(s_o2[i % 4], 16)

        run(ALONE, None, 0, True)
        run(BOTH, 0, 1, True)
        with sp.Fori(1, NE - 2, 1) as k:
            run(BOTH, k, k + 1, True)
        run(BOTH, NE - 2, NE - 1, False)
        run(LAST, NE - 1, None, False)
        for i in range(4):
            sp.wait_ge(s_o2[i], 16 * 2 * NE)

    @block.tensor
    def _(pe):
        mm, tr = nc.tensor.matmul, nc.tensor.transpose

        def turn_slots(f, i):
            if i == 0:
                pe.wait_ge(s_yk[0], 16 * f + 16)
                if exists(8 * (f - 2) + 7):
                    pe.wait_ge(x_ev, 8 * (f - 2) + 8)
                if exists(f - 1):
                    pe.wait_ge(b1_ev, f)
            if i == 4:
                pe.wait_ge(s_yk[1], 16 * f + 16)
            if i < 2:
                if exists(2 * NQ * (f - 1) + 2 * NQ - 1):
                    pe.wait_ge(s2_lo, 2 * NQ * (f - 1) + 2 * NQ)
            if exists(8 * f + i - 2):
                pe.wait_ge(yT_ev, 8 * f + i - 1)
            for c in two:
                for t in two:
                    ins = tr(bank[5 + i % 2][0:F, (2 * c + t) * P:(2 * c + t + 1) * P], yk[:, 2 * i + t, c * F:(c + 1) * F], ident)
            ins.then_inc(yT_mm, 1)

        def inner(f, k, r):
            if r == 0:
                pe.wait_ge(s_ws, 16 * f + 16)
                pe.wait_ge(yT_ev, 8 * f + 8)
            pe.wait_ge(mean, NR * f + r + 1)
            if exists(NR * f + r - (2 if k is None else 1)):
                pe.wait_ge(se_n, NR * f + r - (2 if k is None else 1) + 1)
            for h in two:
                for c in two:
                    ins = mm(bank[INNER_BANKS[r % 2 if k is None else 0][h]][:, 0:2 * D], mT[:, c, r * P:(r + 1) * P], ws[:, c, h * 2 * D:(h + 1) * 2 * D],
                             start=c == 0, stop=c == 1)
            ins.then_inc(se_mm, 1)

        def turn_inner(f, i):
            r, c = i // 2, i % 2
            pe.wait_ge(se_n, NR * f + r + 1)
            if exists(NR * f + r - (1 - c)):
                pe.wait_ge(seT_e0 if c else seT_e1, NR * f + r - (1 - c) + 1)
            for e in range(E2):
                ins = tr(bank[7][0:F, e * P:(e + 1) * P], se[r % 2][:, e, c * F:(c + 1) * F], ident)
            ins.then_inc(seT_mm, 1)

        def logits(f, q):
            pe.wait_ge(seT_e0, NR * f + q + 1)
            pe.wait_ge(seT_e1, NR * f + q + 1)
            if exists(NQ * f + q - 1):
                pe.wait_ge(l_add, NQ * f + q)
            for j in range(4):
                t = 4 * q + j
                for c in two:
                    ins = mm(bank[5][:, j * P:(j + 1) * P], ykT[:, c, t * P:(t + 1) * P], seT[:, c, t, :],
                             start=c == 0, stop=c == 1)
            ins.then_inc(l_mm, 1)

        def turn_logits(f, q):
            pe.wait_ge(l_add, NQ * f + q + 1)
            if exists(NQ * f + q - 1):
                pe.wait_ge(d_sub, NQ * f + q)
            for j in range(4):
                ins = tr(bank[6][:, j * P:(j + 1) * P], lm[q % 2][:, j, :], ident)
            ins.then_inc(lT_mm, 1)

        def turn_disp(f, q):
            pe.wait_ge(e_n, NQ * f + q + 1)
            if exists(NQ * f + q - 1):
                pe.wait_ge(t_d, NQ * f + q)
            if q == 0:
                pe.wait_ge(seT_e1, NR * f + NR)
            for j in range(4):
                ins = tr(bank[7][:, j * P:(j + 1) * P], exd[q % 2][:, j, :], ident)
            ins.then_inc(d_mm, 1)

        def slots2(f, k, i):
            q, c = i // 2, i % 2
            pe.wait_ge(t_d, NQ * f + q + 1)
            if i == 0:
                pe.wait_ge(yk_dup, f + 1)
            if i == 0:
                if k is not None:
                    pe.wait_ge(u_act, 16 * k + 15)
            elif i < 3:
                pe.wait_ge(d_sub, NQ * f + NQ)
            elif i == 3:
                if k is not None:
                    pe.wait_ge(u_act, 16 * k + 16)
            else:
                pe.wait_ge(s2_lo, 2 * NQ * f + i - 3)
            for j in range(4):
                ins = mm(bank[S2_BANKS[i % 4]][:, j * P:(j + 1) * P], yk[:, 4 * q + j, c * P:(c + 1) * P], dm[:, 4 * q + j, :],
                         start=True, stop=True)
            ins.then_inc(s2_mm, 1)

        def bias(f):
            pe.wait_ge(s_b1, 16 * f + 16)
            pe.wait_ge(t_d, NQ * f + NQ)
            tr(bank[7][:, 0:P], b1r[:, :], ident).then_inc(b1_mm, 1)

        def turn_comb(f, k, q):
            pe.wait_ge(l_exp, NQ * f + q + 1)
            if q > 1:
                pe.wait_ge(t_c, NQ * f + q - 1)
            elif k is not None:
                pe.wait_ge(u_act, 16 * k + 16)
            for j in range(4):
                ins = tr(bank[q % 2][:, j * P:(j + 1) * P], exc[:, 4 * q + j, :], ident)
            ins.then_inc(c_mm, 1)

        def up(k, n):
            e, h = n // NHC, n % NHC
            j = n // 2
            cols = slice((n % 2) * P, (n % 2 + 1) * P)
            if n % 2 == 0:
                pe.wait_ge(w1_lo, NU * k + j + 1)
            if n == 0:
                pe.wait_ge(s2_lo, 2 * NQ * k + 2 * NQ)
                pe.wait_ge(t_c, NQ * k + NQ - 1)
            if n == 1:
                pe.wait_ge(t_c, NQ * k + NQ)
            if n > 1:
                pe.wait_ge(u_act, 16 * k + n - 1)
            wh, wl = w1h[j % 2], w1l[j % 2]
            for c, b in ((1, 2), (0, 0)):
                out = bank[b + n % 2][:, :]
                mm(out, wh[:, 0, c, cols], sAh[:, e, :], start=True, stop=False)
                mm(out, wh[:, 0, c, cols], sAl[:, e, :], start=False, stop=False)
                mm(out, wl[:, 0, c, cols], sAh[:, e, :], start=False, stop=False)
                mm(out, wh[:, 1, c, cols], sB[:, e, :], start=False, stop=False)
                ins = mm(out, wl[0:DB, 1, c, cols], sB[0:DB, e, :], start=False, stop=True)
            ins.then_inc(u_mm, 1)

        def down(k, n):
            e, i = n // 2, n % 2
            if i == 0:
                pe.wait_ge(u_act, 16 * k + NHC * e + NHC)
                pe.wait_ge(s_w2[e % 2], (2 * k + e // 2 + 1) * 16)
            if n == 0:
                if exists(8 * (k - 1) + 7):
                    pe.wait_ge(x_ev, 8 * (k - 1) + 8)
            else:
                pe.wait_ge(o_ev, 2 * E2 * k + n)
            for r in range(2 * i, 2 * i + 2):
                out, cols = bank[4][:, (r % 2) * D:(r % 2 + 1) * D], slice(r * P, (r + 1) * P)
                for h in range(NHC):
                    ins = mm(out, av[:, (NHC * e + h) % (NHC + 2), cols], w2r[e % 2][:, h, :], start=h == 0, stop=h == NHC - 1)
            ins.then_inc(o_mm, 1)

        def back(k, f, i):
            if i == 0:
                for j in two:
                    pe.wait_ge(s_os[j], (2 * k + 2) * 16 * SH)
                pe.wait_ge(o_ev, 2 * E2 * k + 2 * E2)
                pe.wait_ge(t_c, NQ * k + NQ)
            elif i >= 4:
                pe.wait_ge(x_ev, 8 * k + i - 3)
            elif f is not None:
                if i == 1:
                    pe.wait_ge(b1_ev, f + 1)
                else:
                    pe.wait_ge(s2_lo, 2 * NQ * f + i + 4)
            for t in two:
                ins = mm(bank[BACK_BANKS[i % 4]][:, t * D:(t + 1) * D], cmT[:, 2 * i + t, :], oS[:, 2 * i + t, :], start=True, stop=True)
            ins.then_inc(x_mm, 1)

        def run(order, k, f):
            for name, i in order:
                if name == "turn_slots":
                    turn_slots(f, i)
                elif name == "inner":
                    inner(f, k, i)
                elif name == "turn_inner":
                    turn_inner(f, i)
                elif name == "logits":
                    logits(f, i)
                elif name == "turn_logits":
                    turn_logits(f, i)
                elif name == "turn_disp":
                    turn_disp(f, i)
                elif name == "slots2":
                    slots2(f, k, i)
                elif name == "bias":
                    bias(f)
                elif name == "turn_comb":
                    turn_comb(f, k, i)
                elif name == "up":
                    up(k, i)
                elif name == "down":
                    down(k, i)
                elif name == "back":
                    back(k, f, i)

        all_experts(pe, run)

    @block.vector
    def _(dve):
        v = nc.vector
        v.memset(b1r[:, :], 0.0).then_inc(s_zero, 1)

        def means(f, r):
            dve.wait_ge(yT_ev, 8 * f + 2 * r + 2)
            for c in two:
                ins = v.reduce_sum(mT[:, c, r * P:(r + 1) * P].rearrange("p (m q) -> p m q", q=2 * GQ),
                                   ykT[:, c, 512 * r:512 * (r + 1)].rearrange("p (m n q) -> p m q n", n=4, q=2 * GQ), AX.X)
            ins.then_inc(mean, 1)

        def inner(f, k, r):
            i = NR * f + r
            dve.wait_ge(se_sq, i + 1)
            if exists(i - 1):
                dve.wait_ge(se_r, i)
            v.tensor_scalar(s_sv[:, :], s_ss[:, :], 1.0 / D, NS * 1e-6 / D, ALU.mult, ALU.add).then_inc(se_v, 1)
            dve.wait_ge(se_r, i + 1)
            if exists(2 * (i - 2) + 1):
                dve.wait_ge(seT_mm, 2 * (i - 2) + 2)
            for h in two:
                ins = v.tensor_tensor(se[r % 2][:, 2 * h:2 * h + 2, :], bank[INNER_BANKS[r % 2 if k is None else 0][h]][:, 0:2 * D].rearrange("p (e d) -> p e d", e=2),
                                      s_sr[:, 2 * h:2 * h + 2].unsqueeze(2).to_broadcast([P, 2, D]), ALU.mult)
            ins.then_inc(se_n, 1)

        def turn_inner(f, i):
            if i % 2:
                r = i // 2
                dve.wait_ge(seT_mm, 2 * (NR * f + r) + 2)
                v.tensor_copy(seT[:, 1, 4 * r:4 * r + 4, :].rearrange("p t (e n) -> p t e n", e=E2),
                              bank[7][0:F, :].rearrange("p (e t n) -> p t e n", e=E2, t=4)).then_inc(seT_e1, 1)

        def logits(f, q):
            i = NQ * f + q
            dve.wait_ge(l_mm, i + 1)
            if exists(i - 2):
                dve.wait_ge(lT_mm, i - 1)
            if exists(i - 2):
                dve.wait_ge(c_sub, i - 1)
            v.tensor_tensor(lm[q % 2][:, :, :], bank[5][:, :].rearrange("p (j n) -> p j n", j=4),
                            cst[:, C_M1:C_M1 + P].unsqueeze(1).to_broadcast([P, 4, P]), ALU.add).then_inc(l_add, 1)
            dve.wait_ge(l_add, i + 1)
            v.reduce_max(mc[:, :], lm[q % 2][:, :, :], AX.X).then_inc(c_max, 1)
            dve.wait_ge(c_max, i + 1)
            if exists(NQ * (f - 1) + q):
                dve.wait_ge(c_mm, NQ * (f - 1) + q + 1)
            v.tensor_tensor(exc[:, 4 * q:4 * q + 4, :], lm[q % 2][:, :, :], mc[:, :].unsqueeze(2).to_broadcast([P, 4, P]),
                            ALU.subtract).then_inc(c_sub, 1)

        def turn_logits(f, q):
            i = NQ * f + q
            dve.wait_ge(lT_mm, i + 1)
            if exists(i - 1):
                dve.wait_ge(d_sub, i)
            b = bank[6][:, :].rearrange("p (j n) -> p j n", j=4)
            v.reduce_max(md[:, :], b, AX.X).then_inc(d_max, 1)
            dve.wait_ge(d_max, i + 1)
            if exists(i - 2):
                dve.wait_ge(d_mm, i - 1)
            v.tensor_tensor(exd[q % 2][:, :, :], b, md[:, :].unsqueeze(2).to_broadcast([P, 4, P]), ALU.subtract).then_inc(d_sub, 1)

        def sums(f, q):
            i = NQ * f + q
            dve.wait_ge(l_exp, i + 1)
            if exists(i - 1):
                dve.wait_ge(z_r, i)
            v.reduce_sum(zi[:, :], exd[q % 2][:, :, :], AX.X).then_inc(z_d, 1)
            dve.wait_ge(z_d, i + 1)
            if exists(i - 1):
                dve.wait_ge(e_n, i)
            v.reciprocal(rzi[:, :], zi[:, :]).then_inc(z_r, 1)
            if q == 0:
                if exists(f - 1):
                    dve.wait_ge(x_rz, f)
            v.reduce_sum(zc[:, 4 * q:4 * q + 4], exc[:, 4 * q:4 * q + 4, :], AX.X).then_inc(z_c, 1)

        def slots2(f, i):
            q, c = i // 2, i % 2
            dve.wait_ge(s2_hi, 2 * NQ * f + i + 1)
            lo, hi = (slice(0, P), sAh) if c == 0 else (slice(DB, P), sB)
            out = sAl if c == 0 else sB
            v.tensor_tensor(out[lo, :, P * q:P * (q + 1)].rearrange("p e (j n) -> p j e n", j=4),
                            bank[S2_BANKS[i % 4]][lo, :].rearrange("p (j e n) -> p j e n", j=4, e=E2),
                            hi[lo, :, P * q:P * (q + 1)].rearrange("p e (j n) -> p j e n", j=4).bitcast(F32),
                            ALU.subtract).then_inc(s2_lo, 1)

        def bias(f):
            dve.wait_ge(b1_mm, f + 1)
            v.tensor_copy(b1T[:, :], bank[7][:, 0:E2 * 2 * NHC]).then_inc(b1_ev, 1)

        def up(k, n):
            dve.wait_ge(u_gl, 16 * k + n + 1)
            if n < NHC + 2:
                if exists(2 * E2 * (k - 1) + 2 * E2 - 1):
                    dve.wait_ge(o_mm, 2 * E2 * (k - 1) + 2 * E2)
            else:
                dve.wait_ge(o_mm, 2 * (E2 * k + (n - NHC - 2) // NHC) + 2)
            c = n // NHC * 2 * NHC + n % NHC
            v.scalar_tensor_tensor(av[:, n % (NHC + 2), :], bank[n % 2][:, :], b1T[:, c:c + 1], gl[n % 2][:, :],
                                   ALU.add, ALU.mult).then_inc(u_act, 1)

        def down(k, n):
            e, i = n // 2, n % 2
            dve.wait_ge(o_mm, 2 * E2 * k + n + 1)
            if n == 0:
                dve.wait_ge(s_b2, 16 * k + 16)
            if i == 0:
                if exists(2 * k + e // 2 - 1):
                    dve.wait_ge(s_os[e % 2], (2 * k + e // 2) * 16 * SH)
                if e < 2:
                    for j in two:
                        if exists(2 * k - 1):
                            dve.wait_ge(s_o2[2 * e + j], (2 * k) * 16)
            v.tensor_tensor(os_[e % 2][:, 2 * i:2 * i + 2, :], bank[4][:, 0:2 * D].rearrange("p (r d) -> p r d", r=2),
                            b2b[:, e, :].unsqueeze(1).to_broadcast([P, 2, D]), ALU.add).then_inc(o_ev, 1)

        def back(k, i):
            dve.wait_ge(x_mm, 8 * k + i + 1)
            if i == 0:
                dve.wait_ge(x_rz, k + 1)
            if i >= 4:
                dve.wait_ge(s_o2[i % 4], (2 * k + 1) * 16)
            v.tensor_tensor(o2[i % 4], bank[BACK_BANKS[i % 4]][:, 0:2 * D].rearrange("p (t d) -> p t d", t=2),
                            rzc[:, 2 * i:2 * i + 2].unsqueeze(2).to_broadcast([P, 2, D]), ALU.mult).then_inc(x_ev, 1)

        def run(order, k, f):
            for name, i in order:
                if name == "turn_slots":
                    if i % 2:
                        means(f, i // 2)
                elif name == "inner":
                    inner(f, k, i)
                elif name == "turn_inner":
                    turn_inner(f, i)
                elif name == "logits":
                    logits(f, i)
                elif name == "turn_logits":
                    turn_logits(f, i)
                elif name == "sums":
                    sums(f, i)
                elif name == "slots2":
                    slots2(f, i)
                elif name == "bias":
                    bias(f)
                elif name == "up":
                    up(k, i)
                elif name == "down":
                    down(k, i)
                elif name == "back":
                    back(k, i)
            if f is not None:
                dve.wait_ge(z_c, NQ * f + NQ)
                if exists(8 * (f - 1) + 7):
                    dve.wait_ge(x_ev, 8 * (f - 1) + 8)
                v.reciprocal(rzc[:, :], zc[:, :]).then_inc(x_rz, 1)

        all_experts(dve, run)

    @block.scalar
    def _(act):
        f_ = nc.scalar.activation

        def split_w1(k, j):
            act.wait_ge(s_w1[j % 2], (4 * k + j // 2 + 1) * 48)
            if exists(16 * k + 2 * (j - 2) + 1):
                act.wait_ge(u_mm, 16 * k + 2 * (j - 2) + 2)
            f_(w1h[j % 2][:, :, :, :], w1r[j % 2][:, :, :, :], ACT.Copy).then_inc(w1_hi, 1)

        def turn_slots(f, i):
            act.wait_ge(yT_mm, 8 * f + i + 1)
            f_(ykT[:, :, 256 * i:256 * (i + 1)], bank[5 + i % 2][0:F, :].rearrange("p (c n) -> p c n", c=2),
               ACT.Copy).then_inc(yT_ev, 1)
            if i == 7:
                for h in two:
                    act.wait_ge(s_yk[h], 16 * f + 16)
                f_(yk[:, :, D:D + DB], yk[:, :, P:D], ACT.Copy).then_inc(yk_dup, 1)

        def inner(f, k, r):
            act.wait_ge(se_mm, NR * f + r + 1)
            if exists(NR * f + r - 1):
                act.wait_ge(se_v, NR * f + r)
            for e in range(E2):
                ins = f_(sqj[:, e, :], bank[INNER_BANKS[r % 2 if k is None else 0][e // 2]][:, (e % 2) * D:(e % 2 + 1) * D], ACT.Square, accum_out=s_ss[:, e:e + 1])
            ins.then_inc(se_sq, 1)

        def turn_inner(f, i):
            if i % 2 == 0:
                r = i // 2
                act.wait_ge(seT_mm, 2 * (NR * f + r) + 1)
                f_(seT[:, 0, 4 * r:4 * r + 4, :].rearrange("p t (e n) -> p t e n", e=E2),
                   bank[7][0:F, :].rearrange("p (e t n) -> p t e n", e=E2, t=4), ACT.Copy).then_inc(seT_e0, 1)

        def exp(f, q):
            i = NQ * f + q
            act.wait_ge(c_sub, i + 1)
            f_(exc[:, 4 * q:4 * q + 4, :], exc[:, 4 * q:4 * q + 4, :], ACT.Exp)
            act.wait_ge(d_sub, i + 1)
            f_(exd[q % 2][:, :, :], exd[q % 2][:, :, :], ACT.Exp).then_inc(l_exp, 1)

        def turn_disp(f, q):
            act.wait_ge(d_mm, NQ * f + q + 1)
            f_(dm[:, 4 * q:4 * q + 4, :].rearrange("p t n -> p (t n)"), bank[7][:, :], ACT.Copy).then_inc(t_d, 1)

        def slots2(f, i):
            q, c = i // 2, i % 2
            act.wait_ge(s2_mm, 2 * NQ * f + i + 1)
            f_((sB if c else sAh)[:, :, P * q:P * (q + 1)].rearrange("p e (j n) -> p j e n", j=4),
               bank[S2_BANKS[i % 4]][:, :].rearrange("p (j e n) -> p j e n", j=4, e=E2), ACT.Copy).then_inc(s2_hi, 1)

        def turn_comb(f, q):
            act.wait_ge(c_mm, NQ * f + q + 1)
            if exists(8 * (f - 1) + 2 * q + 1):
                act.wait_ge(x_mm, 8 * (f - 1) + 2 * q + 2)
            f_(cmT[:, 4 * q:4 * q + 4, :].rearrange("p t n -> p (t n)"), bank[q % 2][:, :], ACT.Copy).then_inc(t_c, 1)

        def up(k, n):
            i = 16 * k + n
            act.wait_ge(u_mm, i + 1)
            if n == 0:
                act.wait_ge(b1_ev, k + 1)
            if exists(i - 2):
                act.wait_ge(u_act, i - 1)
            c = n // NHC * 2 * NHC + NHC + n % NHC
            f_(gl[n % 2][:, :], bank[2 + n % 2][:, :], ACT.Gelu_apprx_tanh, bias=b1T[:, c:c + 1]).then_inc(u_gl, 1)

        def run(order, k, f):
            if k is None:
                split_w1(0, 0)
            for name, i in order:
                if name == "turn_slots":
                    turn_slots(f, i)
                elif name == "inner":
                    inner(f, k, i)
                elif name == "turn_inner":
                    turn_inner(f, i)
                elif name == "exp":
                    exp(f, i)
                elif name == "turn_disp":
                    turn_disp(f, i)
                elif name == "slots2":
                    slots2(f, i)
                elif name == "bias":
                    split_w1(f, 1)
                elif name == "turn_comb":
                    turn_comb(f, i)
                elif name == "up":
                    up(k, i)
                    if i % 2 == 0 and i > 0:
                        if i // 2 + 1 < NU:
                            split_w1(k, i // 2 + 1)
                        elif f is not None:
                            split_w1(f, 0)

        all_experts(act, run)

    @block.gpsimd
    def _(pool):
        p = nc.gpsimd

        def split_w1(k, j):
            pool.wait_ge(w1_hi, NU * k + j + 1)
            p.tensor_tensor(w1l[j % 2][:, :, :, :].rearrange("p a c n -> p (a c n)"),
                            w1r[j % 2][:, :, :, :].rearrange("p a c n -> p (a c n)"),
                            w1h[j % 2][:, :, :, :].rearrange("p a c n -> p (a c n)").bitcast(F32), ALU.subtract).then_inc(w1_lo, 1)

        def run(order, k, f):
            if k is None:
                split_w1(0, 0)
            for name, n in order:
                if name == "inner":
                    i = NR * f + n
                    pool.wait_ge(se_v, i + 1)
                    if exists(i - 1):
                        pool.wait_ge(se_n, i)
                    p.tensor_tensor(s_sr[:, :], s_sv[:, :], half[:, 0:E2], ALU.pow).then_inc(se_r, 1)
                elif name == "sums":
                    pool.wait_ge(z_r, NQ * f + n + 1)
                    p.tensor_tensor(exd[n % 2][:, :, :], exd[n % 2][:, :, :], rzi[:, :].unsqueeze(2).to_broadcast([P, 4, P]),
                                    ALU.mult).then_inc(e_n, 1)
                elif name == "bias":
                    split_w1(f, 1)
                elif name == "up":
                    if n % 2 == 0 and n > 0:
                        if n // 2 + 1 < NU:
                            split_w1(k, n // 2 + 1)
                        elif f is not None:
                            split_w1(f, 0)

        all_experts(pool, run)


def combine(nc, ctx, sem, sb, bank, g):
    two = range(2)
    NP = NB // 2
    o2 = [sb(f"o2b{i}", [P, 2, GQ, D]) for i in two]
    cT = [sb(f"cTb{i}", [P, 2, S]) for i in two]
    h2 = [sb(f"h2b{i}", [P, 2, NT, D + 1]) for i in two]
    rz = sb("rzb", [P, 2, 2 * NT])
    ob = [sb(f"ob{i}", [P, 2, NT, D]) for i in two]
    s_ld = [sem(f"c_loaded{i}") for i in two]
    s_st = [sem(f"c_stored{i}") for i in two]
    c_mm, c_rz, c_ev = sem("tokens_mm"), sem("tokens_rz"), sem("tokens_out")
    block = ctx.enter_context(nc.Block())
    LD = 3

    def each_pair(eng, body):
        for n in range(4):
            body(n // 2, n % 2, n)
        with eng.Fori(2, NP // 2, 1) as a:
            for u in two:
                body(a, u, 2 * a + u)

    @block.sync
    def _(sp):
        def body(a, u, n):
            if exists(n - 2):
                sp.wait_ge(c_ev, 1)
                sp.wait_ge(c_ev, n - 1)
            sp.dma_start(o2[u][:, :, :, :].rearrange("p b q d -> p (b q d)"),
                         g["o2_d"].rearrange("t e s b q d -> t (e s) (b q d)")[n]).then_inc(s_ld[u], 16)
            sp.dma_start(cT[u][:, :, :], g["combT_d"].rearrange("(t b) p s -> t p b s", b=2)[n]).then_inc(s_ld[u], 16)
            sp.dma_start(h2[u][:, :, :, :].rearrange("p b t d -> p b (t d)"),
                         g["h2_d"].rearrange("(n b) p t d -> n p b (t d)", b=2)[n]).then_inc(s_ld[u], 16)

        each_pair(sp, body)

    @block.tensor
    def _(pe):
        def body(a, u, n):
            pe.wait_ge(s_ld[u], (a + 1) * 16 * LD)
            if exists(n - 2):
                pe.wait_ge(c_ev, n - 1)
            for b in two:
                for t in two:
                    for q in two:
                        c = t * P + 64 * q
                        ins = nc.tensor.matmul(bank[2 * u + b][64 * q:64 * q + 64, t * D:(t + 1) * D], cT[u][:, b, c:c + 64],
                                               o2[u][:, b, 2 * t + q, :], start=True, stop=True)
            ins.then_inc(c_mm, 1)

        each_pair(pe, body)

    @block.vector
    def _(dve):
        def body(a, u, n):
            dve.wait_ge(s_ld[u], (a + 1) * 16 * LD)
            if exists(n - 2):
                dve.wait_ge(c_ev, n - 1)
            nc.vector.reciprocal(rz[:, u, :], h2[u][:, :, :, D].rearrange("p b t -> p (b t)")).then_inc(c_rz, 1)
            dve.wait_ge(c_rz, n + 1)
            dve.wait_ge(c_mm, n + 1)
            if exists(a - 1):
                dve.wait_ge(s_st[u], a * 16)
            for b in two:
                for t in two:
                    ins = nc.vector.scalar_tensor_tensor(ob[u][:, b, t, :], bank[2 * u + b][:, t * D:(t + 1) * D],
                                                         rz[:, u, 2 * b + t:2 * b + t + 1], h2[u][:, b, t, 0:D],
                                                         ALU.mult, ALU.add)
            ins.then_inc(c_ev, 1)

        each_pair(dve, body)

    @block.scalar
    def _(act):
        def body(a, u, n):
            act.wait_ge(c_ev, n + 1)
            act.dma_start(g["out"].rearrange("(n b) (t p) d -> n p b t d", b=2, p=P)[n], ob[u][:, :, :, :]).then_inc(s_st[u], 16)

        each_pair(act, body)
        for u in two:
            act.wait_ge(s_st[u], 16 * NP // 2)


_INS = ["x", "consts", "rows", "L0_tok_scale", "L0_attn_W_qkv", "L0_attn_W_proj", "L0_attn_b_proj", "L0_attn_gamma",
        "L0_attn_beta", "L0_attn_random_features", "L0_ffn_gamma_in", "L0_ffn_slots1", "L0_ffn_gamma2",
        "L0_ffn_w_slot2", "L0_ffn_w1", "L0_ffn_b1", "L0_ffn_w2", "L0_ffn_b2"]


def kernel(**inputs):
    import concourse.bacc as _bacc
    from concourse.bass_utils import run_bass_kernel_spmd as _run

    inputs["consts"], inputs["rows"] = shape_constants()
    nc = _bacc.Bacc("TRN2", target_bir_lowering=False, num_devices=1)
    arrays, args = {}, []
    for name in _INS:
        a = np.ascontiguousarray(inputs[name])
        arrays[f"in_{name}"] = a
        args.append(nc.dram_tensor(f"in_{name}", a.shape, mybir.dt.from_np(a.dtype), kind="ExternalInput").ap())
    args.append(nc.dram_tensor("out_0", (NB, S, D), F32, kind="ExternalOutput").ap())
    build(nc, *args)
    r = _run(nc, [arrays], core_ids=[0])
    return r.results[0]["out_0"]
```
